# Optimizing a Trainium2 kernel written in Bass

```python
import numpy as np
import jax
import jax.numpy as jnp

def _softmax(x, axis=-1):
    return jax.nn.softmax(x, axis=axis)

def _gelu(x):
    return jax.nn.gelu(x, approximate=True)

def _silu(x):
    return jax.nn.silu(x)

def _sigmoid(x):
    return jax.nn.sigmoid(x)

def _layernorm(x, axis=-1, eps=1e-05):
    m = jnp.mean(x, axis=axis, keepdims=True)
    v = jnp.var(x, axis=axis, keepdims=True)
    return (x - m) / jnp.sqrt(v + eps)

def _scatter_add(tgt, idx, src, axis=0):
    return tgt.at[idx].add(src)

def _segment_sum(src, seg, n):
    return jax.ops.segment_sum(src, seg, n)
kernel_name = 'mk_gnn_resnorm_d2_gnn_r64_56425e'

def setup_inputs(seed: int=0):
    np.random.seed(seed)
    _w = jnp.asarray

    def _rec_inputs():
        import jax
        import jax.numpy as jnp
        _gk = jax.random.key(seed)
        x = -0.0005121 + 1.001 * jax.random.normal(jax.random.fold_in(_gk, 1), (50000, 64), jnp.float32)
        src = jax.random.randint(jax.random.fold_in(_gk, 2), (25000,), 0, 50000, jnp.int32)
        dst = jnp.minimum((50000 * jax.random.uniform(jax.random.fold_in(_gk, 3), (25000,)) ** 2.0).astype(jnp.int32), 49999)
        _o = jnp.argsort(dst, stable=True)
        src = src[_o]
        dst = dst[_o]
        edge_weight = -0.0026448 + 0.998911 * jax.random.normal(jax.random.fold_in(_gk, 12), (25000,), jnp.float32)
        edge_weight1 = jax.random.uniform(jax.random.fold_in(_gk, 13), (25000, 1), jnp.float32, 0.0, 1)
        node_vec1 = jax.random.uniform(jax.random.fold_in(_gk, 14), (50000, 1), jnp.float32, 0.0, 1)
        return (x, src, dst, edge_weight, edge_weight1, node_vec1)
    x, src, dst, edge_weight, edge_weight1, node_vec1 = _rec_inputs()

    def _L0_gnn_setup():
        import jax, jax.numpy as jnp
        import numpy as np
        N = 50000
        E = 6250
        IN = 64
        HID = 64
        H = 2
        C = HID
        L = 2
        R = 4
        EPS = 1e-05
        NEG_SLOPE = 0.2

        def _gat(x, W, a_src, a_dst, bias, s, d, m):
            h = (x @ W).reshape(-1, H, C)
            es = jnp.sum(h * a_src, axis=-1)
            ed = jnp.sum(h * a_dst, axis=-1)
            e = jax.nn.leaky_relu(es[s] + ed[d], NEG_SLOPE)
            e = jnp.where(m[:, None], e, -jnp.inf)
            emax = jax.ops.segment_max(e, d, num_segments=N)
            p = jnp.exp(e - emax[d]) * m[:, None]
            den = jax.ops.segment_sum(p, d, num_segments=N)
            alpha = p / den[d]
            out = jax.ops.segment_sum(alpha[:, :, None] * h[s], d, num_segments=N)
            return out.reshape(N, H * C) + bias
        key = jax.random.key(seed)
        ks = jax.random.split(key, 10)
        x = jax.random.normal(ks[0], (N, IN), jnp.float32)
        edge_index = jax.random.randint(ks[1], (2, E), 0, N, jnp.int32)
        edge_weight = jax.random.normal(ks[2], (E,), jnp.float32)
        s_in = 1.0 / np.sqrt(IN)
        gat_W = jax.random.normal(ks[3], (L, R, IN, H * C), jnp.float32) * s_in
        gat_asrc = jax.random.normal(ks[4], (L, R, H, C), jnp.float32) * (1.0 / np.sqrt(C))
        gat_adst = jax.random.normal(ks[5], (L, R, H, C), jnp.float32) * (1.0 / np.sqrt(C))
        gat_bias = jnp.zeros((L, R, H * C), jnp.float32)
        mlp_in = IN + R * H * C
        mlp_W1 = jax.random.normal(ks[6], (L, mlp_in, HID), jnp.float32) / np.sqrt(mlp_in)
        mlp_b1 = jnp.zeros((L, HID), jnp.float32)
        mlp_W2 = jax.random.normal(ks[7], (L, HID, HID), jnp.float32) / np.sqrt(HID)
        mlp_b2 = jnp.zeros((L, HID), jnp.float32)
        ln_g = jnp.ones((L, HID), jnp.float32)
        ln_b = jnp.zeros((L, HID), jnp.float32)
        return dict(x=x, edge_index=edge_index, edge_weight=edge_weight, gat_W=gat_W, gat_asrc=gat_asrc, gat_adst=gat_adst, gat_bias=gat_bias, mlp_W1=mlp_W1, mlp_b1=mlp_b1, mlp_W2=mlp_W2, mlp_b2=mlp_b2, ln_g=ln_g, ln_b=ln_b)
    _L0_gnn_all = _L0_gnn_setup()
    _L0_gnn_in = {k: v for k, v in _L0_gnn_all.items() if k in ('gat_W', 'gat_asrc', 'gat_adst', 'gat_bias', 'mlp_W1', 'mlp_b1', 'mlp_W2', 'mlp_b2', 'ln_g', 'ln_b')}
    del _L0_gnn_all

    def _L1_gnn_setup():
        import jax, jax.numpy as jnp
        import numpy as np
        C = 1.0
        SQC = 1.0
        MIN_NORM = 1e-15
        PROJ_EPS = 0.004
        NORM_FACTOR = 100.0
        N_NODES, E_EDGES, D = (50000, 12500, 64)

        def _artanh(x):
            x = jnp.clip(x, -1.0 + 1e-07, 1.0 - 1e-07)
            return 0.5 * (jnp.log1p(x) - jnp.log1p(-x))

        def _norm(x):
            return jnp.maximum(jnp.linalg.norm(x, axis=-1, keepdims=True), MIN_NORM)

        def proj(x):
            maxnorm = (1.0 - PROJ_EPS) / SQC
            n = _norm(x)
            return jnp.where(n > maxnorm, x / n * maxnorm, x)

        def logmap0(p):
            n = _norm(p)
            return p / (SQC * n) * _artanh(SQC * n)

        def expmap0(u):
            n = _norm(u)
            return proj(jnp.tanh(SQC * n) * u / (SQC * n))

        def mobius_add(x, y):
            x2 = jnp.sum(x * x, -1, keepdims=True)
            y2 = jnp.sum(y * y, -1, keepdims=True)
            xy = jnp.sum(x * y, -1, keepdims=True)
            num = (1.0 + 2.0 * C * xy + C * y2) * x + (1.0 - C * x2) * y
            den = 1.0 + 2.0 * C * xy + C * C * x2 * y2
            return num / jnp.maximum(den, MIN_NORM)

        def lambda_x(p):
            return 2.0 / jnp.maximum(1.0 - C * jnp.sum(p * p, -1, keepdims=True), MIN_NORM)

        def sqdist(p1, p2):
            d = 2.0 / SQC * _artanh(SQC * _norm(mobius_add(-p1, p2)))
            return d * d

        def logmap(p1, p2):
            sub = mobius_add(-p1, p2)
            n = _norm(sub)
            return 2.0 / (SQC * lambda_x(p1)) * _artanh(SQC * n) * sub / n

        def expmap(u, p):
            n = _norm(u)
            second = jnp.tanh(SQC * lambda_x(p) * n / 2.0) * u / (SQC * n)
            return proj(mobius_add(p, second))
        key = jax.random.key(seed)
        ks = jax.random.split(key, 8)
        h_tan = 0.05 * jax.random.normal(ks[0], (N_NODES, D), jnp.float32)
        h = expmap0(h_tan)
        distances = jax.random.uniform(ks[1], (E_EDGES, 1), jnp.float32)
        edges = jax.random.randint(ks[2], (2, E_EDGES), 0, N_NODES, jnp.int32)
        node_mask = jnp.ones((N_NODES, 1), jnp.float32)
        edge_mask = jnp.ones((E_EDGES, 1), jnp.float32)
        lin_W = jax.random.normal(ks[3], (D, D), jnp.float32) / np.sqrt(D)
        bias = jnp.full((1, D), 0.1, jnp.float32)
        att_W1 = jax.random.normal(ks[4], (D, 2 * D + 2), jnp.float32) / np.sqrt(2 * D + 2)
        att_b1 = jnp.zeros((D,), jnp.float32)
        att_W2 = jax.random.normal(ks[5], (1, D), jnp.float32) / np.sqrt(D)
        att_b2 = jnp.zeros((1,), jnp.float32)
        ln_g = jnp.ones((D,), jnp.float32)
        ln_b = jnp.zeros((D,), jnp.float32)
        return {'h': h, 'distances': distances, 'edges': edges, 'node_mask': node_mask, 'edge_mask': edge_mask, 'lin_W': lin_W, 'bias': bias, 'att_W1': att_W1, 'att_b1': att_b1, 'att_W2': att_W2, 'att_b2': att_b2, 'ln_g': ln_g, 'ln_b': ln_b}
    _L1_gnn_all = _L1_gnn_setup()
    _L1_gnn_in = {k: v for k, v in _L1_gnn_all.items() if k in ('lin_W', 'bias', 'att_W1', 'att_b1', 'att_W2', 'att_b2', 'ln_g', 'ln_b')}
    del _L1_gnn_all
    return {'x': x, 'src': src, 'dst': dst, 'edge_weight': edge_weight, 'edge_weight1': edge_weight1, 'node_vec1': node_vec1, 'L0_gnn_gat_W': _L0_gnn_in['gat_W'], 'L0_gnn_gat_asrc': _L0_gnn_in['gat_asrc'], 'L0_gnn_gat_adst': _L0_gnn_in['gat_adst'], 'L0_gnn_gat_bias': _L0_gnn_in['gat_bias'], 'L0_gnn_mlp_W1': _L0_gnn_in['mlp_W1'], 'L0_gnn_mlp_b1': _L0_gnn_in['mlp_b1'], 'L0_gnn_mlp_W2': _L0_gnn_in['mlp_W2'], 'L0_gnn_mlp_b2': _L0_gnn_in['mlp_b2'], 'L0_gnn_ln_g': _L0_gnn_in['ln_g'], 'L0_gnn_ln_b': _L0_gnn_in['ln_b'], 'L1_gnn_lin_W': _L1_gnn_in['lin_W'], 'L1_gnn_bias': _L1_gnn_in['bias'], 'L1_gnn_att_W1': _L1_gnn_in['att_W1'], 'L1_gnn_att_b1': _L1_gnn_in['att_b1'], 'L1_gnn_att_W2': _L1_gnn_in['att_W2'], 'L1_gnn_att_b2': _L1_gnn_in['att_b2'], 'L1_gnn_ln_g': _L1_gnn_in['ln_g'], 'L1_gnn_ln_b': _L1_gnn_in['ln_b']}

def reference(x, src, dst, edge_weight, edge_weight1, node_vec1, L0_gnn_gat_W, L0_gnn_gat_asrc, L0_gnn_gat_adst, L0_gnn_gat_bias, L0_gnn_mlp_W1, L0_gnn_mlp_b1, L0_gnn_mlp_W2, L0_gnn_mlp_b2, L0_gnn_ln_g, L0_gnn_ln_b, L1_gnn_lin_W, L1_gnn_bias, L1_gnn_att_W1, L1_gnn_att_b1, L1_gnn_att_W2, L1_gnn_att_b2, L1_gnn_ln_g, L1_gnn_ln_b):
    import jax
    import jax.numpy as jnp

    def _L0_gnn_ref(x, edge_index, edge_weight, gat_W, gat_asrc, gat_adst, gat_bias, mlp_W1, mlp_b1, mlp_W2, mlp_b2, ln_g, ln_b):
        import jax, jax.numpy as jnp
        import numpy as np
        N = 50000
        E = 6250
        IN = 64
        HID = 64
        H = 2
        C = HID
        L = 2
        R = 4
        EPS = 1e-05
        NEG_SLOPE = 0.2

        def _gat(x, W, a_src, a_dst, bias, s, d, m):
            h = (x @ W).reshape(-1, H, C)
            es = jnp.sum(h * a_src, axis=-1)
            ed = jnp.sum(h * a_dst, axis=-1)
            e = jax.nn.leaky_relu(es[s] + ed[d], NEG_SLOPE)
            e = jnp.where(m[:, None], e, -jnp.inf)
            emax = jax.ops.segment_max(e, d, num_segments=N)
            p = jnp.exp(e - emax[d]) * m[:, None]
            den = jax.ops.segment_sum(p, d, num_segments=N)
            alpha = p / den[d]
            out = jax.ops.segment_sum(alpha[:, :, None] * h[s], d, num_segments=N)
            return out.reshape(N, H * C) + bias
        src, dst = (edge_index[0], edge_index[1])
        loop = jnp.arange(N, dtype=src.dtype)
        pos = edge_weight > 0
        neg = edge_weight < 0
        ones = jnp.ones((N,), bool)
        rels = [(jnp.concatenate([src, loop]), jnp.concatenate([dst, loop]), jnp.concatenate([pos, ones])), (jnp.concatenate([dst, loop]), jnp.concatenate([src, loop]), jnp.concatenate([pos, ones])), (jnp.concatenate([src, loop]), jnp.concatenate([dst, loop]), jnp.concatenate([neg, ones])), (jnp.concatenate([dst, loop]), jnp.concatenate([src, loop]), jnp.concatenate([neg, ones]))]
        h = x
        for l in range(L):
            feats = [_gat(h, gat_W[l, r], gat_asrc[l, r], gat_adst[l, r], gat_bias[l, r], rels[r][0], rels[r][1], rels[r][2]) for r in range(R)]
            comb = jnp.concatenate([h] + feats, axis=1)
            z = jnp.tanh(comb @ mlp_W1[l] + mlp_b1[l]) @ mlp_W2[l] + mlp_b2[l]
            z = z + h
            mu = jnp.mean(z, axis=-1, keepdims=True)
            var = jnp.var(z, axis=-1, keepdims=True)
            h = (z - mu) / jnp.sqrt(var + EPS) * ln_g[l] + ln_b[l]
        return h

    def _L1_gnn_ref(h, distances, edges, node_mask, edge_mask, lin_W, bias, att_W1, att_b1, att_W2, att_b2, ln_g, ln_b):
        import jax, jax.numpy as jnp
        import numpy as np
        C = 1.0
        SQC = 1.0
        MIN_NORM = 1e-15
        PROJ_EPS = 0.004
        NORM_FACTOR = 100.0
        N_NODES, E_EDGES, D = (50000, 12500, 64)

        def _artanh(x):
            x = jnp.clip(x, -1.0 + 1e-07, 1.0 - 1e-07)
            return 0.5 * (jnp.log1p(x) - jnp.log1p(-x))

        def _norm(x):
            return jnp.maximum(jnp.linalg.norm(x, axis=-1, keepdims=True), MIN_NORM)

        def proj(x):
            maxnorm = (1.0 - PROJ_EPS) / SQC
            n = _norm(x)
            return jnp.where(n > maxnorm, x / n * maxnorm, x)

        def logmap0(p):
            n = _norm(p)
            return p / (SQC * n) * _artanh(SQC * n)

        def expmap0(u):
            n = _norm(u)
            return proj(jnp.tanh(SQC * n) * u / (SQC * n))

        def mobius_add(x, y):
            x2 = jnp.sum(x * x, -1, keepdims=True)
            y2 = jnp.sum(y * y, -1, keepdims=True)
            xy = jnp.sum(x * y, -1, keepdims=True)
            num = (1.0 + 2.0 * C * xy + C * y2) * x + (1.0 - C * x2) * y
            den = 1.0 + 2.0 * C * xy + C * C * x2 * y2
            return num / jnp.maximum(den, MIN_NORM)

        def lambda_x(p):
            return 2.0 / jnp.maximum(1.0 - C * jnp.sum(p * p, -1, keepdims=True), MIN_NORM)

        def sqdist(p1, p2):
            d = 2.0 / SQC * _artanh(SQC * _norm(mobius_add(-p1, p2)))
            return d * d

        def logmap(p1, p2):
            sub = mobius_add(-p1, p2)
            n = _norm(sub)
            return 2.0 / (SQC * lambda_x(p1)) * _artanh(SQC * n) * sub / n

        def expmap(u, p):
            n = _norm(u)
            second = jnp.tanh(SQC * lambda_x(p) * n / 2.0) * u / (SQC * n)
            return proj(mobius_add(p, second))
        n_nodes = h.shape[0]
        xt = logmap0(h) @ lin_W.T
        x = expmap0(xt)
        x = mobius_add(x, expmap0(bias))
        x_tan = logmap0(x)
        row, col = (edges[0], edges[1])
        xr, xc = (x[row], x[col])
        geo = sqdist(xr, xc)
        d2 = jnp.concatenate([distances, geo], axis=-1)
        feat = jnp.concatenate([x_tan[row], x_tan[col], d2], axis=-1)
        a = jax.nn.silu(feat @ att_W1.T + att_b1)
        att = jax.nn.sigmoid(a @ att_W2.T + att_b2) * edge_mask
        x_local = logmap(xr, xc)
        agg = jax.ops.segment_sum(x_local * att, row, num_segments=n_nodes) / NORM_FACTOR
        x = expmap(agg, x)
        t = logmap0(x)
        mu = jnp.mean(t, -1, keepdims=True)
        var = jnp.var(t, -1, keepdims=True)
        t = (t - mu) / jnp.sqrt(var + 1e-05) * ln_g + ln_b
        x = expmap0(t)
        x = expmap0(jax.nn.relu(logmap0(x)))
        return x
    edge_index = jnp.stack([src, dst])
    x = _layernorm(x + _L0_gnn_ref(x, edge_index, edge_weight, L0_gnn_gat_W, L0_gnn_gat_asrc, L0_gnn_gat_adst, L0_gnn_gat_bias, L0_gnn_mlp_W1, L0_gnn_mlp_b1, L0_gnn_mlp_W2, L0_gnn_mlp_b2, L0_gnn_ln_g, L0_gnn_ln_b), axis=-1)
    x = _layernorm(x + _L1_gnn_ref(x, edge_weight1, edge_index, node_vec1, edge_weight1, L1_gnn_lin_W, L1_gnn_bias, L1_gnn_att_W1, L1_gnn_att_b1, L1_gnn_att_W2, L1_gnn_att_b2, L1_gnn_ln_g, L1_gnn_ln_b), axis=-1)
    return x

_drawn_inputs = setup_inputs


def setup_inputs(seed=0):
    import zlib

    import numpy as np

    out = dict(_drawn_inputs(seed))
    spreads = {'L0_gnn_gat_bias': (0.0, 0.1),
     'L0_gnn_mlp_b1': (0.0, 0.1),
     'L0_gnn_mlp_b2': (0.0, 0.1),
     'L0_gnn_ln_g': (1.0, 0.2),
     'L0_gnn_ln_b': (0.0, 0.1),
     'L1_gnn_bias': (0.10000000149011612, 0.6),
     'L1_gnn_att_b1': (0.0, 0.8),
     'L1_gnn_ln_g': (1.0, 0.6),
     'L1_gnn_ln_b': (0.0, 0.729)}
    factors = {'edge_weight1': 64.0, 'L0_gnn_gat_adst': 2.87, 'L1_gnn_att_W1': 8.0, 'L1_gnn_att_W2': 8.0}
    for name, (base, spread) in spreads.items():
        noise = np.random.default_rng([zlib.crc32(name.encode()), seed]).standard_normal(out[name].shape)
        drawn = base * np.exp(spread * noise) if base else spread * noise
        out[name] = jnp.asarray(drawn.astype(out[name].dtype))
    for name, factor in factors.items():
        out[name] = (out[name] * factor).astype(out[name].dtype)
    return out
```

```python
import concourse.bass as bass
from concourse import mybir
from concourse.alu_op_type import AluOpType as ALU
from contextlib import ExitStack

N, E, D = 50000, 25000, 64
P = 125
TN, TE = N // P, E // P
L, R, H = 2, 4, 2
NCHUNK = 20
CE, CN = TE // NCHUNK, TN // NCHUNK
NTAB = TN // CE
ROW = D + 16
HROW = 2 * D + 1
RADIX = 256
BIG = 1e30
MAXNORM = 1.0 - 0.004
MIN_NORM = 1e-15
CLIP = 1.0 - 1e-7
GRP = 4
NGRP = TE // GRP
REC = 5
SKIP = 1000000


def build(nc, a, out):
    fp32, i32 = mybir.dt.float32, mybir.dt.int32
    ACT = mybir.ActivationFunctionType
    X = mybir.AxisListType.X
    ctx = ExitStack()
    with ctx:
        def sb(name, shape, dt=fp32):
            return ctx.enter_context(nc.sbuf_tensor(name, shape, dt))

        def sem(name):
            return ctx.enter_context(nc.semaphore(name))

        def dram(name, shape):
            return nc.dram_tensor(name, shape, fp32, kind="Internal").ap()

        rec_dram = dram("rec_dram", (E, REC))
        gat_table = [dram(f"gat_table{l}", (N, ROW)) for l in range(L)]
        h2_dram = dram("h2_dram", (N, D))
        pair_dram = dram("pair_dram", (E, ROW))
        corr_dram = [dram(f"corr_dram{d}", (N, D)) for d in range(2)]
        agg_dram = dram("agg_dram", (N, D))
        x0_dram = dram("x0_dram", (N, D))
        row_table = dram("row_table", (N, HROW))
        col_table = dram("col_table", (N, HROW))

        def by_part(t):
            return t.rearrange("(p t) w -> p (t w)", p=P)

        def chunk(t, c, width, cols):
            return by_part(t)[:, bass.ds(c * (cols * width), cols * width)]


        arena = sb("arena", [128, 2 * TE * ROW])

        def area(at, cols, width):
            return arena[0:P, at:at + cols * width].rearrange("p (t w) -> p t w", w=width)

        G = [area(d * TE * ROW, TE, ROW) for d in range(2)]
        nodes = area(0, TN, D)
        edges_v = area(0, TE, D)
        SPARE = TN * D
        pool_a = sb("pool_a", [128, 2 * CE * HROW])
        pool_b = sb("pool_b", [128, 2 * CE * HROW])

        def slot_of(pool, s, cols, width):
            return pool[0:P, s * CE * HROW:s * CE * HROW + cols * width].rearrange("p (t w) -> p t w", w=width)

        scratch = sb("scratch", [128, 12 * TN])
        att = [scratch[0:P, k * 4 * TE:(k + 1) * 4 * TE].rearrange("p (s t) -> p s t", s=4) for k in range(6)]
        sc = [scratch[0:P, k * TN:(k + 1) * TN] for k in range(12)]
        ident = sb("ident", [128, 128])
        ones = sb("ones", [128, 128])
        tri_lt = sb("tri_lt", [128, 128])
        tri_gt = sb("tri_gt", [128, 128])
        position_i = sb("position_i", [128, TE], i32)
        rec = scratch[:, 0:TE * REC]
        rec_v = rec[0:P, :].rearrange("p (t c) -> p t c", c=REC)
        hist, total, cursor, matched, digits_row, digits_i = (scratch[:, TE * REC + k * RADIX:TE * REC + (k + 1) * RADIX] for k in range(6))
        digits_i = digits_i.bitcast(i32)
        digit, digit_i = (scratch[:, TE * REC + 6 * RADIX + k * TE:TE * REC + 6 * RADIX + (k + 1) * TE] for k in range(2))
        digit_i = digit_i.bitcast(i32)
        rank = sb("rank", [128, CE])
        rec_stage = sb("rec_stage", [128, 2, CE * REC])
        place_i = sb("place_i", [128, 2, CE], i32)
        idx_a = sb("idx_a", [128, 2, CE], i32)
        idx_b = sb("idx_b", [128, 2, CE], i32)
        src_i = [sb(f"src_i{o}", [128, TE], i32) for o in range(2)]
        dst_i = [sb(f"dst_i{o}", [128, TE], i32) for o in range(2)]
        out_i = [sb(f"out_i{o}", [128, TE], i32) for o in range(2)]
        pair_i = sb("pair_i", [128, TE], i32)
        keep = [sb(f"keep{o}", [128, TE]) for o in range(2)]
        keep_b = [sb(f"keep_b{o}", [128, TE]) for o in range(2)]
        first = [sb(f"first{o}", [128, TE]) for o in range(2)]
        last = [sb(f"last{o}", [128, TE]) for o in range(2)]
        off = [sb(f"off{o}", [128, 2, TE]) for o in range(2)]
        carry_f = [sb(f"carry_f{o}", [128, 128]) for o in range(2)]
        carry_b = [sb(f"carry_b{o}", [128, 128]) for o in range(2)]
        far_f = [sb(f"far_f{o}", [128, 128]) for o in range(2)]
        far_b = [sb(f"far_b{o}", [128, 128]) for o in range(2)]
        weight1 = sb("weight1", [128, TE])
        prod = sb("prod", [128, GRP * 4 * D])
        diag = prod[:, 0:4 * P].rearrange("p (s q) -> p s q", s=4)
        far = prod[:, 4 * P:8 * P].rearrange("p (s q) -> p s q", s=4)
        key_diag = prod[:, 0:256].rearrange("p (k q) -> p k q", k=2)
        goes_on = sb("goes_on", [128, 1])
        seg_off = scratch[:, 5 * 4 * TE:6 * 4 * TE].rearrange("p (k t) -> p k t", k=4)
        carry4 = sb("carry4", [128, 4, 4])
        carry_v = sb("carry_v", [128, D])
        tr = sb("tr", [64, 2, GRP * P])
        grp_stage = sb("grp_stage", [128, 2, GRP * D])
        proj_w = [sb(f"proj_w{l}", [64, 16]) for l in range(L)]
        edge_w = [sb(f"edge_w{l}", [64, 2, 4 * D]) for l in range(L)]
        dense_w = [sb(f"dense_w{l}", [64, D]) for l in range(L)]
        mlp_w2 = [sb(f"mlp_w2{l}", [64, D]) for l in range(L)]
        b1_row = [sb(f"b1_row{l}", [128, D]) for l in range(L)]
        b2_row = [sb(f"b2_row{l}", [128, D]) for l in range(L)]
        g_row = [sb(f"g_row{l}", [128, D]) for l in range(L)]
        be_row = [sb(f"be_row{l}", [128, D]) for l in range(L)]
        lin_t = sb("lin_t", [64, D])
        att_t = sb("att_t", [64, 2 * D])
        hyp_bias = sb("hyp_bias", [128, D])
        hyp_row = {k: sb(f"hyp_{k}", [128, D]) for k in ("b1", "w2", "g", "b", "wd", "wg")}
        att_b2 = sb("att_b2", [128, 1])
        power = sb("power", [128, 2])
        bias_sc = sb("bias_sc", [128, 16])
        small = sb("small", [128, 3, 2 * CE])
        raw_at = [16000]

        def raw(parts, n):
            raw_at[0] += n
            return arena[0:parts, raw_at[0] - n:raw_at[0]]

        w_raw = [raw(64, R * H * D) for l in range(L)]
        a_raw = [raw(64, 2 * R * H * D) for l in range(L)]
        w_prod = raw(64, R * H * D)
        w_red = raw(64, 2 * R * H)
        w1_edge = [raw(128, R * D) for l in range(L)]
        w1_top = [raw(64, D) for l in range(L)]
        w_t = [raw(128, R * D) for l in range(L)]
        gat_b = [raw(128, R) for l in range(L)]
        lin_raw = raw(64, D)
        att_raw = raw(64, 2 * D + 2)
        zeros = raw(128, CN * D)
        ps = ctx.enter_context(nc.psum_tensor("ps", [128, 8 * 512], fp32))

        def bank(b, n=1):
            return ps[:, b * 512:(b + n) * 512]

        spacer = {k: sem(f"s_spacer_{k}") for k in ("sp", "act", "pool", "pe", "dve")}

        def hold(eng, who, s, value):
            if isinstance(value, int):
                if value > 0:
                    eng.wait_ge(s, value)
            else:
                eng.wait_ge(s, value)
                eng.sem_inc(spacer[who], 1)

        def steps(eng, n, body):
            for s in range(2):
                body(0, s, s)
            with eng.Fori(1, n // 2) as it:
                for s in range(2):
                    body(it, s, it * 2 + s)

        class Signals(dict):
            run, per_run = 0, {}

            def upto(self, key, value):
                return self.run * self.per_run[key] + value if self.run else value

        def sems(name, names, slotted=()):
            made = Signals({k: sem(f"s_{name}_{k}") for k in names})
            made.update({k: [sem(f"s_{name}_{k}{s}") for s in range(2)] for k in slotted})
            return made

        def runs(made, n, per_run):
            out_ = []
            for k in range(n):
                ph = Signals(made)
                ph.run, ph.per_run = k, per_run
                out_.append(ph)
            return out_

        s_w = sem("s_weights_loaded")
        s_in = sem("s_edges_loaded")
        s_const = sem("s_constants")
        s_zeroed = sem("s_tables_zeroed")
        WP = sems("wprep", ("dve", "t", "tc", "mm", "act", "row"))
        TAB = sems("tab", ("tr", "trc", "mm", "rows"), ("load", "store"))
        SORT = runs(sems("sort", ("rec", "hist", "base", "staged"), ("scattered",)), 4,
                    dict(rec=16, hist=1, base=1, staged=NCHUNK, scattered=16 * TE // 2))
        ORD = runs(sems("order", ("diag", "bc", "done")), 2, dict(diag=1, bc=1, done=1))
        EDGE = runs(sems("edge", ("idx", "rows", "pair", "copied"), ("gathered", "permuted")), L,
                    dict(idx=2 * NCHUNK, rows=NCHUNK, pair=16 * NCHUNK, copied=NCHUNK, gathered=16 * TE, permuted=16 * TE // 2))
        att_runs = runs(sems("att", ("diag", "bc", "dve", "exp", "sums", "copied", "tr", "trc", "mm", "prod", "scan", "cv", "cvc", "stage"),
                             ("scattered",)), 2 * L,
                        dict(diag=3, bc=2, dve=1, exp=2, sums=1, copied=NGRP, tr=NGRP, trc=NGRP, mm=NGRP, prod=NGRP, scan=1, cv=1, cvc=1,
                             stage=NCHUNK, scattered=16 * TE // 2))
        ATT = [att_runs[2 * l:2 * l + 2] for l in range(L)]
        NODE = [sems(f"node{l}", ("pre", "tr", "trc", "mm", "u", "th", "z", "var", "rstd", "h", "rows"), ("load", "store"))
                for l in range(L)]
        HYP = sems("hyp", ("act_asked", "pool_asked", "act", "pool", "used", "x0", "y", "tr", "trc", "mm", "x1", "rows"), ("load", "store", "store2"))
        HE = sems("hedge", ("idx", "rows", "act_asked", "pool_asked", "act", "pool", "pre", "gate", "scan", "cv", "cvc", "stage"), ("gathered", "scattered"))
        FIN = sems("fin", ("act_asked", "pool_asked", "act", "pool", "used1", "used2", "used3", "rows"), ("load1", "load2", "load3", "store"))
        s_link = sem("s_dve_link")
        block = ctx.enter_context(nc.Block())


        NCONST = 10
        NTAB_G, NODE_G = CN // GRP, [3 * CN // GRP, 2 * CN // GRP]
        V, A, T, GP = nc.vector, nc.scalar, nc.tensor, nc.gpsimd

        def cols(v, width=D):
            return v.unsqueeze(2).broadcast_to([P, v.shape[1], width])

        def rows_of(r, n):
            return r[0:P, :].unsqueeze(1).broadcast_to([P, n, D])

        def flat(v):
            return v.rearrange("p t w -> p (t w)")

        def chunk3(t, c, width, ncols):
            return chunk(t, c, width, ncols).rearrange("p (t w) -> p t w", w=width)

        def nchunk(c):
            return nodes[:, bass.ds(c * CN, CN), :]

        tab_rows = [area(s * CN * ROW, CN, ROW) for s in range(2)]
        n_h = [area((2 + s) * CN * ROW, CN, ROW) for s in range(2)]
        n_f = [area(4 * CN * ROW + s * CN * D, CN, D) for s in range(2)]
        n_r = [area(4 * CN * ROW + (2 + s) * CN * D, CN, D) for s in range(2)]
        n_u = area(4 * CN * ROW + 4 * CN * D, CN, D)
        n_z = area(4 * CN * ROW + 5 * CN * D, CN, D)
        sp_a = [area(SPARE + s * CN * D, CN, D) for s in range(2)]
        sp_b = [area(SPARE + (2 + s) * CN * D, CN, D) for s in range(2)]
        sp_t = area(SPARE + 4 * CN * D, CN, D)
        hyp_tmp = pool_a[0:P, 0:CN * D].rearrange("p (t w) -> p t w", w=D)
        hyp_r = [pool_a[0:P, 0:CN * HROW].rearrange("p (t w) -> p t w", w=HROW), area(SPARE, CN, HROW)]
        hyp_c = [pool_b[0:P, 0:CN * HROW].rearrange("p (t w) -> p t w", w=HROW), area(SPARE + CN * HROW, CN, HROW)]
        edges_pre = area(TE * D, TE, D)
        g_src = [slot_of(pool_a, s, CE, ROW) for s in range(2)]
        g_dst = [slot_of(pool_b, s, CE, ROW) for s in range(2)]
        h_row = [slot_of(pool_a, s, CE, HROW) for s in range(2)]
        h_col = [slot_of(pool_b, s, CE, HROW) for s in range(2)]
        gat_stage = [slot_of(pool_b, s, CE, D) for s in range(2)]
        hyp_stage = [area(SPARE + s * CE * D, CE, D) for s in range(2)]
        perm = g_src
        trv = [tr[:, s, :] for s in range(2)]

        weight_loads = []

        def bc(v, n=128):
            return v.rearrange("(a n) -> a n", a=1).broadcast_to([n, v.shape[0]])

        for l in range(L):
            weight_loads.append((w_raw[l].rearrange("i (r c) -> i r c", r=R), a["L0_gnn_gat_W"][l].rearrange("r i c -> i r c")))
            for k, name in enumerate(("L0_gnn_gat_asrc", "L0_gnn_gat_adst")):
                weight_loads.append((a_raw[l][:, k * R * H * D:(k + 1) * R * H * D], bc(a[name][l].rearrange("r h c -> (r h c)"), 64)))
            weight_loads += [
                (w1_edge[l].rearrange("p (r n) -> p r n", r=R), a["L0_gnn_mlp_W1"][l, D:, :].rearrange("(r p) n -> p r n", r=R)),
                (w1_top[l], a["L0_gnn_mlp_W1"][l, 0:D, :]),
                *((gat_b[l][:, r:r + 1], a["L0_gnn_gat_bias"][l, r].rearrange("(p a) -> p a", a=1)) for r in range(R)),
                (mlp_w2[l][:, :], a["L0_gnn_mlp_W2"][l]),
                (b1_row[l][:, :], bc(a["L0_gnn_mlp_b1"][l])),
                (b2_row[l][:, :], bc(a["L0_gnn_mlp_b2"][l])),
                (g_row[l][:, :], bc(a["L0_gnn_ln_g"][l])),
                (be_row[l][:, :], bc(a["L0_gnn_ln_b"][l]))]
        weight_loads += [
            (lin_raw, a["L1_gnn_lin_W"]), (att_raw, a["L1_gnn_att_W1"]),
            (hyp_bias[:, :], a["L1_gnn_bias"].broadcast_to([128, D])),
            (hyp_row["b1"][:, :], bc(a["L1_gnn_att_b1"])),
            (hyp_row["w2"][:, :], a["L1_gnn_att_W2"].broadcast_to([128, D])),
            (hyp_row["g"][:, :], bc(a["L1_gnn_ln_g"])), (hyp_row["b"][:, :], bc(a["L1_gnn_ln_b"])),
            (att_b2[:, :], bc(a["L1_gnn_att_b2"]))]
        NW = 16 * len(weight_loads)

        def sp_load_inputs(sp):
            for dst, name in ((dst_i[1][0:P, :], "dst"), (src_i[1][0:P, :], "src"), (off[0][0:P, 0, :], "edge_weight")):
                sp.dma_start(dst, a[name].rearrange("(p t) -> p t", p=P)).then_inc(s_in, 16)
            sp.dma_start(off[0][0:P, 1, :], a["edge_weight1"].rearrange("(p t) a -> p (t a)", p=P)).then_inc(s_in, 16)
            for dst, src in weight_loads:
                sp.dma_start(dst, src).then_inc(s_w, 16)
            sp.wait_ge(s_const, NCONST)
            for t in (corr_dram[0], corr_dram[1], agg_dram):
                with sp.Fori(0, NCHUNK) as c:
                    sp.dma_start(chunk(t, c, D, CN), zeros[0:P, :]).then_inc(s_zeroed, 16)

        def sp_table0(sp):
            def load(s, c):
                sp.dma_start(tab_rows[s][:, :, 0:D], chunk3(a["x"], c, D, CN)).then_inc(TAB["load"][s], 16)

            def store(s, c):
                hold(sp, "sp", TAB["rows"], c + 1)
                sp.dma_start(chunk(gat_table[0], c, ROW, CN), flat(tab_rows[s])).then_inc(TAB["store"][s], 16)

            for s in range(2):
                load(s, s)
            with sp.Fori(0, NCHUNK // 2 - 1) as it:
                for s in range(2):
                    store(s, it * 2 + s)
                    hold(sp, "sp", TAB["store"][s], it * 16 + 16)
                    load(s, it * 2 + s + 2)
            for s in range(2):
                store(s, NCHUNK - 2 + s)

        def sp_sort(sp, k):
            for s in range(2):
                sp.wait_ge(SORT[k]["scattered"][s], SORT[k].upto("scattered", 16 * TE // 2))
            sp.dma_start(rec[0:P, :], by_part(rec_dram)).then_inc(SORT[k]["rec"], 16)

        def sp_pairs(sp, l):
            with sp.Fori(0, NCHUNK) as c:
                hold(sp, "sp", EDGE[l]["rows"], EDGE[l].upto("rows", c + 1))
                sp.dma_start(chunk(pair_dram, c, ROW, CE), flat(G[0][:, bass.ds(c * CE, CE), :])).then_inc(EDGE[l]["pair"], 16)

        def sp_node(sp, l):
            ph, table = NODE[l], gat_table[l]
            for d in range(2):
                for s in range(2):
                    sp.wait_ge(ATT[l][d]["scattered"][s], ATT[l][d].upto("scattered", 16 * TE // 2))

            def load(s, c):
                sp.dma_start(flat(n_h[s]), chunk(table, c, ROW, CN)).then_inc(ph["load"][s], 16)
                for d, to in enumerate((n_f, n_r)):
                    sp.dma_start(flat(to[s]), chunk(corr_dram[d], c, D, CN)).then_inc(ph["load"][s], 16)

            def store(s, c):
                hold(sp, "sp", ph["rows"], ph.upto("rows", c + 1))
                if l + 1 < L:
                    sp.dma_start(chunk(gat_table[l + 1], c, ROW, CN), flat(tab_rows[s])).then_inc(ph["store"][s], 16)
                else:
                    sp.dma_start(chunk3(h2_dram, c, D, CN), tab_rows[s][:, :, 0:D]).then_inc(ph["store"][s], 16)

            for s in range(2):
                load(s, s)
            with sp.Fori(0, NCHUNK // 2 - 1) as it:
                for s in range(2):
                    store(s, it * 2 + s)
                    load(s, it * 2 + s + 2)
            for s in range(2):
                store(s, NCHUNK - 2 + s)
            for s in range(2):
                sp.wait_ge(ph["store"][s], ph.upto("store", 16 * NCHUNK // 2))

        def sp_hyp(sp):
            ph = HYP

            def load(s, c):
                sp.dma_start(flat(sp_a[s]), chunk(h2_dram, c, D, CN)).then_inc(ph["load"][s], 16)
                sp.dma_start(flat(sp_b[s]), chunk(a["x"], c, D, CN)).then_inc(ph["load"][s], 16)

            for s in range(2):
                load(s, s)
            with sp.Fori(0, NCHUNK // 2 - 1) as it:
                for s in range(2):
                    hold(sp, "sp", ph["used"], ph.upto("used", it * 2 + s + 1))
                    load(s, it * 2 + s + 2)
            with sp.Fori(0, NCHUNK // 2) as it:
                for s in range(2):
                    hold(sp, "sp", ph["x0"], ph.upto("x0", it * 2 + s + 1))
                    sp.dma_start(chunk(x0_dram, it * 2 + s, D, CN), flat(sp_a[s])).then_inc(ph["store"][s], 16)
            with sp.Fori(0, NCHUNK // 2) as it:
                for s in range(2):
                    hold(sp, "sp", ph["rows"], ph.upto("rows", it * 2 + s + 1))
                    sp.dma_start(chunk(row_table, it * 2 + s, HROW, CN), flat(hyp_r[s])).then_inc(ph["store2"][s], 16)
                    sp.dma_start(chunk(col_table, it * 2 + s, HROW, CN), flat(hyp_c[s])).then_inc(ph["store2"][s], 16)

        def sp_final(sp):
            ph = FIN

            def pass_in(key, used, srcs):
                def load(s, c):
                    for to, t, w in srcs:
                        sp.dma_start(to[s], chunk3(t, c, w, CN)[:, :, 0:D]).then_inc(ph[key][s], 16)
                for s in range(2):
                    load(s, s)
                with sp.Fori(0, NCHUNK // 2 - 1) as it:
                    for s in range(2):
                        hold(sp, "sp", ph[used], it * 2 + s + 1)
                        load(s, it * 2 + s + 2)

            for s in range(2):
                sp.wait_ge(HE["scattered"][s], 16 * TE // 2)
            pu = ((sp_a, row_table, HROW), (sp_b, agg_dram, D))
            pass_in("load1", "used1", pu)
            sp.wait_ge(ph["used1"], ph.upto("used1", NCHUNK))
            pass_in("load2", "used2", pu)
            sp.wait_ge(ph["used2"], ph.upto("used2", NCHUNK))
            pass_in("load3", "used3", ((sp_a, x0_dram, D),))
            with sp.Fori(0, NCHUNK // 2) as it:
                for s in range(2):
                    hold(sp, "sp", ph["rows"], ph.upto("rows", it * 2 + s + 1))
                    sp.dma_start(chunk(out, it * 2 + s, D, CN), flat(sp_b[s])).then_inc(ph["store"][s], 16)
            for s in range(2):
                sp.wait_ge(ph["store"][s], ph.upto("store", 16 * NCHUNK // 2))

        @block.sync
        def _(sp):
            sp_load_inputs(sp)
            sp_table0(sp)
            for k in range(4):
                sp_sort(sp, k)
            for l in range(L):
                sp_pairs(sp, l)
                sp_node(sp, l)
            sp_hyp(sp)
            sp_final(sp)

        def pool_constants(gp):
            GP.memset(ones[:, :], 1.0).then_inc(s_const, 1)
            GP.memset(ident[:, :], 0.0).then_inc(s_const, 1)
            GP.memset(zeros[:, :], 0.0).then_inc(s_const, 1)
            GP.memset(power[:, 0:1], 0.5).then_inc(s_const, 1)
            GP.memset(power[:, 1:2], -0.5).then_inc(s_const, 1)
            gp.wait_ge(s_const, 5)
            GP.affine_select(out=ident[:, :], in_=ident[:, :], compare_op=ALU.not_equal, fill=1.0, base=0,
                             pattern=[[-1, 128]], channel_multiplier=1).then_inc(s_const, 1)
            GP.affine_select(out=tri_lt[:, :], in_=ones[:, :], compare_op=ALU.is_gt, fill=0.0, base=0,
                             pattern=[[1, 128]], channel_multiplier=-1).then_inc(s_const, 1)
            GP.affine_select(out=tri_gt[:, :], in_=ones[:, :], compare_op=ALU.is_gt, fill=0.0, base=0,
                             pattern=[[-1, 128]], channel_multiplier=1).then_inc(s_const, 1)
            GP.iota(digits_i[:, :], pattern=[[1, RADIX]], base=0, channel_multiplier=0).then_inc(s_const, 1)
            GP.iota(position_i[:, :], pattern=[[1, TE]], base=0, channel_multiplier=TE).then_inc(s_const, 1)

        def pool_sort(gp, k, limit):
            if k:
                gp.wait_ge(SORT[k - 1]["rec"], SORT[k - 1].upto("rec", 16))

            def body(it, s, c):
                hold(gp, "pool", SORT[k]["staged"], SORT[k].upto("staged", c + 1))
                for j in range(CE):
                    gp.indirect_dma_start(rec_dram, bass.IndirectOffsetOnAxis(ap=place_i[0:P, s, j:j + 1], axis=0),
                                          rec_stage[0:P, s, j * REC:(j + 1) * REC], None,
                                          bounds_check=limit, oob_is_err=False).then_inc(SORT[k]["scattered"][s], 16)
            steps(gp, NCHUNK, body)

        def pool_gather(gp, dst, table, idx, limit, signal):
            gp.indirect_dma_start(dst, None, table, bass.IndirectOffsetOnAxis(ap=idx, axis=0),
                                  bounds_check=limit, oob_is_err=False).then_inc(signal, 16)

        def pool_edges(gp, l, limit, limit_e):
            ph = EDGE[l]
            before = TAB if l == 0 else NODE[l - 1]
            for s in range(2):
                gp.wait_ge(before["store"][s], before.upto("store", 16 * NCHUNK // 2))

            def ends(it, s, c):
                hold(gp, "pool", ph["rows"], ph.upto("rows", c - 1))
                hold(gp, "pool", ph["idx"], ph.upto("idx", c + 1))
                for j in range(CE):
                    pool_gather(gp, g_src[s][:, j, :], gat_table[l], idx_a[0:P, s, j:j + 1], limit, ph["gathered"][s])
                    pool_gather(gp, g_dst[s][:, j, :], gat_table[l], idx_b[0:P, s, j:j + 1], limit, ph["gathered"][s])
            steps(gp, NCHUNK, ends)
            gp.wait_ge(ph["pair"], ph.upto("pair", 16 * NCHUNK))

            def pairs(it, s, c):
                hold(gp, "pool", ph["copied"], ph.upto("copied", c - 1))
                hold(gp, "pool", ph["idx"], ph.upto("idx", NCHUNK + c + 1))
                for j in range(CE):
                    pool_gather(gp, perm[s][:, j, :], pair_dram, idx_a[0:P, s, j:j + 1], limit_e, ph["permuted"][s])
            steps(gp, NCHUNK, pairs)

        def pool_scatter(gp, ph, table, stage, limit):
            def body(it, s, c):
                hold(gp, "pool", ph["stage"], ph.upto("stage", c + 1))
                for j in range(CE):
                    gp.indirect_dma_start(table, bass.IndirectOffsetOnAxis(ap=idx_b[0:P, s, j:j + 1], axis=0),
                                          stage[s][:, j, :], None, bounds_check=limit, oob_is_err=False).then_inc(ph["scattered"][s], 16)
            steps(gp, NCHUNK, body)

        def pool_node(gp, l):
            ph = NODE[l]

            def body(it, s, c):
                hold(gp, "pool", ph["load"][s], ph.upto("load", it * 48 + 48))
                GP.tensor_tensor(n_f[s], n_f[s], n_r[s], ALU.add).then_inc(ph["pre"], 1)
                hold(gp, "pool", ph["pre"], ph.upto("pre", c * 3 + 1))
                GP.tensor_tensor(n_f[s], n_f[s], rows_of(b1_row[l], CN), ALU.add).then_inc(ph["pre"], 1)
                GP.tensor_tensor(n_r[s], n_h[s][:, :, 0:D], rows_of(b2_row[l], CN), ALU.add).then_inc(ph["pre"], 1)
                hold(gp, "pool", ph["var"], ph.upto("var", c + 1))
                GP.tensor_tensor(small[0:P, 2, :], small[0:P, 1, :], power[0:P, 1:2].broadcast_to([P, CN]), ALU.pow).then_inc(ph["rstd"], 1)
            steps(gp, NCHUNK, body)

        def pool_pow(gp, ph, n, out_, in_, which):
            gp.wait_ge(ph["pool_asked"], ph.upto("pool_asked", n + 1))
            GP.tensor_tensor(out_, in_, power[0:P, which:which + 1].broadcast_to([P, in_.shape[1]]), ALU.pow).then_inc(ph["pool"], 1)

        @block.gpsimd
        def _(gp):
            pool_constants(gp)
            limit, limit_e = gp.to_reg(N - 1), gp.to_reg(E - 1)
            for k in range(4):
                pool_sort(gp, k, limit_e)
            gp.wait_ge(s_zeroed, 16 * 3 * NCHUNK)
            for l in range(L):
                pool_edges(gp, l, limit, limit_e)
                for d in range(2):
                    pool_scatter(gp, ATT[l][d], corr_dram[d], gat_stage, limit)
                pool_node(gp, l)
            pool_pow(gp, HYP, 0, bias_sc[0:P, 1:2], bias_sc[0:P, 0:1], 0)
            pool_pow(gp, HYP, 1, sc[3], sc[2], 1)
            pool_pow(gp, HYP, 2, sc[5], sc[4], 0)
            pool_pow(gp, HYP, 3, sc[4], sc[0], 0)
            pool_pow(gp, HYP, 4, sc[1], sc[11], 0)
            for s in range(2):
                gp.wait_ge(HYP["store2"][s], 32 * NCHUNK // 2)

            def ends(it, s, c):
                hold(gp, "pool", HE["rows"], c - 1)
                hold(gp, "pool", HE["idx"], c + 1)
                for j in range(CE):
                    pool_gather(gp, h_row[s][:, j, :], row_table, idx_a[0:P, s, j:j + 1], limit, HE["gathered"][s])
                    pool_gather(gp, h_col[s][:, j, :], col_table, idx_b[0:P, s, j:j + 1], limit, HE["gathered"][s])
            steps(gp, NCHUNK, ends)
            pool_pow(gp, HE, 0, sc[5][:, 0:TE], sc[3][:, 0:TE], 0)
            pool_scatter(gp, HE, agg_dram, hyp_stage, limit)
            pool_pow(gp, FIN, 0, sc[2], sc[0], 0)
            pool_pow(gp, FIN, 1, sc[2], sc[0], 0)
            pool_pow(gp, FIN, 2, sc[2], sc[1], 1)
            pool_pow(gp, FIN, 3, sc[2], sc[0], 0)
            pool_pow(gp, FIN, 4, sc[3], sc[1], 0)
            pool_pow(gp, FIN, 5, sc[2], sc[1], 1)

        def act_copy(dst, src):
            return A.activation(dst, src, ACT.Copy)

        def act_weights(act):
            for l in range(L):
                act.wait_ge(WP["t"], l + 1)
                act_copy(w_t[l], bank(0)[:, 0:R * D]).then_inc(WP["tc"], 1)
                act.wait_ge(WP["mm"], l + 1)
                for d in range(2):
                    for h in range(H):
                        act_copy(edge_w[l][:, d, :].rearrange("i (g h n) -> i g h n", g=2, h=H)[:, :, h, :],
                                 bank((1, 4)[h])[0:64, 0:R * D].rearrange("i (g d n) -> i g d n", g=2, d=2)[:, :, d, :])
                act_copy(dense_w[l][:, :], bank(2)[0:64, 0:D]).then_inc(WP["act"], 1)
            act.wait_ge(WP["mm"], L + 1)
            act_copy(lin_t[:, :], bank(0)[0:64, 0:D])
            act_copy(att_t[:, :], bank(0)[0:64, D:3 * D])
            act_copy(hyp_row["wd"][:, :], bank(0)[:, 3 * D:4 * D])
            act_copy(hyp_row["wg"][:, :], bank(0)[:, 4 * D:5 * D]).then_inc(WP["act"], 1)

        def act_groups(act, ph, base, parity, n):
            for j in range(n):
                b = (parity + j) % 2
                hold(act, "act", ph["mm"], ph.upto("mm", base + j - 1))
                hold(act, "act", ph["tr"], ph.upto("tr", base + j + 1))
                act_copy(trv[b], bank(b)[0:64, 0:GRP * P]).then_inc(ph["trc"], 1)

        def act_table0(act):
            steps(act, NCHUNK, lambda it, s, c: act_groups(act, TAB, c * NTAB_G, s * NTAB_G, NTAB_G))

        def act_edges(act, l):
            ph = EDGE[l]
            act.wait_ge(ORD[0]["done"], ORD[0].upto("done", 1))

            def ends(it, s, c):
                hold(act, "act", ph["gathered"][s], ph.upto("gathered", it * (32 * CE)))
                act_copy(idx_a[0:P, s, :], src_i[0][0:P, bass.ds(c * CE, CE)])
                act_copy(idx_b[0:P, s, :], dst_i[0][0:P, bass.ds(c * CE, CE)]).then_inc(ph["idx"], 1)
            steps(act, NCHUNK, ends)
            act.wait_ge(ORD[1]["done"], ORD[1].upto("done", 1))
            for s in range(2):
                act.wait_ge(ph["gathered"][s], ph.upto("gathered", 32 * CE * NCHUNK // 2))

            def copy_out(s, c, it1):
                hold(act, "act", ph["permuted"][s], ph.upto("permuted", it1 * (16 * CE)))
                act_copy(G[1][:, bass.ds(c * CE, CE), :], perm[s]).then_inc(ph["copied"], 1)

            def stage(s, c):
                act_copy(idx_a[0:P, s, :], pair_i[0:P, bass.ds(c * CE, CE)]).then_inc(ph["idx"], 1)

            for s in range(2):
                stage(s, s)
            with act.Fori(0, NCHUNK // 2 - 1) as it:
                for s in range(2):
                    copy_out(s, it * 2 + s, it + 1)
                    stage(s, it * 2 + s + 2)
            for s in range(2):
                copy_out(s, NCHUNK - 2 + s, NCHUNK // 2)

        def act_attention(act, l, d):
            ph = ATT[l][d]
            Es, Sf, F, B, mx, pp = att
            act.wait_ge(ph["dve"], ph.upto("dve", 1))
            A.activation(pp, F, ACT.Exp)
            A.activation(Sf, B, ACT.Exp).then_inc(ph["exp"], 1)
            act.wait_ge(ph["sums"], ph.upto("sums", 1))
            act_copy(carry4[0:P, 2:4, :], bank(7)[0:P, 0:8].rearrange("p (k s) -> p k s", k=2)).then_inc(ph["exp"], 1)

            def group(it, s, g):
                hold(act, "act", ph["tr"], ph.upto("tr", g - 1))
                act_copy(grp_stage[0:P, s, :].rearrange("p (t w) -> p t w", w=D), G[d][:, bass.ds(g * GRP, GRP), 0:D]).then_inc(ph["copied"], 1)
                hold(act, "act", ph["mm"], ph.upto("mm", g - 1))
                hold(act, "act", ph["tr"], ph.upto("tr", g + 1))
                act_copy(trv[s], bank(s)[0:64, 0:GRP * P]).then_inc(ph["trc"], 1)
            steps(act, NGRP, group)
            act_carry(act, ph)

        def act_carry(act, ph):
            act.wait_ge(ph["cv"], ph.upto("cv", 1))
            act_copy(carry_v[0:P, :], bank(7)[0:P, 64:64 + D]).then_inc(ph["cvc"], 1)

        def act_node(act, l):
            ph, ng, nb = NODE[l], NODE_G[l], CN // GRP

            def body(it, s, c):
                act_groups(act, ph, c * ng, s * ng, nb)
                hold(act, "act", ph["u"], ph.upto("u", c + 1))
                A.activation(n_u, n_u, ACT.Tanh).then_inc(ph["th"], 1)
                act_groups(act, ph, c * ng + nb, s * ng + nb, nb)
                if l + 1 < L:
                    act_groups(act, ph, c * ng + 2 * nb, s * ng + 2 * nb, nb)
            steps(act, NCHUNK, body)

        def act_logs(act, ph, n, c_, lp, lm):
            act.wait_ge(ph["act_asked"], ph.upto("act_asked", n + 1))
            A.activation(lp, c_, ACT.Ln, bias=1.0)
            A.activation(lm, c_, ACT.Ln, bias=1.0, scale=-1.0).then_inc(ph["act"], 1)

        def act_fn(act, ph, n, out_, in_, fn, **kw):
            act.wait_ge(ph["act_asked"], ph.upto("act_asked", n + 1))
            A.activation(out_, in_, fn, **kw).then_inc(ph["act"], 1)


        def ends_idx(act, ph, order):
            def ends(it, s, c):
                hold(act, "act", ph["gathered"][s], ph.upto("gathered", it * (32 * CE)))
                act_copy(idx_a[0:P, s, :], src_i[order][0:P, bass.ds(c * CE, CE)])
                act_copy(idx_b[0:P, s, :], dst_i[order][0:P, bass.ds(c * CE, CE)]).then_inc(ph["idx"], 1)
            steps(act, NCHUNK, ends)

        @block.scalar
        def _(act):
            act_weights(act)
            act_table0(act)
            for l in range(L):
                act_edges(act, l)
                for d in range(2):
                    act_attention(act, l, d)
                act_node(act, l)
            act_fn(act, HYP, 0, bias_sc[0:P, 2:3], bias_sc[0:P, 1:2], ACT.Tanh)
            act_logs(act, HYP, 1, sc[6], sc[7], sc[8])
            steps(act, NCHUNK, lambda it, s, c: act_groups(act, HYP, c * NTAB_G, s * NTAB_G, NTAB_G))
            act_fn(act, HYP, 2, sc[6], sc[5], ACT.Tanh)
            act_logs(act, HYP, 3, sc[6], sc[7], sc[8])
            steps(act, NCHUNK, lambda it, s, c: act_groups(act, HYP, c * NTAB_G + NCHUNK * NTAB_G, s * NTAB_G, NTAB_G))
            ends_idx(act, HE, 1)
            act_logs(act, HE, 0, sc[6][:, 0:TE], sc[7][:, 0:TE], sc[8][:, 0:TE])

            def gate(it, s, c):
                hold(act, "act", HE["pre"], c + 1)
                A.activation(hyp_stage[s], edges_pre[:, bass.ds(c * CE, CE), :], ACT.Sigmoid).then_inc(HE["gate"], 1)
            steps(act, NCHUNK, gate)
            act_fn(act, HE, 1, sc[2][:, 0:TE], sc[0][:, 0:TE], ACT.Sigmoid, bias=att_b2[0:P, :])
            act_carry(act, HE)
            act_fn(act, FIN, 0, sc[5], sc[4], ACT.Tanh)
            act_logs(act, FIN, 1, sc[6], sc[7], sc[8])
            act_fn(act, FIN, 2, sc[4], sc[2], ACT.Tanh)
            act_logs(act, FIN, 3, sc[6], sc[7], sc[8])
            act_fn(act, FIN, 4, sc[4], sc[3], ACT.Tanh)

        def mm(out_, w, x, start=True, stop=True):
            return T.matmul(out_, w, x, start=start, stop=stop)

        def pe_weights(pe):
            pe.wait_ge(s_w, NW)
            pe.wait_ge(s_const, NCONST)
            for l in range(L):
                if l:
                    pe.wait_ge(WP["act"], l)
                for r in range(R):
                    t = T.transpose(bank(0)[:, r * D:(r + 1) * D], w_raw[l][:, r * H * D:(r + 1) * H * D], ident[0:64, 0:64])
                t.then_inc(WP["t"], 1)
                pe.wait_ge(WP["tc"], l + 1)
                for r in range(R):
                    for h in range(H):
                        mm(bank((1, 4)[h])[0:64, r * D:(r + 1) * D], w_t[l][h * D:(h + 1) * D, r * D:(r + 1) * D],
                           w1_edge[l][h * D:(h + 1) * D, r * D:(r + 1) * D])
                for r in range(R):
                    mm(bank(2)[0:64, 0:D], w_t[l][:, r * D:(r + 1) * D], w1_edge[l][:, r * D:(r + 1) * D], start=(r == 0), stop=False)
                mm(bank(2)[0:64, 0:D], ident[0:64, 0:64], w1_top[l], start=False)
                for r in range(R):
                    t = mm(bank(3)[:, 0:D], gat_b[l][:, r:r + 1].broadcast_to([128, 128]), w1_edge[l][:, r * D:(r + 1) * D],
                           start=(r == 0), stop=(r == R - 1))
                t.then_inc(WP["mm"], 1)
                pe.wait_ge(WP["row"], l + 1)
            pe.wait_ge(WP["act"], L)
            T.transpose(bank(0)[0:64, 0:D], lin_raw, ident[0:64, 0:64])
            for k in range(2):
                T.transpose(bank(0)[0:64, (1 + k) * D:(2 + k) * D], att_raw[:, k * D:(k + 1) * D], ident[0:64, 0:64])
            for k in range(2):
                t = mm(bank(0)[:, (3 + k) * D:(4 + k) * D], att_raw[:, 2 * D + k:2 * D + k + 1].broadcast_to([64, 128]), ident[0:64, 0:64])
            t.then_inc(WP["mm"], 1)
            pe.wait_ge(WP["act"], L + 1)

        def pe_transpose_group(pe, ph, b, value, tile):
            hold(pe, "pe", ph["trc"], ph.upto("trc", value - 1))
            for i in range(GRP):
                t = T.transpose(bank(b)[0:64, i * P:(i + 1) * P], tile(i), ident[0:P, 0:P])
            t.then_inc(ph["tr"], 1)

        def pe_groups(pe, ph, base, parity, n, tile, w, out_):
            def products(j):
                hold(pe, "pe", ph["trc"], ph.upto("trc", base + j + 1))
                b = (parity + j) % 2
                for i in range(GRP):
                    t = mm(out_(j * GRP + i), trv[b][:, i * P:(i + 1) * P], w)
                t.then_inc(ph["mm"], 1)
            for j in range(n):
                pe_transpose_group(pe, ph, (parity + j) % 2, base + j, lambda i: tile(j * GRP + i))
                if j:
                    products(j - 1)
            products(n - 1)

        def out_tile(b, width):
            return lambda t: ps[0:P, b * 512 + t * width:b * 512 + (t + 1) * width]

        def pe_table0(pe):
            def body(it, s, c):
                hold(pe, "pe", TAB["load"][s], it * 16 + 16)
                hold(pe, "pe", TAB["rows"], c)
                pe_groups(pe, TAB, c * NTAB_G, s * NTAB_G, NTAB_G, lambda t: tab_rows[s][:, t, 0:D], proj_w[0][:, :], out_tile(5, 16))
            steps(pe, NCHUNK, body)

        def pe_sort(pe, k):
            pe.wait_ge(SORT[k]["hist"], SORT[k].upto("hist", 1))
            mm(bank(7)[0:P, 0:RADIX], tri_lt[0:P, 0:P], hist[0:P, :])
            mm(bank(7)[0:P, RADIX:2 * RADIX], ones[0:P, 0:P], hist[0:P, :]).then_inc(SORT[k]["base"], 1)

        def pe_order(pe, o):
            pe.wait_ge(ORD[o]["diag"], ORD[o].upto("diag", 1))
            for k in range(2):
                t = mm(bank(7)[0:P, k * 128:k * 128 + P], ones[0:P, 0:P], key_diag[0:P, k, 0:P])
            t.then_inc(ORD[o]["bc"], 1)

        def pe_carry(pe, ph, o, v_last):
            pe.wait_ge(ph["scan"], ph.upto("scan", 1))
            mm(bank(7)[0:P, 64:64 + D], carry_f[o][0:P, 0:P], v_last).then_inc(ph["cv"], 1)

        def pe_attention(pe, l, d):
            ph = ATT[l][d]
            for k in range(2):
                pe.wait_ge(ph["diag"], ph.upto("diag", k + 1))
                mm(bank(6)[0:P, 0:4 * P], ones[0:P, 0:P], diag[0:P, :, :].rearrange("p s q -> p (s q)")).then_inc(ph["bc"], 1)
            pe.wait_ge(ph["diag"], ph.upto("diag", 3))
            mm(bank(7)[0:P, 0:4], carry_f[d][0:P, 0:P], att[2][:, :, TE - 1])
            mm(bank(7)[0:P, 4:8], carry_b[d][0:P, 0:P], att[3][:, :, 0]).then_inc(ph["sums"], 1)

            def group(it, s, g):
                hold(pe, "pe", ph["copied"], ph.upto("copied", g + 1))
                pe_transpose_group(pe, ph, s, g, lambda i: grp_stage[0:P, s, i * D:(i + 1) * D])
                hold(pe, "pe", ph["trc"], ph.upto("trc", g + 1))
                hold(pe, "pe", ph["prod"], ph.upto("prod", g - 1))
                for i in range(GRP):
                    t = mm(bank(2 + 2 * s, 2)[0:P, i * 4 * D:(i + 1) * 4 * D], trv[s][:, i * P:(i + 1) * P], edge_w[l][:, d, :])
                t.then_inc(ph["mm"], 1)
            steps(pe, NGRP, group)
            pe_carry(pe, ph, d, G[d][:, TE - 1, 0:D])

        def pe_node(pe, l):
            ph, ng, nb = NODE[l], NODE_G[l], CN // GRP

            def body(it, s, c):
                hold(pe, "pe", ph["load"][s], ph.upto("load", it * 48 + 48))
                hold(pe, "pe", ph["z"], ph.upto("z", c))
                pe_groups(pe, ph, c * ng, s * ng, nb, lambda t: n_h[s][:, t, 0:D], dense_w[l][:, :], out_tile(2, D))
                hold(pe, "pe", ph["th"], ph.upto("th", c + 1))
                pe_groups(pe, ph, c * ng + nb, s * ng + nb, nb, lambda t: n_u[:, t, :], mlp_w2[l][:, :], out_tile(2, D))
                if l + 1 < L:
                    hold(pe, "pe", ph["h"], ph.upto("h", c + 1))
                    pe_groups(pe, ph, c * ng + 2 * nb, s * ng + 2 * nb, nb, lambda t: tab_rows[s][:, t, 0:D], proj_w[l + 1][:, :], out_tile(5, 16))
            steps(pe, NCHUNK, body)

        def pe_hyp(pe):
            ph = HYP

            def lin(it, s, c):
                hold(pe, "pe", ph["x0"], ph.upto("x0", c + 1))
                hold(pe, "pe", ph["y"], ph.upto("y", c))
                pe_groups(pe, ph, c * NTAB_G, s * NTAB_G, NTAB_G, lambda t: sp_a[s][:, t, :], lin_t[:, :], out_tile(2, D))
            steps(pe, NCHUNK, lin)

            def mlp(it, s, c):
                hold(pe, "pe", ph["x1"], ph.upto("x1", c + 1))
                hold(pe, "pe", ph["rows"], ph.upto("rows", c))
                pe_groups(pe, ph, c * NTAB_G + NCHUNK * NTAB_G, s * NTAB_G, NTAB_G, lambda t: hyp_r[s][:, t, 0:D], att_t[:, :], out_tile(2, 2 * D))
            steps(pe, NCHUNK, mlp)

        @block.tensor
        def _(pe):
            pe_weights(pe)
            pe.wait_ge(WP["dve"], 1)
            pe_table0(pe)
            pe_sort(pe, 0)
            pe_sort(pe, 1)
            pe_order(pe, 0)
            pe_sort(pe, 2)
            pe_sort(pe, 3)
            pe_order(pe, 1)
            for l in range(L):
                for d in range(2):
                    pe_attention(pe, l, d)
                pe_node(pe, l)
            pe_hyp(pe)
            pe_carry(pe, HE, 1, edges_v[:, TE - 1, :])

        @block.vector
        def _(dve):
            chain = [0]

            def link(ins, wait=True):
                chain[0] += 1
                ins.then_inc(s_link, 1)
                if wait:
                    dve.wait_ge(s_link, chain[0])

            def reset():
                if chain[0]:
                    dve.wait_ge(s_link, chain[0])
                    dve.sem_clear(s_link)
                    chain[0] = 0

            def done(s):
                if chain[0]:
                    dve.wait_ge(s_link, chain[0])
                dve.sem_inc(s, 1)

            def wait(s, v):
                hold(dve, "dve", s, v)

            def tt(o, x, y, op, w=True):
                link(V.tensor_tensor(o, x, y, op), w)

            def ts(o, x, s1, s2, op0, op1=None, w=True):
                link(V.tensor_scalar(o, x, s1, s2, op0, op1) if op1 is not None else V.tensor_scalar(o, x, s1, None, op0), w)

            def stt(o, x, s, y, op0, op1, w=True):
                link(V.scalar_tensor_tensor(o, x, s, y, op0, op1), w)

            def red(o, x, op=ALU.add, w=True):
                link(V.tensor_reduce(o, x, X, op), w)

            def copy(o, x, w=True):
                link(V.tensor_copy(o, x), w)

            def recip(o, x):
                link(V.reciprocal(o, x))

            def center(x, mean, n):
                red(mean, x)
                ts(mean, mean, -1.0 / D, None, ALU.mult)
                tt(x, x, cols(mean), ALU.add)

            def sum_squares(o, x, tmp):
                tt(tmp, x, x, ALU.mult)
                red(o, tmp)

            asked = {}

            def ask(ph, who):
                key = (id(ph), who)
                asked[key] = asked.get(key, 0) + 1
                done(ph[who + "_asked"])
                dve.wait_ge(ph[who], asked[key])

            def artanh_ratio(o, c, lp, lm, t1, t2):
                tt(t1, c, c, ALU.mult)
                ts(o, t1, 1.0 / 13, None, ALU.mult)
                for k in (11, 9, 7, 5, 3):
                    stt(o, o, 1.0 / k, t1, ALU.add, ALU.mult)
                ts(o, o, 1.0, None, ALU.add)
                tt(t2, lp, lm, ALU.subtract)
                recip(t1, c)
                stt(t2, t2, 0.5, t1, ALU.mult, ALU.mult)
                ts(t1, c, 0.25, None, ALU.is_lt)
                tt(o, o, t2, ALU.subtract)
                tt(o, o, t1, ALU.mult)
                tt(o, o, t2, ALU.add)

            dve.wait_ge(s_w, NW)
            for l in range(L):
                for k in range(2):
                    tt(w_prod, w_raw[l], a_raw[l][:, k * R * H * D:(k + 1) * R * H * D], ALU.mult)
                    red(w_red[:, k * R * H:(k + 1) * R * H], w_prod.rearrange("i (r c) -> i r c", c=D))
                for k in range(2):
                    for d in range(2):
                        copy(proj_w[l][:, k * 8 + d * 4:k * 8 + d * 4 + 4].rearrange("i (g h) -> i g h", g=2),
                             w_red[:, k * 8:(k + 1) * 8].rearrange("i (g d h) -> i g d h", g=2, d=2)[:, :, d, :])
            done(WP["dve"])
            for l in range(L):
                dve.wait_ge(WP["mm"], l + 1)
                tt(b1_row[l][:, :], b1_row[l][:, :], bank(3)[:, 0:D], ALU.add)
                done(WP["row"])
            reset()

            def table0(it, s, c):
                wait(TAB["mm"], (c + 1) * NTAB_G)
                copy(tab_rows[s][:, :, D:ROW], bank(5)[0:P, 0:CN * 16].rearrange("p (t w) -> p t w", w=16))
                done(TAB["rows"])
                reset()
            steps(dve, NCHUNK, table0)

            dve.wait_ge(s_in, 64)
            dve.wait_ge(s_const, NCONST)
            copy(digits_row[:, :], digits_i[:, :], False)
            for k in range(2):
                copy(rec_v[:, :, k], (dst_i, src_i)[k][1][0:P, :], False)
                copy(rec_v[:, :, 2 + k], off[0][0:P, k, :], False)
            copy(rec_v[:, :, 4], position_i[0:P, :])

            def sort_pass(k):
                ph = SORT[k]
                key, high = k // 2, k % 2
                if k:
                    dve.wait_ge(SORT[k - 1]["rec"], SORT[k - 1].upto("rec", 16))
                copy(digit_i[0:P, :], rec_v[:, :, key])
                if high:
                    ts(digit_i[0:P, :], digit_i[0:P, :], 8, None, ALU.logical_shift_right)
                else:
                    ts(digit_i[0:P, :], digit_i[0:P, :], RADIX - 1, None, ALU.bitwise_and)
                copy(digit[0:P, :], digit_i[0:P, :])
                link(V.memset(hist[0:P, :], 0.0))
                reset()
                with dve.Fori(0, NCHUNK) as c:
                    for j in range(CE):
                        stt(hist[0:P, :], digits_row[0:P, :], digit[0:P, bass.ds(c * CE + j, 1)], hist[0:P, :], ALU.is_equal, ALU.add)
                    reset()
                done(ph["hist"])
                dve.wait_ge(ph["base"], ph.upto("base", 1))
                copy(total[0:P, :], bank(7)[0:P, RADIX:2 * RADIX])
                link(V.tensor_tensor_scan(cursor[0:P, :], ones[0:P, 0:1].broadcast_to([P, RADIX]), total[0:P, :], 0.0, ALU.mult, ALU.add))
                tt(cursor[0:P, :], cursor[0:P, :], total[0:P, :], ALU.subtract)
                tt(cursor[0:P, :], cursor[0:P, :], bank(7)[0:P, 0:RADIX], ALU.add)
                reset()

                def places(it, s, c):
                    for j in range(CE):
                        mine = digit[0:P, bass.ds(c * CE + j, 1)]
                        link(V.scalar_tensor_tensor(matched[0:P, :], digits_row[0:P, :], mine, cursor[0:P, :], ALU.is_equal, ALU.mult,
                                                    accum_out=rank[0:P, j:j + 1]))
                        stt(cursor[0:P, :], digits_row[0:P, :], mine, cursor[0:P, :], ALU.is_equal, ALU.add)
                    wait(ph["scattered"][s], ph.upto("scattered", it * (16 * CE)))
                    copy(place_i[0:P, s, :], rank[0:P, :], False)
                    copy(rec_stage[0:P, s, :].rearrange("p (t c) -> p t c", c=REC), rec_v[:, bass.ds(c * CE, CE), :])
                    done(ph["staged"])
                    reset()
                steps(dve, NCHUNK, places)

            def order_info(o):
                key = rec_v[:, :, o]
                dve.wait_ge(SORT[2 * o + 1]["rec"], SORT[2 * o + 1].upto("rec", 16))
                copy(dst_i[o][0:P, :], rec_v[:, :, 0], False)
                copy(src_i[o][0:P, :], rec_v[:, :, 1], False)
                for g, op in enumerate((ALU.is_gt, ALU.is_lt)):
                    ts(off[o][0:P, g, :], rec_v[:, :, 2], 0.0, BIG, op, ALU.mult)
                    ts(off[o][0:P, g, :], off[o][0:P, g, :], -BIG, None, ALU.add)
                link(V.memset(keep[o][0:P, 0:1], 0.0), False)
                link(V.memset(keep_b[o][0:P, TE - 1:TE], 0.0), False)
                tt(keep[o][0:P, 1:TE], key[:, 1:TE], key[:, 0:TE - 1], ALU.is_equal, False)
                tt(keep_b[o][0:P, 0:TE - 1], key[:, 1:TE], key[:, 0:TE - 1], ALU.is_equal, False)
                ts(first[o][0:P, :], key, key[:, 0:1], None, ALU.is_equal, w=False)
                ts(last[o][0:P, :], key, key[:, TE - 1:TE], None, ALU.is_equal, w=False)
                for k, t in enumerate((0, TE - 1)):
                    ts(key_diag[0:P, k, 0:P], ident[0:P, 0:P], key[:, t:t + 1], None, ALU.mult, w=False)
                done(ORD[o]["diag"])
                dve.wait_ge(ORD[o]["bc"], ORD[o].upto("bc", 1))
                kf, kl = bank(7)[0:P, 0:P], bank(7)[0:P, 128:128 + P]
                k0, k1 = key[:, 0:1], key[:, TE - 1:TE]
                stt(carry_f[o][0:P, 0:P], kf, k1, tri_lt[0:P, 0:P], ALU.is_equal, ALU.mult, False)
                stt(carry_b[o][0:P, 0:P], kl, k0, tri_gt[0:P, 0:P], ALU.is_equal, ALU.mult, False)
                stt(far_f[o][0:P, 0:P], kl, k0, tri_gt[0:P, 0:P], ALU.is_equal, ALU.mult, False)
                stt(far_b[o][0:P, 0:P], kf, k1, tri_lt[0:P, 0:P], ALU.is_equal, ALU.mult)
                red(goes_on[0:P, :], far_b[o][0:P, 0:P], ALU.max)
                for m in (far_f, far_b):
                    ts(m[o][0:P, 0:P], m[o][0:P, 0:P], BIG, -BIG, ALU.mult, ALU.add, w=False)
                stt(digit[0:P, :], keep_b[o][0:P, :], float(SKIP), key, ALU.mult, ALU.add)
                stt(digit[0:P, TE - 1:TE], goes_on[0:P, :], float(SKIP), digit[0:P, TE - 1:TE], ALU.mult, ALU.add)
                copy(out_i[o][0:P, :], digit[0:P, :], False)
                if o:
                    copy(pair_i[0:P, :], rec_v[:, :, 4], False)
                    copy(weight1[0:P, :], rec_v[:, :, 3], False)
                done(ORD[o]["done"])

            for o in range(2):
                for k in range(2):
                    sort_pass(2 * o + k)
                order_info(o)
                if o == 0:
                    copy(rec_v[:, :, 4], position_i[0:P, :])
            reset()

            def edge_rows(l):
                ph = EDGE[l]

                def body(it, s, c):
                    wait(ph["gathered"][s], ph.upto("gathered", it * (32 * CE) + 32 * CE))
                    g, a_, b_ = G[0][:, bass.ds(c * CE, CE), :], g_src[s], g_dst[s]
                    es, ed = D, D + 8
                    tt(g[:, :, 0:D], a_[:, :, 0:D], b_[:, :, 0:D], ALU.subtract, False)
                    tt(g[:, :, D:D + 4], a_[:, :, es:es + 4], b_[:, :, ed:ed + 4], ALU.add, False)
                    tt(g[:, :, D + 4:D + 8], b_[:, :, es:es + 4], b_[:, :, ed:ed + 4], ALU.add, False)
                    tt(g[:, :, D + 8:D + 12], b_[:, :, es + 4:es + 8], a_[:, :, ed + 4:ed + 8], ALU.add, False)
                    tt(g[:, :, D + 12:D + 16], a_[:, :, es + 4:es + 8], a_[:, :, ed + 4:ed + 8], ALU.add, False)
                    done(ph["rows"])
                    reset()
                steps(dve, NCHUNK, body)

            def scan(o, d0, d1, init, op0, op1, back=False, w=False):
                if back:
                    o, d0, d1 = o[:, ::-1], d0[:, ::-1], d1[:, ::-1]
                link(V.tensor_tensor_scan(o, d0, d1, init, op0, op1), w)

            def attention(l, d):
                ph, o = ATT[l][d], d
                Es, Sf, F, B, mx, pp = att
                if d:
                    dve.wait_ge(EDGE[l]["copied"], EDGE[l].upto("copied", NCHUNK))
                for k, m in enumerate((keep, keep_b, first, last)):
                    ts(seg_off[0:P, k, :], m[o][0:P, :], BIG, -BIG, ALU.mult, ALU.add, w=False)
                for to, at in ((Es, D + 8 * d), (Sf, D + 8 * d + 4)):
                    x = G[d][:, :, at:at + 4].rearrange("p t s -> p s t")
                    stt(to, x, 0.2, x, ALU.mult, ALU.max, False)
                dve.wait_ge(s_link, chain[0])
                for g in range(2):
                    tt(Es[:, 2 * g:2 * g + 2, :], Es[:, 2 * g:2 * g + 2, :], off[o][0:P, g:g + 1, :].broadcast_to([P, 2, TE]), ALU.add, False)
                dve.wait_ge(s_link, chain[0])
                for s in range(4):
                    scan(F[:, s, :], seg_off[0:P, 0, :], Es[:, s, :], -BIG, ALU.add, ALU.max)
                    scan(B[:, s, :], seg_off[0:P, 1, :], Es[:, s, :], -BIG, ALU.add, ALU.max, back=True)
                dve.wait_ge(s_link, chain[0])
                tt(mx, F, B, ALU.max)
                tt(mx, mx, Sf, ALU.max)
                for k, (edge, farm) in enumerate(((F[:, :, TE - 1], far_f), (B[:, :, 0], far_b))):
                    if k:
                        dve.wait_ge(ph["bc"], ph.upto("bc", k))
                    for s in range(4):
                        ts(diag[0:P, s, :], ident[0:P, 0:P], edge[:, s:s + 1], None, ALU.mult, w=False)
                    done(ph["diag"])
                    dve.wait_ge(ph["bc"], ph.upto("bc", k + 1))
                    tt(far[0:P, :, :], bank(6)[0:P, 0:4 * P].rearrange("p (s q) -> p s q", s=4),
                       farm[o][0:P, 0:P].unsqueeze(1).broadcast_to([P, 4, P]), ALU.add)
                    red(carry4[0:P, k, :], far[0:P, :, :], ALU.max)
                for k in range(2):
                    for s in range(4):
                        stt(mx[:, s, :], seg_off[0:P, 2 + k, :], carry4[0:P, k, s:s + 1], mx[:, s, :], ALU.add, ALU.max, False)
                    dve.wait_ge(s_link, chain[0])
                tt(F, Es, mx, ALU.subtract, False)
                tt(B, Sf, mx, ALU.subtract, False)
                done(ph["dve"])
                dve.wait_ge(ph["exp"], ph.upto("exp", 1))
                for s in range(4):
                    scan(F[:, s, :], keep[o][0:P, :], pp[:, s, :], 0.0, ALU.mult, ALU.add)
                    scan(B[:, s, :], keep_b[o][0:P, :], pp[:, s, :], 0.0, ALU.mult, ALU.add, back=True)
                done(ph["diag"])
                dve.wait_ge(ph["exp"], ph.upto("exp", 2))
                tt(F, F, B, ALU.add)
                tt(F, F, pp, ALU.subtract)
                tt(F, F, Sf, ALU.add)
                for k, m in ((2, first), (3, last)):
                    for s in range(4):
                        stt(F[:, s, :], m[o][0:P, :], carry4[0:P, k, s:s + 1], F[:, s, :], ALU.mult, ALU.add, False)
                    dve.wait_ge(s_link, chain[0])
                recip(F, F)
                stt(Es, pp, 1.0 if d == 0 else -1.0, F, ALU.mult, ALU.mult)
                if d == 0:
                    dve.wait_ge(EDGE[l]["pair"], EDGE[l].upto("pair", 16 * NCHUNK))
                reset()

                def group(it, s, g):
                    wait(ph["mm"], ph.upto("mm", g + 1))
                    pr = prod[0:P, :].rearrange("p (t s n) -> p t s n", t=GRP, s=4)
                    tt(pr, bank(2 + 2 * s, 2)[0:P, :].rearrange("p (t s n) -> p t s n", t=GRP, s=4),
                       Es[:, :, bass.ds(g * GRP, GRP)].rearrange("p s t -> p t s").unsqueeze(3).broadcast_to([P, GRP, 4, D]), ALU.mult)
                    dve.sem_inc(ph["prod"], 1)
                    red(G[d][:, bass.ds(g * GRP, GRP), 0:D], pr.rearrange("p t s n -> p t n s"))
                    reset()
                steps(dve, NGRP, group)

            def segment_sums(ph, v, o):
                with dve.Fori(0, D // 8) as f:
                    for j in range(8):
                        vf = v[:, :, bass.ds(f * 8 + j, 1)].rearrange("p t a -> p (t a)")
                        scan(vf, keep[o][0:P, :], vf, 0.0, ALU.mult, ALU.add)
                    reset()
                done(ph["scan"])
                dve.wait_ge(ph["cvc"], ph.upto("cvc", 1))

            def scatter_rows(ph, v, o, stage, before):
                if before is not None:
                    for s in range(2):
                        dve.wait_ge(before["scattered"][s], before.upto("scattered", 16 * TE // 2))

                def body(it, s, c):
                    wait(ph["scattered"][s], ph.upto("scattered", it * (16 * CE)))
                    tt(stage[s], cols(first[o][0:P, bass.ds(c * CE, CE)]), rows_of(carry_v, CE), ALU.mult)
                    tt(stage[s], stage[s], v[:, bass.ds(c * CE, CE), 0:D], ALU.add, False)
                    copy(idx_b[0:P, s, :], out_i[o][0:P, bass.ds(c * CE, CE)], False)
                    done(ph["stage"])
                    reset()
                steps(dve, NCHUNK, body)

            def node_update(l):
                ph, ng, nb = NODE[l], NODE_G[l], CN // GRP
                z_ps = bank(2, 3)[0:P, 0:CN * D].rearrange("p (t w) -> p t w", w=D)

                def body(it, s, c):
                    wait(ph["pre"], ph.upto("pre", c * 3 + 3))
                    wait(ph["mm"], ph.upto("mm", c * ng + nb))
                    tt(n_u, z_ps, n_f[s], ALU.add)
                    done(ph["u"])
                    wait(ph["mm"], ph.upto("mm", c * ng + 2 * nb))
                    tt(n_z, z_ps, n_r[s], ALU.add)
                    done(ph["z"])
                    center(n_z, small[0:P, 0, :], CN)
                    sum_squares(small[0:P, 1, :], n_z, n_u)
                    ts(small[0:P, 1, :], small[0:P, 1, :], 1.0 / D, 1e-5, ALU.mult, ALU.add)
                    done(ph["var"])
                    wait(ph["rstd"], ph.upto("rstd", c + 1))
                    tt(n_z, n_z, cols(small[0:P, 2, :]), ALU.mult)
                    tt(n_z, n_z, rows_of(g_row[l], CN), ALU.mult)
                    wait(ph["store"][s], ph.upto("store", it * 16))
                    tt(tab_rows[s][:, :, 0:D], n_z, rows_of(be_row[l], CN), ALU.add)
                    if l + 1 < L:
                        done(ph["h"])
                        wait(ph["mm"], ph.upto("mm", c * ng + 3 * nb))
                        copy(tab_rows[s][:, :, D:ROW], bank(5)[0:P, 0:CN * 16].rearrange("p (t w) -> p t w", w=16))
                    done(ph["rows"])
                    reset()
                steps(dve, NCHUNK, body)

            for l in range(L):
                edge_rows(l)
                for d in range(2):
                    attention(l, d)
                    segment_sums(ATT[l][d], G[d], d)
                    scatter_rows(ATT[l][d], G[d], d, gat_stage, ATT[l][0] if d else None)
                node_update(l)

            tt(hyp_tmp[:, 0, :], hyp_bias[0:P, :], hyp_bias[0:P, :], ALU.mult)
            red(bias_sc[0:P, 0:1], hyp_tmp[:, 0, :])
            ask(HYP, "pool")
            ts(bias_sc[0:P, 1:2], bias_sc[0:P, 1:2], MIN_NORM, None, ALU.max)
            ask(HYP, "act")
            ts(bias_sc[0:P, 2:3], bias_sc[0:P, 2:3], MAXNORM, None, ALU.min)
            recip(bias_sc[0:P, 3:4], bias_sc[0:P, 1:2])
            tt(bias_sc[0:P, 3:4], bias_sc[0:P, 3:4], bias_sc[0:P, 2:3], ALU.mult)
            ts(hyp_bias[0:P, :], hyp_bias[0:P, :], bias_sc[0:P, 3:4], None, ALU.mult)
            tt(hyp_tmp[:, 0, :], hyp_bias[0:P, :], hyp_bias[0:P, :], ALU.mult)
            red(bias_sc[0:P, 4:5], hyp_tmp[:, 0, :])
            y2 = bias_sc[0:P, 4:5]
            reset()
            ph = HYP

            def scol(k, c):
                return sc[k][:, bass.ds(c * CN, CN)]

            def residual(it, s, c):
                wait(ph["load"][s], ph.upto("load", it * 32 + 32))
                x = nchunk(c)
                tt(x, sp_a[s], sp_b[s], ALU.add)
                dve.sem_inc(ph["used"], 1)
                center(x, small[0:P, 0, :], CN)
                sum_squares(scol(1, c), x, hyp_tmp)
                reset()
            steps(dve, NCHUNK, residual)
            ts(sc[2], sc[1], 1.0 / D, 1e-5, ALU.mult, ALU.add)
            ask(ph, "pool")
            tt(sc[4], sc[1], sc[3], ALU.mult)
            tt(sc[4], sc[4], sc[3], ALU.mult)
            ask(ph, "pool")
            ts(sc[5], sc[5], MIN_NORM, None, ALU.max)
            ts(sc[6], sc[5], CLIP, None, ALU.min)
            ask(ph, "act")
            artanh_ratio(sc[9], sc[6], sc[7], sc[8], sc[10], sc[4])
            tt(sc[9], sc[9], sc[6], ALU.mult)
            recip(sc[5], sc[5])
            tt(sc[9], sc[9], sc[5], ALU.mult)
            reset()

            def linear(it, s, c):
                if not isinstance(c, int):
                    wait(ph["store"][s], ph.upto("store", it * 16))
                    wait(ph["y"], ph.upto("y", c))
                x = nchunk(c)
                tt(sp_a[s], x, cols(scol(3, c)), ALU.mult)
                done(ph["x0"])
                wait(ph["mm"], ph.upto("mm", (c + 1) * NTAB_G))
                copy(x, bank(2, 3)[0:P, 0:CN * D].rearrange("p (t w) -> p t w", w=D))
                done(ph["y"])
                sum_squares(scol(0, c), x, hyp_tmp)
                tt(hyp_tmp, x, rows_of(hyp_bias, CN), ALU.mult)
                red(scol(2, c), hyp_tmp)
                reset()
            steps(dve, NCHUNK, linear)
            ask(ph, "pool")
            tt(sc[5], sc[4], sc[9], ALU.mult)
            ts(sc[5], sc[5], MIN_NORM, None, ALU.max)
            ask(ph, "act")
            ts(sc[7], sc[6], MAXNORM, None, ALU.min)
            recip(sc[8], sc[5])
            tt(sc[8], sc[8], sc[7], ALU.mult)
            tt(sc[8], sc[8], sc[9], ALU.mult)
            tt(sc[10], sc[8], sc[8], ALU.mult)
            tt(sc[10], sc[10], sc[0], ALU.mult)
            tt(sc[6], sc[8], sc[2], ALU.mult)
            ts(sc[4], sc[6], 2.0, 1.0, ALU.mult, ALU.add)
            stt(sc[7], sc[10], y2, sc[4], ALU.mult, ALU.add)
            ts(sc[7], sc[7], MIN_NORM, None, ALU.max)
            recip(sc[7], sc[7])
            ts(sc[4], sc[4], y2, None, ALU.add)
            tt(sc[8], sc[8], sc[4], ALU.mult)
            tt(sc[8], sc[8], sc[7], ALU.mult)
            ts(sc[5], sc[10], -1.0, 1.0, ALU.mult, ALU.add)
            tt(sc[5], sc[5], sc[7], ALU.mult)
            reset()

            def point(it, s, c):
                x = nchunk(c)
                tt(x, x, cols(scol(8, c)), ALU.mult, False)
                tt(hyp_tmp, cols(scol(5, c)), rows_of(hyp_bias, CN), ALU.mult)
                tt(x, x, hyp_tmp, ALU.add)
                sum_squares(scol(11, c), x, hyp_tmp)
                reset()
            steps(dve, NCHUNK, point)
            ask(ph, "pool")
            ts(sc[1], sc[1], MIN_NORM, None, ALU.max)
            ts(sc[6], sc[1], CLIP, None, ALU.min)
            ask(ph, "act")
            artanh_ratio(sc[9], sc[6], sc[7], sc[8], sc[10], sc[4])
            tt(sc[9], sc[9], sc[6], ALU.mult)
            recip(sc[1], sc[1])
            tt(sc[9], sc[9], sc[1], ALU.mult)
            for s in range(2):
                dve.wait_ge(ph["store"][s], ph.upto("store", 16 * NCHUNK // 2))
            reset()

            def tables(it, s, c):
                wait(ph["store2"][s], ph.upto("store2", it * 32))
                r_, c_ = hyp_r[s], hyp_c[s]
                copy(r_[:, :, 0:D], nchunk(c))
                done(ph["x1"])
                copy(c_[:, :, 0:D], nchunk(c), False)
                for t in (r_, c_):
                    copy(t[:, :, 2 * D], scol(11, c), False)
                wait(ph["mm"], ph.upto("mm", (c + 1) * NTAB_G + NCHUNK * NTAB_G))
                pq = bank(2, 5)[0:P, 0:CN * 2 * D].rearrange("p (t w) -> p t w", w=2 * D)
                tt(c_[:, :, D:2 * D], pq[:, :, D:2 * D], cols(scol(9, c)), ALU.mult, False)
                tt(r_[:, :, D:2 * D], pq[:, :, 0:D], cols(scol(9, c)), ALU.mult)
                tt(r_[:, :, D:2 * D], r_[:, :, D:2 * D], rows_of(hyp_row["b1"], CN), ALU.add)
                done(ph["rows"])
                reset()
            steps(dve, NCHUNK, tables)

            ph = HE

            def ecol(k, c=None):
                return sc[k][:, 0:TE] if c is None else sc[k][:, bass.ds(c * CE, CE)]

            def edge_points(it, s, c):
                wait(ph["gathered"][s], ph.upto("gathered", it * (32 * CE) + 32 * CE))
                r_, c_ = h_row[s], h_col[s]
                xr, xc, tmp = r_[:, :, 0:D], c_[:, :, 0:D], hyp_stage[s]
                v, pre = edges_v[:, bass.ds(c * CE, CE), :], edges_pre[:, bass.ds(c * CE, CE), :]
                tt(tmp, xr, xc, ALU.mult)
                red(ecol(0, c), tmp)
                copy(ecol(1, c), r_[:, :, 2 * D], False)
                copy(ecol(2, c), c_[:, :, 2 * D], False)
                stt(small[0:P, 0, 0:CE], ecol(0, c), 2.0, c_[:, :, 2 * D], ALU.mult, ALU.subtract, False)
                ts(small[0:P, 1, 0:CE], r_[:, :, 2 * D], -1.0, 1.0, ALU.mult, ALU.add)
                ts(small[0:P, 0, 0:CE], small[0:P, 0, 0:CE], -1.0, None, ALU.add)
                tt(v, xr, cols(small[0:P, 0, 0:CE]), ALU.mult, False)
                tt(tmp, xc, cols(small[0:P, 1, 0:CE]), ALU.mult)
                tt(v, v, tmp, ALU.add)
                sum_squares(ecol(3, c), v, tmp)
                tt(pre, r_[:, :, D:2 * D], c_[:, :, D:2 * D], ALU.add, False)
                tt(tmp, cols(weight1[0:P, bass.ds(c * CE, CE)]), rows_of(hyp_row["wd"], CE), ALU.mult)
                tt(pre, pre, tmp, ALU.add)
                done(ph["rows"])
                reset()
            steps(dve, NCHUNK, edge_points)
            tt(ecol(4), ecol(1), ecol(2), ALU.mult)
            stt(ecol(4), ecol(0), -2.0, ecol(4), ALU.mult, ALU.add)
            ts(ecol(4), ecol(4), 1.0, MIN_NORM, ALU.add, ALU.max)
            recip(ecol(4), ecol(4))
            ask(ph, "pool")
            tt(ecol(5), ecol(5), ecol(4), ALU.mult)
            ts(ecol(5), ecol(5), MIN_NORM, None, ALU.max)
            ts(ecol(6), ecol(5), CLIP, None, ALU.min)
            ask(ph, "act")
            artanh_ratio(ecol(9), ecol(6), ecol(7), ecol(8), ecol(10), ecol(2))
            tt(ecol(9), ecol(9), ecol(6), ALU.mult)
            stt(ecol(10), ecol(9), 4.0, ecol(9), ALU.mult, ALU.mult)
            reset()

            def mlp(it, s, c):
                pre = edges_pre[:, bass.ds(c * CE, CE), :]
                tt(hyp_stage[s], cols(ecol(10, c)), rows_of(hyp_row["wg"], CE), ALU.mult)
                tt(pre, pre, hyp_stage[s], ALU.add)
                done(ph["pre"])
                wait(ph["gate"], ph.upto("gate", c + 1))
                tt(pre, pre, hyp_stage[s], ALU.mult)
                tt(pre, pre, rows_of(hyp_row["w2"], CE), ALU.mult)
                red(ecol(0, c), pre)
                reset()
            steps(dve, NCHUNK, mlp)
            ask(ph, "act")
            tt(ecol(2), ecol(2), weight1[0:P, :], ALU.mult)
            ts(ecol(1), ecol(1), -1.0, 1.0, ALU.mult, ALU.add)
            ts(ecol(1), ecol(1), MIN_NORM, None, ALU.max)
            tt(ecol(1), ecol(1), ecol(9), ALU.mult)
            recip(ecol(5), ecol(5))
            tt(ecol(1), ecol(1), ecol(5), ALU.mult)
            tt(ecol(1), ecol(1), ecol(4), ALU.mult)
            stt(ecol(8), ecol(1), 1.0 / 100.0, ecol(2), ALU.mult, ALU.mult)
            tt(edges_v, edges_v, cols(ecol(8)), ALU.mult)
            reset()
            segment_sums(ph, edges_v, 1)
            scatter_rows(ph, edges_v, 1, hyp_stage, None)

            ph = FIN

            def dots(it, s, c):
                wait(ph["load1"][s], ph.upto("load1", it * 32 + 32))
                sum_squares(scol(0, c), sp_b[s], sp_t)
                tt(sp_t, sp_a[s], sp_b[s], ALU.mult)
                red(scol(1, c), sp_t)
                done(ph["used1"])
                reset()
            steps(dve, NCHUNK, dots)
            ask(ph, "pool")
            ts(sc[2], sc[2], MIN_NORM, None, ALU.max)
            ts(sc[3], sc[11], -1.0, 1.0, ALU.mult, ALU.add)
            ts(sc[3], sc[3], MIN_NORM, None, ALU.max)
            recip(sc[3], sc[3])
            tt(sc[4], sc[2], sc[3], ALU.mult)
            ask(ph, "act")
            recip(sc[6], sc[2])
            tt(sc[6], sc[6], sc[5], ALU.mult)
            tt(sc[7], sc[6], sc[6], ALU.mult)
            tt(sc[7], sc[7], sc[0], ALU.mult)
            tt(sc[8], sc[6], sc[1], ALU.mult)
            ts(sc[8], sc[8], 2.0, 1.0, ALU.mult, ALU.add)
            tt(sc[9], sc[8], sc[7], ALU.add)
            tt(sc[10], sc[11], sc[7], ALU.mult)
            tt(sc[10], sc[10], sc[8], ALU.add)
            ts(sc[10], sc[10], MIN_NORM, None, ALU.max)
            recip(sc[10], sc[10])
            ts(sc[4], sc[11], -1.0, 1.0, ALU.mult, ALU.add)
            tt(sc[4], sc[4], sc[6], ALU.mult)
            tt(sc[4], sc[4], sc[10], ALU.mult)
            tt(sc[9], sc[9], sc[10], ALU.mult)
            reset()

            def combine(it, s, c):
                wait(ph["load2"][s], ph.upto("load2", it * 32 + 32))
                x = nchunk(c)
                tt(x, sp_a[s], cols(scol(9, c)), ALU.mult, False)
                tt(sp_t, sp_b[s], cols(scol(4, c)), ALU.mult)
                done(ph["used2"])
                tt(x, x, sp_t, ALU.add)
                sum_squares(scol(0, c), x, sp_t)
                reset()
            steps(dve, NCHUNK, combine)
            ask(ph, "pool")
            ts(sc[2], sc[2], MIN_NORM, None, ALU.max)
            ts(sc[6], sc[2], MAXNORM, None, ALU.min)
            ask(ph, "act")
            artanh_ratio(sc[9], sc[6], sc[7], sc[8], sc[10], sc[5])
            tt(sc[9], sc[9], sc[6], ALU.mult)
            recip(sc[2], sc[2])
            tt(sc[9], sc[9], sc[2], ALU.mult)
            reset()

            def tangent(it, s, c):
                x = nchunk(c)
                tt(x, x, cols(scol(9, c)), ALU.mult)
                center(x, small[0:P, 0, :], CN)
                sum_squares(scol(1, c), x, sp_t)
                reset()
            steps(dve, NCHUNK, tangent)
            ts(sc[1], sc[1], 1.0 / D, 1e-5, ALU.mult, ALU.add)
            ask(ph, "pool")
            reset()

            def normed(it, s, c):
                x = nchunk(c)
                tt(x, x, cols(scol(2, c)), ALU.mult)
                tt(x, x, rows_of(hyp_row["g"], CN), ALU.mult)
                tt(x, x, rows_of(hyp_row["b"], CN), ALU.add)
                sum_squares(scol(0, c), x, sp_t)
                ts(x, x, 0.0, None, ALU.max)
                sum_squares(scol(1, c), x, sp_t)
                reset()
            steps(dve, NCHUNK, normed)
            ask(ph, "pool")
            ask(ph, "pool")
            ts(sc[2], sc[2], MIN_NORM, None, ALU.max)
            ask(ph, "act")
            ts(sc[6], sc[4], MAXNORM, MIN_NORM, ALU.min, ALU.max)
            ask(ph, "act")
            artanh_ratio(sc[9], sc[6], sc[7], sc[8], sc[10], sc[5])
            recip(sc[2], sc[2])
            tt(sc[9], sc[9], sc[6], ALU.mult)
            tt(sc[9], sc[9], sc[2], ALU.mult)
            tt(sc[3], sc[3], sc[9], ALU.mult)
            ts(sc[3], sc[3], MIN_NORM, None, ALU.max)
            ask(ph, "act")
            ts(sc[4], sc[4], MAXNORM, None, ALU.min)
            recip(sc[3], sc[3])
            tt(sc[9], sc[9], sc[4], ALU.mult)
            tt(sc[9], sc[9], sc[3], ALU.mult)
            reset()

            def add_x0(it, s, c):
                wait(ph["load3"][s], ph.upto("load3", it * 16 + 16))
                x = nchunk(c)
                tt(x, x, cols(scol(9, c)), ALU.mult)
                tt(x, x, sp_a[s], ALU.add)
                done(ph["used3"])
                center(x, small[0:P, 0, :], CN)
                sum_squares(scol(1, c), x, sp_t)
                reset()
            steps(dve, NCHUNK, add_x0)
            ts(sc[1], sc[1], 1.0 / D, 1e-5, ALU.mult, ALU.add)
            ask(ph, "pool")
            reset()

            def output(it, s, c):
                wait(ph["store"][s], ph.upto("store", it * 16))
                tt(sp_b[s], nchunk(c), cols(scol(2, c)), ALU.mult)
                done(ph["rows"])
                reset()
            steps(dve, NCHUNK, output)


_INS = ["x", "src", "dst", "edge_weight", "edge_weight1",
        "L0_gnn_gat_W", "L0_gnn_gat_asrc", "L0_gnn_gat_adst", "L0_gnn_gat_bias", "L0_gnn_mlp_W1", "L0_gnn_mlp_b1",
        "L0_gnn_mlp_W2", "L0_gnn_mlp_b2", "L0_gnn_ln_g", "L0_gnn_ln_b", "L1_gnn_lin_W", "L1_gnn_bias", "L1_gnn_att_W1",
        "L1_gnn_att_b1", "L1_gnn_att_W2", "L1_gnn_att_b2", "L1_gnn_ln_g", "L1_gnn_ln_b"]


def kernel(**inputs):
    import numpy as np
    import concourse.bacc as bacc
    from concourse.bass_utils import run_bass_kernel_spmd

    nc = bacc.Bacc("TRN2", target_bir_lowering=False, num_devices=1)
    arrays, aps = {}, {}
    for name in _INS:
        arr = np.ascontiguousarray(inputs[name])
        arrays["in_" + name] = arr
        aps[name] = nc.dram_tensor("in_" + name, arr.shape, mybir.dt.from_np(arr.dtype), kind="ExternalInput").ap()
    out = nc.dram_tensor("out", (N, D), mybir.dt.float32, kind="ExternalOutput").ap()
    build(nc, aps, out)
    return run_bass_kernel_spmd(nc, [arrays], core_ids=[0]).results[0]["out"]
```

```python
import concourse.bass as bass
from concourse import mybir
from concourse.alu_op_type import AluOpType as ALU
from contextlib import ExitStack

N, E, D = 50000, 25000, 64
P = 125
TN, TE = N // P, E // P
L, R, H = 2, 4, 2
NCHUNK = 20
CE, CN = TE // NCHUNK, TN // NCHUNK
NTAB = TN // CE
ROW = D + 16
HROW = 2 * D + 1
RADIX = 256
BIG = 1e30
MAXNORM = 1.0 - 0.004
MIN_NORM = 1e-15
CLIP = 1.0 - 1e-7
GRP = 4
NGRP = TE // GRP
GROUPS = CN // GRP
REC = 5
SKIP = 1000000


def build(nc, a, out):
    fp32, i32 = mybir.dt.float32, mybir.dt.int32
    ACT = mybir.ActivationFunctionType
    X = mybir.AxisListType.X
    ctx = ExitStack()
    with ctx:
        def sb(name, shape, dt=fp32):
            return ctx.enter_context(nc.sbuf_tensor(name, shape, dt))

        def sem(name):
            return ctx.enter_context(nc.semaphore(name))

        def dram(name, shape):
            return nc.dram_tensor(name, shape, fp32, kind="Internal").ap()

        rec_dram = dram("rec_dram", (E, REC))
        gat_table = [dram(f"gat_table{l}", (N, ROW)) for l in range(L)]
        h2_dram = dram("h2_dram", (N, D))
        pair_dram = dram("pair_dram", (E, ROW))
        corr_dram = [dram(f"corr_dram{d}", (N, D)) for d in range(2)]
        agg_dram = dram("agg_dram", (N, D))
        x0_dram = dram("x0_dram", (N, D))
        row_table = dram("row_table", (N, HROW))
        col_table = dram("col_table", (N, HROW))

        def by_part(t):
            return t.rearrange("(p t) w -> p (t w)", p=P)

        def chunk(t, c, width, cols):
            return by_part(t)[:, bass.ds(c * (cols * width), cols * width)]


        arena = sb("arena", [128, 2 * TE * ROW])

        def area(at, cols, width):
            return arena[0:P, at:at + cols * width].rearrange("p (t w) -> p t w", w=width)

        G = [area(d * TE * ROW, TE, ROW) for d in range(2)]
        nodes = area(0, TN, D)
        edges_v = area(0, TE, D)
        SPARE = TN * D
        pool_a = sb("pool_a", [128, 2 * CE * HROW])
        pool_b = sb("pool_b", [128, 2 * CE * HROW])

        def slot_of(pool, s, cols, width):
            return pool[0:P, s * CE * HROW:s * CE * HROW + cols * width].rearrange("p (t w) -> p t w", w=width)

        scratch = sb("scratch", [128, 12 * TN])
        att = [scratch[0:P, k * 4 * TE:(k + 1) * 4 * TE].rearrange("p (s t) -> p s t", s=4) for k in range(6)]
        sc = [scratch[0:P, k * TN:(k + 1) * TN] for k in range(12)]
        ident = sb("ident", [128, 128])
        ones = sb("ones", [128, 128])
        tri_lt = sb("tri_lt", [128, 128])
        tri_gt = sb("tri_gt", [128, 128])
        position_i = sb("position_i", [128, TE], i32)
        rec = scratch[:, 0:TE * REC]
        rec_v = rec[0:P, :].rearrange("p (t c) -> p t c", c=REC)
        hist, total, cursor, matched, digits_row, digits_i = (scratch[:, TE * REC + k * RADIX:TE * REC + (k + 1) * RADIX] for k in range(6))
        digits_i = digits_i.bitcast(i32)
        digit, digit_i = (scratch[:, TE * REC + 6 * RADIX + k * TE:TE * REC + 6 * RADIX + (k + 1) * TE] for k in range(2))
        digit_i = digit_i.bitcast(i32)
        rank = sb("rank", [128, CE])
        rec_stage = sb("rec_stage", [128, 2, CE * REC])
        place_i = sb("place_i", [128, 2, CE], i32)
        idx_a = sb("idx_a", [128, 2, CE], i32)
        idx_b = sb("idx_b", [128, 2, CE], i32)
        src_i = [sb(f"src_i{o}", [128, TE], i32) for o in range(2)]
        dst_i = [sb(f"dst_i{o}", [128, TE], i32) for o in range(2)]
        out_i = [sb(f"out_i{o}", [128, TE], i32) for o in range(2)]
        pair_i = sb("pair_i", [128, TE], i32)
        keep = [sb(f"keep{o}", [128, TE]) for o in range(2)]
        keep_b = [sb(f"keep_b{o}", [128, TE]) for o in range(2)]
        first = [sb(f"first{o}", [128, TE]) for o in range(2)]
        last = [sb(f"last{o}", [128, TE]) for o in range(2)]
        off = [sb(f"off{o}", [128, 2, TE]) for o in range(2)]
        carry_f = [sb(f"carry_f{o}", [128, 128]) for o in range(2)]
        carry_b = [sb(f"carry_b{o}", [128, 128]) for o in range(2)]
        far_f = [sb(f"far_f{o}", [128, 128]) for o in range(2)]
        far_b = [sb(f"far_b{o}", [128, 128]) for o in range(2)]
        weight1 = sb("weight1", [128, TE])
        prod = sb("prod", [128, GRP * 4 * D])
        diag = prod[:, 0:4 * P].rearrange("p (s q) -> p s q", s=4)
        far = prod[:, 4 * P:8 * P].rearrange("p (s q) -> p s q", s=4)
        key_diag = prod[:, 0:256].rearrange("p (k q) -> p k q", k=2)
        goes_on = sb("goes_on", [128, 1])
        seg_off = scratch[:, 5 * 4 * TE:6 * 4 * TE].rearrange("p (k t) -> p k t", k=4)
        carry4 = sb("carry4", [128, 4, 4])
        carry_v = sb("carry_v", [128, D])
        tr = sb("tr", [D + 1, 2, GRP * P])
        grp_stage = sb("grp_stage", [128, 2, GRP * D])
        proj_w = [sb(f"proj_w{l}", [D + 1, 16]) for l in range(L)]
        edge_w = [sb(f"edge_w{l}", [64, 2, 4 * D]) for l in range(L)]
        dense_w = [sb(f"dense_w{l}", [D + 1, D]) for l in range(L)]
        mlp_w2 = [sb(f"mlp_w2{l}", [D + 1, D]) for l in range(L)]
        g_row = [sb(f"g_row{l}", [128, D]) for l in range(L)]
        be_row = [sb(f"be_row{l}", [128, D]) for l in range(L)]
        lin_t = sb("lin_t", [64, D])
        att_t = sb("att_t", [64, 2 * D])
        hyp_bias = sb("hyp_bias", [128, D])
        hyp_row = {k: sb(f"hyp_{k}", [128, D]) for k in ("b1", "w2", "g", "b", "wd", "wg")}
        att_b2 = sb("att_b2", [128, 1])
        power = sb("power", [128, 2])
        bias_sc = sb("bias_sc", [128, 16])
        part = sb("part", [128, CN * 8])
        small = sb("small", [128, 6, 2 * CE])
        raw_at = [16000]

        def raw(parts, n):
            raw_at[0] += n
            return arena[0:parts, raw_at[0] - n:raw_at[0]]

        w_raw = [raw(64, R * H * D) for l in range(L)]
        a_raw = [raw(64, 2 * R * H * D) for l in range(L)]
        w_prod = raw(64, R * H * D)
        w_red = raw(64, 2 * R * H)
        w1_edge = [raw(128, R * D) for l in range(L)]
        w1_top = [raw(64, D) for l in range(L)]
        w_t = [raw(128, R * D) for l in range(L)]
        gat_b = [raw(128, R) for l in range(L)]
        lin_raw = raw(64, D)
        att_raw = raw(64, 2 * D + 2)
        zeros = raw(128, CN * D)
        ps = ctx.enter_context(nc.psum_tensor("ps", [128, 8 * 512], fp32))

        def bank(b, n=1):
            return ps[:, b * 512:(b + n) * 512]

        spacer = {k: sem(f"s_spacer_{k}") for k in ("sp", "act", "pool", "pe", "dve")}

        def hold(eng, who, s, value):
            if isinstance(value, int):
                if value > 0:
                    eng.wait_ge(s, value)
            else:
                eng.wait_ge(s, value)
                eng.sem_inc(spacer[who], 1)

        def steps(eng, n, body, at=0):
            if at == 0:
                for s in range(2):
                    body(0, s, s)
                at = 2
            with eng.Fori(at // 2, n // 2) as it:
                for s in range(2):
                    body(it, s, it * 2 + s)

        def pipelined(eng, n, depth, body, head=0):
            head = head or depth + depth % 2

            def peel(c):
                body(c // 2, c % 2, c, lambda k: 0 <= c - k < n)
            for c in range(head):
                peel(c)
            with eng.Fori(head // 2, n // 2) as it:
                for s in range(2):
                    body(it, s, it * 2 + s, lambda k: True)
            for c in range(n, n + depth):
                peel(c)

        def groups_by(c, s, lags, upto=-1):
            if isinstance(c, int):
                v = sum(GROUPS * min(max(c - k, 0), NCHUNK) for k in lags)
                v += sum(GROUPS for k in lags if k <= upto and 0 <= c - k < NCHUNK)
                return v, v % 2
            more = sum(1 for k in lags if k <= upto) - sum(lags)
            return c * (GROUPS * len(lags)) + GROUPS * more, (GROUPS * (len(lags) * s + more)) % 2

        class Signals(dict):
            run, per_run = 0, {}

            def upto(self, key, value):
                return self.run * self.per_run[key] + value if self.run else value

        def sems(name, names, slotted=()):
            made = Signals({k: sem(f"s_{name}_{k}") for k in names})
            made.update({k: [sem(f"s_{name}_{k}{s}") for s in range(2)] for k in slotted})
            return made

        def runs(made, n, per_run):
            out_ = []
            for k in range(n):
                ph = Signals(made)
                ph.run, ph.per_run = k, per_run
                out_.append(ph)
            return out_

        s_w = sem("s_weights_loaded")
        s_in = sem("s_edges_loaded")
        s_const = sem("s_constants")
        s_zeroed = sem("s_tables_zeroed")
        WP = sems("wprep", ("dve", "t", "tc", "mm", "act", "row"))
        TAB = sems("tab", ("tr", "trc", "mm", "rows"), ("load", "store"))
        SORT = runs(sems("sort", ("rec", "hist", "base", "staged"), ("scattered",)), 4,
                    dict(rec=16, hist=1, base=1, staged=NCHUNK, scattered=16 * TE // 2))
        ORD = runs(sems("order", ("diag", "bc", "done")), 2, dict(diag=1, bc=1, done=1))
        EDGE = runs(sems("edge", ("idx", "rows", "pair"), ("gathered", "permuted", "copied")), L,
                    dict(idx=3 * NCHUNK, rows=NCHUNK, pair=16 * NCHUNK, copied=16 * NCHUNK // 2, gathered=16 * TE, permuted=16 * TE // 2))
        att_runs = runs(sems("att", ("diag", "bc", "dve", "exp", "sums", "copied", "tr", "trc", "mm", "prod", "scan", "cv", "cvc", "carried", "places"),
                             ("staged", "scattered")), 2 * L,
                        dict(diag=3, bc=2, dve=1, exp=2, sums=1, copied=NGRP, tr=NGRP, trc=NGRP, mm=NGRP, prod=NGRP, scan=1, cv=1, cvc=1,
                             carried=1, places=NCHUNK, staged=16 * NCHUNK // 2, scattered=16 * TE // 2))
        ATT = [att_runs[2 * l:2 * l + 2] for l in range(L)]
        NODE = runs(sems("node", ("tr", "trc", "mm", "u", "th", "z", "zc", "sq", "var", "rstd", "h", "rows"), ("corr", "hin", "store")), L,
                    dict(tr=3 * GROUPS * NCHUNK, trc=3 * GROUPS * NCHUNK, mm=3 * GROUPS * NCHUNK, u=NCHUNK, th=NCHUNK, z=NCHUNK,
                         zc=NCHUNK, sq=NCHUNK, var=NCHUNK, rstd=NCHUNK, h=NCHUNK, rows=NCHUNK,
                         corr=16 * NCHUNK, hin=16 * NCHUNK // 2, store=16 * NCHUNK // 2))
        HYP = sems("hyp", ("act_asked", "act", "used", "r0", "sq", "x0", "y", "point", "psq", "copied", "pq", "tr", "trc", "mm", "x1", "rows"), ("load", "store", "store2"))
        HE = sems("hedge", ("idx", "rows", "v", "sq", "act_asked", "act", "pre", "gate", "scan", "cv", "cvc", "carried", "places"), ("gathered", "staged", "scattered"))
        FIN = sems("fin", ("act_asked", "act", "used1", "used2", "used3", "x", "sq", "sq0", "relu", "rows"), ("load1", "load2", "load3", "store"))
        s_link = sem("s_dve_link")
        block = ctx.enter_context(nc.Block())


        NCONST = 10
        SCORE_TILES = ((0, 16, 4 * 512 + 256), (16, CN, 7 * 512 + 256))
        NODE_LAGS = [(0, 1, 3), (0, 1)]
        V, A, T, GP = nc.vector, nc.scalar, nc.tensor, nc.gpsimd

        def cols(v, width=D):
            return v.unsqueeze(2).broadcast_to([P, v.shape[1], width])

        def rows_of(r, n):
            return r[0:P, :].unsqueeze(1).broadcast_to([P, n, D])

        def flat(v):
            return v.rearrange("p t w -> p (t w)")

        def chunk3(t, c, width, ncols):
            return chunk(t, c, width, ncols).rearrange("p (t w) -> p t w", w=width)

        def nchunk(c):
            return nodes[:, bass.ds(c * CN, CN), :]

        tab_rows = [area(s * CN * ROW, CN, ROW) for s in range(2)]
        n_h = [area((2 + s) * CN * ROW, CN, ROW) for s in range(2)]
        n_f, n_r, n_u, n_z, n_q = ([area(4 * CN * ROW + (2 * k + s) * CN * D, CN, D) for s in range(2)] for k in range(5))
        sp_a = [area(SPARE + s * CN * D, CN, D) for s in range(2)]
        sp_b = [area(SPARE + (2 + s) * CN * D, CN, D) for s in range(2)]
        sp_t = area(SPARE + 4 * CN * D, CN, D)
        squares = [slot_of(pool_a, s, CN, D) for s in range(2)]
        products = [slot_of(pool_b, s, CN, D) for s in range(2)]
        hyp_r = [pool_a[0:P, 0:CN * HROW].rearrange("p (t w) -> p t w", w=HROW), area(SPARE, CN, HROW)]
        hyp_c = [pool_b[0:P, 0:CN * HROW].rearrange("p (t w) -> p t w", w=HROW), area(SPARE + CN * HROW, CN, HROW)]
        edges_pre = area(TE * D, TE, D)
        g_src = [slot_of(pool_a, s, CE, ROW) for s in range(2)]
        g_dst = [slot_of(pool_b, s, CE, ROW) for s in range(2)]
        h_row = [slot_of(pool_a, s, CE, HROW) for s in range(2)]
        h_col = [slot_of(pool_b, s, CE, HROW) for s in range(2)]
        gat_stage = [slot_of(pool_b, s, CE, ROW) for s in range(2)]
        e_sq, e_tmp = ([area(SPARE + (2 + 2 * k + s) * CE * D, CE, D) for s in range(2)] for k in range(2))
        hyp_stage = [area(SPARE + s * CE * D, CE, D) for s in range(2)]
        perm = g_src
        trv = [tr[:, s, :] for s in range(2)]

        weight_loads = []

        def bc(v, n=128):
            return v.rearrange("(a n) -> a n", a=1).broadcast_to([n, v.shape[0]])

        for l in range(L):
            weight_loads.append((w_raw[l].rearrange("i (r c) -> i r c", r=R), a["L0_gnn_gat_W"][l].rearrange("r i c -> i r c")))
            for k, name in enumerate(("L0_gnn_gat_asrc", "L0_gnn_gat_adst")):
                weight_loads.append((a_raw[l][:, k * R * H * D:(k + 1) * R * H * D], bc(a[name][l].rearrange("r h c -> (r h c)"), 64)))
            weight_loads += [
                (w1_edge[l].rearrange("p (r n) -> p r n", r=R), a["L0_gnn_mlp_W1"][l, D:, :].rearrange("(r p) n -> p r n", r=R)),
                (w1_top[l], a["L0_gnn_mlp_W1"][l, 0:D, :]),
                *((gat_b[l][:, r:r + 1], a["L0_gnn_gat_bias"][l, r].rearrange("(p a) -> p a", a=1)) for r in range(R)),
                (mlp_w2[l][0:D, :], a["L0_gnn_mlp_W2"][l]),
                (dense_w[l][D:D + 1, :], bc(a["L0_gnn_mlp_b1"][l], 1)),
                (mlp_w2[l][D:D + 1, :], bc(a["L0_gnn_mlp_b2"][l], 1)),
                (g_row[l][:, :], bc(a["L0_gnn_ln_g"][l])),
                (be_row[l][:, :], bc(a["L0_gnn_ln_b"][l]))]
        weight_loads += [
            (lin_raw, a["L1_gnn_lin_W"]), (att_raw, a["L1_gnn_att_W1"]),
            (hyp_bias[:, :], a["L1_gnn_bias"].broadcast_to([128, D])),
            (hyp_row["b1"][:, :], bc(a["L1_gnn_att_b1"])),
            (hyp_row["w2"][:, :], a["L1_gnn_att_W2"].broadcast_to([128, D])),
            (hyp_row["g"][:, :], bc(a["L1_gnn_ln_g"])), (hyp_row["b"][:, :], bc(a["L1_gnn_ln_b"])),
            (att_b2[:, :], bc(a["L1_gnn_att_b2"]))]
        NW = 16 * len(weight_loads)

        def sp_load_inputs(sp):
            for dst, name in ((dst_i[1][0:P, :], "dst"), (src_i[1][0:P, :], "src"), (off[0][0:P, 0, :], "edge_weight")):
                sp.dma_start(dst, a[name].rearrange("(p t) -> p t", p=P)).then_inc(s_in, 16)
            sp.dma_start(off[0][0:P, 1, :], a["edge_weight1"].rearrange("(p t) a -> p (t a)", p=P)).then_inc(s_in, 16)
            for dst, src in weight_loads:
                sp.dma_start(dst, src).then_inc(s_w, 16)
            sp.wait_ge(s_const, NCONST)
            for t in (corr_dram[0], corr_dram[1], agg_dram):
                with sp.Fori(0, NCHUNK) as c:
                    sp.dma_start(chunk(t, c, D, CN), zeros[0:P, :]).then_inc(s_zeroed, 16)

        def sp_table0(sp, at, n):
            def load(s, c):
                sp.dma_start(tab_rows[s][:, :, 0:D], chunk3(a["x"], c, D, CN)).then_inc(TAB["load"][s], 16)

            def store(s, c):
                hold(sp, "sp", TAB["rows"], c + 1)
                sp.dma_start(chunk(gat_table[0], c, ROW, CN), flat(tab_rows[s])).then_inc(TAB["store"][s], 16)

            if at == 0:
                for s in range(2):
                    load(s, s)
            with sp.Fori(at // 2, min(n, NCHUNK - 2) // 2) as it:
                for s in range(2):
                    store(s, it * 2 + s)
                    hold(sp, "sp", TAB["store"][s], it * 16 + 16)
                    load(s, it * 2 + s + 2)
            if n == NCHUNK:
                for s in range(2):
                    store(s, NCHUNK - 2 + s)

        def sp_sort(sp, k):
            for s in range(2):
                sp.wait_ge(SORT[k]["scattered"][s], SORT[k].upto("scattered", 16 * TE // 2))
            sp.dma_start(rec[0:P, :], by_part(rec_dram)).then_inc(SORT[k]["rec"], 16)

        def sp_pairs(sp, l):
            with sp.Fori(0, NCHUNK) as c:
                hold(sp, "sp", EDGE[l]["rows"], EDGE[l].upto("rows", c + 1))
                sp.dma_start(chunk(pair_dram, c, ROW, CE), flat(G[0][:, bass.ds(c * CE, CE), :])).then_inc(EDGE[l]["pair"], 16)

        def sp_permuted(sp, l):
            ph = EDGE[l]

            def body(it, s, c):
                hold(sp, "sp", ph["permuted"][s], ph.upto("permuted", (it + 1) * (16 * CE)))
                sp.dma_start(flat(G[1][:, bass.ds(c * CE, CE), :]), flat(perm[s])).then_inc(ph["copied"][s], 16)
            steps(sp, NCHUNK, body)

        def sp_stage(sp, ph, v, stage):
            sp.wait_ge(ph["carried"], ph.upto("carried", 1))

            def body(it, s, c):
                hold(sp, "sp", ph["scattered"][s], ph.upto("scattered", it * (16 * CE)))
                sp.dma_start(flat(stage[s]), flat(v[:, bass.ds(c * CE, CE), :])).then_inc(ph["staged"][s], 16)
            steps(sp, NCHUNK, body)

        def sp_node(sp, l):
            ph, table = NODE[l], gat_table[l]
            for d in range(2):
                for s in range(2):
                    sp.wait_ge(ATT[l][d]["scattered"][s], ATT[l][d].upto("scattered", 16 * TE // 2))

            def body(it, s, c, on):
                if on(0):
                    hold(sp, "sp", ph["u"], ph.upto("u", c - 1))
                    for d, to in enumerate((n_f, n_r)):
                        sp.dma_start(flat(to[s]), chunk(corr_dram[d], c, D, CN)).then_inc(ph["corr"][s], 16)
                    hold(sp, "sp", ph["z"], ph.upto("z", c - 1))
                    sp.dma_start(flat(n_h[s]), chunk(table, c, ROW, CN)).then_inc(ph["hin"][s], 16)
                if on(4):
                    hold(sp, "sp", ph["rows"], ph.upto("rows", c - 3))
                    if l + 1 < L:
                        sp.dma_start(chunk(gat_table[l + 1], c - 4, ROW, CN), flat(tab_rows[s])).then_inc(ph["store"][s], 16)
                    else:
                        sp.dma_start(chunk3(h2_dram, c - 4, D, CN), tab_rows[s][:, :, 0:D]).then_inc(ph["store"][s], 16)
            pipelined(sp, NCHUNK, 4, body)
            for s in range(2):
                sp.wait_ge(ph["store"][s], ph.upto("store", 16 * NCHUNK // 2))

        def sp_hyp(sp):
            ph = HYP

            def load(s, c):
                sp.dma_start(flat(sp_a[s]), chunk(h2_dram, c, D, CN)).then_inc(ph["load"][s], 16)
                sp.dma_start(flat(sp_b[s]), chunk(a["x"], c, D, CN)).then_inc(ph["load"][s], 16)

            for s in range(2):
                load(s, s)
            with sp.Fori(0, NCHUNK // 2 - 1) as it:
                for s in range(2):
                    hold(sp, "sp", ph["used"], ph.upto("used", it * 2 + s + 1))
                    load(s, it * 2 + s + 2)
            with sp.Fori(0, NCHUNK // 2) as it:
                for s in range(2):
                    hold(sp, "sp", ph["x0"], ph.upto("x0", it * 2 + s + 1))
                    sp.dma_start(chunk(x0_dram, it * 2 + s, D, CN), flat(sp_a[s])).then_inc(ph["store"][s], 16)
            with sp.Fori(0, NCHUNK // 2) as it:
                for s in range(2):
                    hold(sp, "sp", ph["rows"], ph.upto("rows", it * 2 + s + 1))
                    sp.dma_start(chunk(row_table, it * 2 + s, HROW, CN), flat(hyp_r[s])).then_inc(ph["store2"][s], 16)
                    sp.dma_start(chunk(col_table, it * 2 + s, HROW, CN), flat(hyp_c[s])).then_inc(ph["store2"][s], 16)

        def sp_final(sp):
            ph = FIN

            def pass_in(key, used, srcs):
                def load(s, c):
                    for to, t, w in srcs:
                        sp.dma_start(to[s], chunk3(t, c, w, CN)[:, :, 0:D]).then_inc(ph[key][s], 16)
                for s in range(2):
                    load(s, s)
                with sp.Fori(0, NCHUNK // 2 - 1) as it:
                    for s in range(2):
                        hold(sp, "sp", ph[used], it * 2 + s + 1)
                        load(s, it * 2 + s + 2)

            for s in range(2):
                sp.wait_ge(HE["scattered"][s], 16 * TE // 2)
            pu = ((sp_a, row_table, HROW), (sp_b, agg_dram, D))
            pass_in("load1", "used1", pu)
            sp.wait_ge(ph["used1"], ph.upto("used1", NCHUNK))
            pass_in("load2", "used2", pu)
            sp.wait_ge(ph["used2"], ph.upto("used2", NCHUNK))
            pass_in("load3", "used3", ((sp_a, x0_dram, D),))
            with sp.Fori(0, NCHUNK // 2) as it:
                for s in range(2):
                    hold(sp, "sp", ph["rows"], ph.upto("rows", it * 2 + s + 1))
                    sp.dma_start(chunk(out, it * 2 + s, D, CN), flat(sp_b[s])).then_inc(ph["store"][s], 16)
            for s in range(2):
                sp.wait_ge(ph["store"][s], ph.upto("store", 16 * NCHUNK // 2))

        @block.sync
        def _(sp):
            sp_load_inputs(sp)
            sp_table0(sp, 0, 12)
            sp_sort(sp, 0)
            sp_table0(sp, 12, NCHUNK)
            for k in range(1, 4):
                sp_sort(sp, k)
            for l in range(L):
                sp_pairs(sp, l)
                sp_permuted(sp, l)
                for d in range(2):
                    sp_stage(sp, ATT[l][d], G[d], gat_stage)
                sp_node(sp, l)
            sp_hyp(sp)
            sp_stage(sp, HE, edges_v, hyp_stage)
            sp_final(sp)

        def pool_constants(gp):
            GP.memset(ones[:, :], 1.0).then_inc(s_const, 1)
            GP.memset(ident[:, :], 0.0).then_inc(s_const, 1)
            GP.memset(zeros[:, :], 0.0).then_inc(s_const, 1)
            GP.memset(power[:, 0:1], 0.5).then_inc(s_const, 1)
            GP.memset(power[:, 1:2], -0.5).then_inc(s_const, 1)
            gp.wait_ge(s_const, 5)
            GP.affine_select(out=ident[:, :], in_=ident[:, :], compare_op=ALU.not_equal, fill=1.0, base=0,
                             pattern=[[-1, 128]], channel_multiplier=1).then_inc(s_const, 1)
            GP.affine_select(out=tri_lt[:, :], in_=ones[:, :], compare_op=ALU.is_gt, fill=0.0, base=0,
                             pattern=[[1, 128]], channel_multiplier=-1).then_inc(s_const, 1)
            GP.affine_select(out=tri_gt[:, :], in_=ones[:, :], compare_op=ALU.is_gt, fill=0.0, base=0,
                             pattern=[[-1, 128]], channel_multiplier=1).then_inc(s_const, 1)
            GP.iota(digits_i[:, :], pattern=[[1, RADIX]], base=0, channel_multiplier=0).then_inc(s_const, 1)
            GP.iota(position_i[:, :], pattern=[[1, TE]], base=0, channel_multiplier=TE).then_inc(s_const, 1)

        def pool_sort(gp, k, limit):
            if k:
                gp.wait_ge(SORT[k - 1]["rec"], SORT[k - 1].upto("rec", 16))

            def body(it, s, c):
                hold(gp, "pool", SORT[k]["staged"], SORT[k].upto("staged", c + 1))
                for j in range(CE):
                    gp.indirect_dma_start(rec_dram, bass.IndirectOffsetOnAxis(ap=place_i[0:P, s, j:j + 1], axis=0),
                                          rec_stage[0:P, s, j * REC:(j + 1) * REC], None,
                                          bounds_check=limit, oob_is_err=False).then_inc(SORT[k]["scattered"][s], 16)
            steps(gp, NCHUNK, body)

        def pool_gather(gp, dst, table, idx, limit, signal):
            gp.indirect_dma_start(dst, None, table, bass.IndirectOffsetOnAxis(ap=idx, axis=0),
                                  bounds_check=limit, oob_is_err=False).then_inc(signal, 16)

        def pool_edges(gp, l, limit, limit_e):
            ph = EDGE[l]
            before = TAB if l == 0 else NODE[l - 1]
            gp.wait_ge(ORD[0]["done"], 1)
            for s in range(2):
                gp.wait_ge(before["store"][s], before.upto("store", 16 * NCHUNK // 2))

            pool_ends(gp, ph, 0, (g_src, gat_table[l]), (g_dst, gat_table[l]), limit)
            gp.wait_ge(ORD[1]["done"], 2)
            gp.wait_ge(ph["pair"], ph.upto("pair", 16 * NCHUNK))

            def pairs(it, s, c):
                hold(gp, "pool", ph["copied"][s], ph.upto("copied", it * 16))
                GP.tensor_copy(idx_a[0:P, s, :], pair_i[0:P, bass.ds(c * CE, CE)]).then_inc(ph["idx"], 1)
                hold(gp, "pool", ph["idx"], ph.upto("idx", 2 * NCHUNK + c + 1))
                for j in range(CE):
                    pool_gather(gp, perm[s][:, j, :], pair_dram, idx_a[0:P, s, j:j + 1], limit_e, ph["permuted"][s])
            steps(gp, NCHUNK, pairs)

        def pool_ends(gp, ph, order, row_end, col_end, limit):
            def ends(it, s, c):
                hold(gp, "pool", ph["rows"], ph.upto("rows", c - 1))
                GP.tensor_copy(idx_a[0:P, s, :], src_i[order][0:P, bass.ds(c * CE, CE)]).then_inc(ph["idx"], 1)
                GP.tensor_copy(idx_b[0:P, s, :], dst_i[order][0:P, bass.ds(c * CE, CE)]).then_inc(ph["idx"], 1)
                hold(gp, "pool", ph["idx"], ph.upto("idx", c * 2 + 2))
                for j in range(CE):
                    pool_gather(gp, row_end[0][s][:, j, :], row_end[1], idx_a[0:P, s, j:j + 1], limit, ph["gathered"][s])
                    pool_gather(gp, col_end[0][s][:, j, :], col_end[1], idx_b[0:P, s, j:j + 1], limit, ph["gathered"][s])
            steps(gp, NCHUNK, ends)

        def pool_scatter(gp, ph, table, o, stage, limit):
            def body(it, s, c):
                hold(gp, "pool", ph["scattered"][s], ph.upto("scattered", it * (16 * CE)))
                GP.tensor_copy(idx_b[0:P, s, :], out_i[o][0:P, bass.ds(c * CE, CE)]).then_inc(ph["places"], 1)
                hold(gp, "pool", ph["places"], ph.upto("places", c + 1))
                hold(gp, "pool", ph["staged"][s], ph.upto("staged", it * 16 + 16))
                for j in range(CE):
                    gp.indirect_dma_start(table, bass.IndirectOffsetOnAxis(ap=idx_b[0:P, s, j:j + 1], axis=0),
                                          stage[s][:, j, 0:D], None, bounds_check=limit, oob_is_err=False).then_inc(ph["scattered"][s], 16)
            steps(gp, NCHUNK, body)

        def pool_node(gp, l):
            ph = NODE[l]

            def body(it, s, c):
                hold(gp, "pool", ph["var"], ph.upto("var", c + 1))
                GP.tensor_tensor(small[0:P, 4 + s, :], small[0:P, 2 + s, :], power[0:P, 1:2].broadcast_to([P, CN]), ALU.pow).then_inc(ph["rstd"], 1)
            steps(gp, NCHUNK, body)

        @block.gpsimd
        def _(gp):
            pool_constants(gp)
            limit, limit_e = gp.to_reg(N - 1), gp.to_reg(E - 1)
            for k in range(4):
                pool_sort(gp, k, limit_e)
            gp.wait_ge(s_zeroed, 16 * 3 * NCHUNK)
            for l in range(L):
                pool_edges(gp, l, limit, limit_e)
                for d in range(2):
                    pool_scatter(gp, ATT[l][d], corr_dram[d], d, gat_stage, limit)
                pool_node(gp, l)
            for s in range(2):
                gp.wait_ge(HYP["store2"][s], 32 * NCHUNK // 2)

            pool_ends(gp, HE, 1, (h_row, row_table), (h_col, col_table), limit)
            pool_scatter(gp, HE, agg_dram, 1, hyp_stage, limit)

        def act_copy(dst, src):
            return A.activation(dst, src, ACT.Copy)

        def act_weights(act):
            for l in range(L):
                act.wait_ge(WP["t"], l + 1)
                act_copy(w_t[l], bank(0)[:, 0:R * D]).then_inc(WP["tc"], 1)
                act.wait_ge(WP["mm"], l + 1)
                for d in range(2):
                    for h in range(H):
                        act_copy(edge_w[l][:, d, :].rearrange("i (g h n) -> i g h n", g=2, h=H)[:, :, h, :],
                                 bank((1, 4)[h])[0:64, 0:R * D].rearrange("i (g d n) -> i g d n", g=2, d=2)[:, :, d, :])
                act_copy(dense_w[l][0:D, :], bank(2)[0:64, 0:D]).then_inc(WP["act"], 1)
            act.wait_ge(WP["mm"], L + 1)
            act_copy(lin_t[:, :], bank(0)[0:64, 0:D])
            act_copy(att_t[:, :], bank(0)[0:64, D:3 * D])
            act_copy(hyp_row["wd"][:, :], bank(0)[:, 3 * D:4 * D])
            act_copy(hyp_row["wg"][:, :], bank(0)[:, 4 * D:5 * D]).then_inc(WP["act"], 1)

        def act_groups(act, ph, base, parity, n):
            for j in range(n):
                b = (parity + j) % 2
                hold(act, "act", ph["mm"], ph.upto("mm", base + j - 1))
                hold(act, "act", ph["tr"], ph.upto("tr", base + j + 1))
                act_copy(trv[b][0:D, :], bank(b)[0:64, 0:GRP * P]).then_inc(ph["trc"], 1)

        def act_table0(act):
            def body(it, s, c):
                act_groups(act, TAB, c * GROUPS, s * GROUPS, GROUPS)
                hold(act, "act", TAB["mm"], (c + 1) * GROUPS)
                act_copy(tab_rows[s][:, :, D:ROW], bank(5)[0:P, 0:CN * 16].rearrange("p (t w) -> p t w", w=16)).then_inc(TAB["rows"], 1)
            steps(act, NCHUNK, body)

        def act_attention(act, l, d):
            ph = ATT[l][d]
            Es, Sf, F, B, mx, pp = att
            act.wait_ge(ph["dve"], ph.upto("dve", 1))
            A.activation(pp, F, ACT.Exp)
            A.activation(Sf, B, ACT.Exp).then_inc(ph["exp"], 1)
            act.wait_ge(ph["sums"], ph.upto("sums", 1))
            act_copy(carry4[0:P, 2:4, :], bank(7)[0:P, 0:8].rearrange("p (k s) -> p k s", k=2)).then_inc(ph["exp"], 1)

            def group(it, s, g, on):
                if on(0):
                    hold(act, "act", ph["tr"], ph.upto("tr", g - 1))
                    act_copy(grp_stage[0:P, s, :].rearrange("p (t w) -> p t w", w=D), G[d][:, bass.ds(g * GRP, GRP), 0:D]).then_inc(ph["copied"], 1)
                if on(1):
                    hold(act, "act", ph["mm"], ph.upto("mm", g - 2))
                    hold(act, "act", ph["tr"], ph.upto("tr", g))
                    act_copy(trv[1 - s][0:D, :], bank(1 - s)[0:64, 0:GRP * P]).then_inc(ph["trc"], 1)
            pipelined(act, NGRP, 1, group, head=4)
            act_carry(act, ph)

        def act_carry(act, ph):
            act.wait_ge(ph["cv"], ph.upto("cv", 1))
            act_copy(carry_v[0:P, :], bank(7)[0:P, 64:64 + D]).then_inc(ph["cvc"], 1)

        def act_node(act, l):
            ph, lags = NODE[l], NODE_LAGS[l]

            def copies(c, s, k):
                act_groups(act, ph, *groups_by(c, s, lags, k - 1), GROUPS)

            def body(it, s, c, on):
                if on(1):
                    hold(act, "act", ph["u"], ph.upto("u", c))
                    A.activation(n_u[1 - s], n_u[1 - s], ACT.Tanh).then_inc(ph["th"], 1)
                if on(2):
                    hold(act, "act", ph["zc"], ph.upto("zc", c - 1))
                    A.activation(n_q[s], n_z[s], ACT.Square).then_inc(ph["sq"], 1)
                if on(0):
                    copies(c, s, 0)
                if on(1):
                    copies(c, s, 1)
                if l + 1 < L and on(3):
                    copies(c, s, 3)
                    hold(act, "act", ph["mm"], ph.upto("mm", groups_by(c, s, lags, 3)[0]))
                    sc_ = tab_rows[1 - s][:, :, D:ROW]
                    for lo, hi, b in SCORE_TILES:
                        t = act_copy(sc_[:, lo:hi, :], ps[0:P, b:b + (hi - lo) * 16].rearrange("p (t w) -> p t w", w=16))
                    t.then_inc(ph["rows"], 1)
            pipelined(act, NCHUNK, 3 if l + 1 < L else 2, body)

        def act_square(act, ph, asked, told, value, out_, in_):
            hold(act, "act", ph[asked], value)
            A.activation(out_, in_, ACT.Square).then_inc(ph[told], 1)

        def act_square_in(act, it, s, c):
            hold(act, "act", FIN["load1"][s], it * 32 + 32)
            hold(act, "act", FIN["used1"], c - 1)
            A.activation(squares[s], sp_b[s], ACT.Square).then_inc(FIN["sq0"], 1)

        def act_logs(act, ph, n, c_, lp, lm):
            act.wait_ge(ph["act_asked"], ph.upto("act_asked", n + 1))
            A.activation(lp, c_, ACT.Ln, bias=1.0)
            A.activation(lm, c_, ACT.Ln, bias=1.0, scale=-1.0).then_inc(ph["act"], 1)

        def act_fn(act, ph, n, out_, in_, fn, **kw):
            act.wait_ge(ph["act_asked"], ph.upto("act_asked", n + 1))
            A.activation(out_, in_, fn, **kw).then_inc(ph["act"], 1)


        @block.scalar
        def _(act):
            act_weights(act)
            act_table0(act)
            for l in range(L):
                for d in range(2):
                    act_attention(act, l, d)
                act_node(act, l)
            act_fn(act, HYP, 0, bias_sc[0:P, 1:2], bias_sc[0:P, 0:1], ACT.Sqrt)
            act_fn(act, HYP, 1, bias_sc[0:P, 2:3], bias_sc[0:P, 1:2], ACT.Tanh)
            steps(act, NCHUNK, lambda it, s, c: act_square(act, HYP, "r0", "sq", c + 1, squares[s], nchunk(c)))
            act_fn(act, HYP, 2, sc[3], sc[2], ACT.Sqrt)
            act_fn(act, HYP, 3, sc[5], sc[4], ACT.Sqrt)
            act_logs(act, HYP, 4, sc[6], sc[7], sc[8])

            def linear(it, s, c, on):
                if on(0):
                    act_groups(act, HYP, c * GROUPS, s * GROUPS, GROUPS)
                if on(1):
                    hold(act, "act", HYP["mm"], c * GROUPS)
                    y = bank(2 + 3 * (1 - s), 3)[0:P, 0:CN * D].rearrange("p (t w) -> p t w", w=D)
                    act_copy(nchunk(c - 1), y)
                    A.activation(squares[1 - s], y, ACT.Square).then_inc(HYP["y"], 1)
            pipelined(act, NCHUNK, 1, linear)
            act_fn(act, HYP, 5, sc[4], sc[0], ACT.Sqrt)
            act_fn(act, HYP, 6, sc[6], sc[5], ACT.Tanh)
            steps(act, NCHUNK, lambda it, s, c: act_square(act, HYP, "point", "psq", c + 1, squares[s], nchunk(c)))
            act_fn(act, HYP, 7, sc[1], sc[11], ACT.Sqrt)
            act_logs(act, HYP, 8, sc[6], sc[7], sc[8])
            act.wait_ge(HYP["act_asked"], 10)

            def tables(it, s, c):
                hold(act, "act", HYP["store2"][s], it * 32)
                act_copy(hyp_r[s][:, :, 0:D], nchunk(c)).then_inc(HYP["x1"], 1)
                act_copy(hyp_c[s][:, :, 0:D], nchunk(c))
                for t in (hyp_r[s], hyp_c[s]):
                    last_ = act_copy(t[:, :, 2 * D], sc[11][:, bass.ds(c * CN, CN)])
                last_.then_inc(HYP["copied"], 1)
                act_groups(act, HYP, c * GROUPS + NCHUNK * GROUPS, s * GROUPS, GROUPS)
            steps(act, NCHUNK, tables)
            steps(act, NCHUNK, lambda it, s, c: act_square(act, HE, "v", "sq", c + 1, e_sq[s], edges_v[:, bass.ds(c * CE, CE), :]))
            act_fn(act, HE, 0, sc[5][:, 0:TE], sc[3][:, 0:TE], ACT.Sqrt)
            act_logs(act, HE, 1, sc[6][:, 0:TE], sc[7][:, 0:TE], sc[8][:, 0:TE])

            def gate(it, s, c):
                hold(act, "act", HE["pre"], c + 1)
                A.activation(hyp_stage[s], edges_pre[:, bass.ds(c * CE, CE), :], ACT.Sigmoid).then_inc(HE["gate"], 1)
            steps(act, NCHUNK, gate)
            act_fn(act, HE, 2, sc[2][:, 0:TE], sc[0][:, 0:TE], ACT.Sigmoid, bias=att_b2[0:P, :])
            act_carry(act, HE)
            steps(act, NCHUNK, lambda it, s, c: act_square_in(act, it, s, c))
            act_fn(act, FIN, 0, sc[2], sc[0], ACT.Sqrt)
            act_fn(act, FIN, 1, sc[5], sc[4], ACT.Tanh)
            steps(act, NCHUNK, lambda it, s, c: act_square(act, FIN, "x", "sq", c + 1, squares[s], nchunk(c)))
            act_fn(act, FIN, 2, sc[2], sc[0], ACT.Sqrt)
            act_logs(act, FIN, 3, sc[6], sc[7], sc[8])
            steps(act, NCHUNK, lambda it, s, c: act_square(act, FIN, "x", "sq", c + 1 + NCHUNK, squares[s], nchunk(c)))

            act_fn(act, FIN, 4, sc[2], sc[1], ACT.Sqrt)

            def relu(it, s, c):
                hold(act, "act", FIN["x"], c + 1 + 2 * NCHUNK)
                A.activation(squares[s], nchunk(c), ACT.Square)
                A.activation(nchunk(c), nchunk(c), ACT.Relu).then_inc(FIN["relu"], 1)
                hold(act, "act", FIN["relu"], c + 1)
                A.activation(products[s], nchunk(c), ACT.Square).then_inc(FIN["sq"], 1)
            steps(act, NCHUNK, relu)
            act_fn(act, FIN, 5, sc[2], sc[0], ACT.Sqrt)
            act_fn(act, FIN, 6, sc[3], sc[1], ACT.Sqrt)
            act_fn(act, FIN, 7, sc[4], sc[2], ACT.Tanh)
            act_logs(act, FIN, 8, sc[6], sc[7], sc[8])
            act_fn(act, FIN, 9, sc[4], sc[3], ACT.Tanh)
            steps(act, NCHUNK, lambda it, s, c: act_square(act, FIN, "x", "sq", c + 1 + 3 * NCHUNK, squares[s], nchunk(c)))
            act_fn(act, FIN, 10, sc[2], sc[1], ACT.Sqrt)

        def mm(out_, w, x, start=True, stop=True):
            return T.matmul(out_, w, x, start=start, stop=stop)

        def pe_weights(pe):
            pe.wait_ge(s_w, NW)
            pe.wait_ge(s_const, NCONST)
            for l in range(L):
                if l:
                    pe.wait_ge(WP["act"], l)
                for r in range(R):
                    t = T.transpose(bank(0)[:, r * D:(r + 1) * D], w_raw[l][:, r * H * D:(r + 1) * H * D], ident[0:64, 0:64])
                t.then_inc(WP["t"], 1)
                pe.wait_ge(WP["tc"], l + 1)
                for r in range(R):
                    for h in range(H):
                        mm(bank((1, 4)[h])[0:64, r * D:(r + 1) * D], w_t[l][h * D:(h + 1) * D, r * D:(r + 1) * D],
                           w1_edge[l][h * D:(h + 1) * D, r * D:(r + 1) * D])
                for r in range(R):
                    mm(bank(2)[0:64, 0:D], w_t[l][:, r * D:(r + 1) * D], w1_edge[l][:, r * D:(r + 1) * D], start=(r == 0), stop=False)
                mm(bank(2)[0:64, 0:D], ident[0:64, 0:64], w1_top[l], start=False)
                for r in range(R):
                    t = mm(bank(3)[:, 0:D], gat_b[l][:, r:r + 1].broadcast_to([128, 128]), w1_edge[l][:, r * D:(r + 1) * D],
                           start=(r == 0), stop=(r == R - 1))
                t.then_inc(WP["mm"], 1)
                pe.wait_ge(WP["row"], l + 1)
            pe.wait_ge(WP["act"], L)
            T.transpose(bank(0)[0:64, 0:D], lin_raw, ident[0:64, 0:64])
            for k in range(2):
                T.transpose(bank(0)[0:64, (1 + k) * D:(2 + k) * D], att_raw[:, k * D:(k + 1) * D], ident[0:64, 0:64])
            for k in range(2):
                t = mm(bank(0)[:, (3 + k) * D:(4 + k) * D], att_raw[:, 2 * D + k:2 * D + k + 1].broadcast_to([64, 128]), ident[0:64, 0:64])
            t.then_inc(WP["mm"], 1)
            pe.wait_ge(WP["act"], L + 1)

        def pe_transpose_group(pe, ph, b, value, tile):
            hold(pe, "pe", ph["trc"], ph.upto("trc", value - 1))
            for i in range(GRP):
                t = T.transpose(bank(b)[0:64, i * P:(i + 1) * P], tile(i), ident[0:P, 0:P])
            t.then_inc(ph["tr"], 1)

        def pe_groups(pe, ph, base, parity, n, tile, w, out_):
            def products(j):
                hold(pe, "pe", ph["trc"], ph.upto("trc", base + j + 1))
                b = (parity + j) % 2
                for i in range(GRP):
                    t = mm(out_(j * GRP + i), trv[b][0:w.shape[0], i * P:(i + 1) * P], w)
                t.then_inc(ph["mm"], 1)
            for j in range(n):
                pe_transpose_group(pe, ph, (parity + j) % 2, base + j, lambda i: tile(j * GRP + i))
                if j:
                    products(j - 1)
            products(n - 1)

        def out_tile(b, width):
            return lambda t: ps[0:P, b * 512 + t * width:b * 512 + (t + 1) * width]

        def pe_table0(pe, at, n):
            def body(it, s, c):
                hold(pe, "pe", TAB["load"][s], it * 16 + 16)
                hold(pe, "pe", TAB["rows"], c)
                pe_groups(pe, TAB, c * GROUPS, s * GROUPS, GROUPS, lambda t: tab_rows[s][:, t, 0:D], proj_w[0][:, :], out_tile(5, 16))
            steps(pe, n, body, at)

        def pe_sort(pe, k):
            pe.wait_ge(SORT[k]["hist"], SORT[k].upto("hist", 1))
            mm(bank(7)[0:P, 0:RADIX], tri_lt[0:P, 0:P], hist[0:P, :])
            mm(bank(7)[0:P, RADIX:2 * RADIX], ones[0:P, 0:P], hist[0:P, :]).then_inc(SORT[k]["base"], 1)

        def pe_order(pe, o):
            pe.wait_ge(ORD[o]["diag"], ORD[o].upto("diag", 1))
            for k in range(2):
                t = mm(bank(7)[0:P, k * 128:k * 128 + P], ones[0:P, 0:P], key_diag[0:P, k, 0:P])
            t.then_inc(ORD[o]["bc"], 1)

        def pe_carry(pe, ph, o, v_last):
            pe.wait_ge(ph["scan"], ph.upto("scan", 1))
            mm(bank(7)[0:P, 64:64 + D], carry_f[o][0:P, 0:P], v_last).then_inc(ph["cv"], 1)

        def pe_attention(pe, l, d):
            ph = ATT[l][d]
            for k in range(2):
                pe.wait_ge(ph["diag"], ph.upto("diag", k + 1))
                mm(bank(6)[0:P, 0:4 * P], ones[0:P, 0:P], diag[0:P, :, :].rearrange("p s q -> p (s q)")).then_inc(ph["bc"], 1)
            pe.wait_ge(ph["diag"], ph.upto("diag", 3))
            mm(bank(7)[0:P, 0:4], carry_f[d][0:P, 0:P], att[2][:, :, TE - 1])
            mm(bank(7)[0:P, 4:8], carry_b[d][0:P, 0:P], att[3][:, :, 0]).then_inc(ph["sums"], 1)

            def group(it, s, g, on):
                if on(0):
                    hold(pe, "pe", ph["copied"], ph.upto("copied", g + 1))
                    pe_transpose_group(pe, ph, s, g, lambda i: grp_stage[0:P, s, i * D:(i + 1) * D])
                if on(1):
                    hold(pe, "pe", ph["trc"], ph.upto("trc", g))
                    hold(pe, "pe", ph["prod"], ph.upto("prod", g - 2))
                    for i in range(GRP):
                        t = mm(bank(2 + 2 * (1 - s), 2)[0:P, i * 4 * D:(i + 1) * 4 * D], trv[1 - s][0:D, i * P:(i + 1) * P], edge_w[l][:, d, :])
                    t.then_inc(ph["mm"], 1)
            pipelined(pe, NGRP, 1, group, head=4)
            pe_carry(pe, ph, d, G[d][:, TE - 1, 0:D])

        def pe_node(pe, l):
            ph, lags = NODE[l], NODE_LAGS[l]

            def score_tile(t):
                lo, _, b = SCORE_TILES[t >= SCORE_TILES[0][1]]
                return ps[0:P, b + (t - lo) * 16:b + (t - lo + 1) * 16]

            def body(it, s, c, on):
                def groups(k, tile, w, out_):
                    pe_groups(pe, ph, *groups_by(c, s, lags, k - 1), GROUPS, tile, w[:, :], out_)
                if on(0):
                    if l + 1 < L:
                        hold(pe, "pe", ph["rows"], ph.upto("rows", c - 3))
                    hold(pe, "pe", ph["hin"][s], ph.upto("hin", it * 16 + 16))
                    hold(pe, "pe", ph["u"], ph.upto("u", c))
                    groups(0, lambda t: n_h[s][:, t, 0:D], dense_w[l], out_tile(2, D))
                if on(1):
                    hold(pe, "pe", ph["th"], ph.upto("th", c))
                    hold(pe, "pe", ph["z"], ph.upto("z", c - 1))
                    groups(1, lambda t: n_u[1 - s][:, t, :], mlp_w2[l], out_tile(5, D))
                if l + 1 < L and on(3):
                    hold(pe, "pe", ph["h"], ph.upto("h", c - 2))
                    hold(pe, "pe", ph["rows"], ph.upto("rows", c - 3))
                    hold(pe, "pe", ph["u"], ph.upto("u", min(c + 1, NCHUNK) if isinstance(c, int) else c + 1))
                    hold(pe, "pe", ph["z"], ph.upto("z", min(c, NCHUNK) if isinstance(c, int) else c))
                    groups(3, lambda t: tab_rows[1 - s][:, t, 0:D], proj_w[l + 1], score_tile)
            pipelined(pe, NCHUNK, 3 if l + 1 < L else 1, body)

        def pe_hyp(pe):
            ph = HYP

            def lin(it, s, c):
                hold(pe, "pe", ph["x0"], c + 1)
                hold(pe, "pe", ph["y"], c - 1)
                pe_groups(pe, ph, c * GROUPS, s * GROUPS, GROUPS, lambda t: sp_a[s][:, t, :], lin_t[:, :], out_tile(2 + 3 * s, D))
            steps(pe, NCHUNK, lin)

            def mlp(it, s, c):
                hold(pe, "pe", ph["x1"], c + 1)
                hold(pe, "pe", ph["pq"], c)
                pe_groups(pe, ph, c * GROUPS + NCHUNK * GROUPS, s * GROUPS, GROUPS, lambda t: hyp_r[s][:, t, 0:D], att_t[:, :], out_tile(2, 2 * D))
            steps(pe, NCHUNK, mlp)

        @block.tensor
        def _(pe):
            pe_weights(pe)
            pe.wait_ge(WP["dve"], 1)
            pe_table0(pe, 0, 6)
            pe_sort(pe, 0)
            pe_table0(pe, 6, 12)
            pe_sort(pe, 1)
            pe_table0(pe, 12, NCHUNK)
            pe_order(pe, 0)
            pe_sort(pe, 2)
            pe_sort(pe, 3)
            pe_order(pe, 1)
            for l in range(L):
                for d in range(2):
                    pe_attention(pe, l, d)
                pe_node(pe, l)
            pe_hyp(pe)
            pe_carry(pe, HE, 1, edges_v[:, TE - 1, :])

        @block.vector
        def _(dve):
            chain = [0]

            def link(ins, wait=True):
                chain[0] += 1
                ins.then_inc(s_link, 1)
                if wait:
                    dve.wait_ge(s_link, chain[0])

            def reset():
                if chain[0]:
                    dve.wait_ge(s_link, chain[0])
                    dve.sem_clear(s_link)
                    chain[0] = 0

            def done(s):
                if chain[0]:
                    dve.wait_ge(s_link, chain[0])
                dve.sem_inc(s, 1)

            def wait(s, v):
                hold(dve, "dve", s, v)

            def tt(o, x, y, op, w=True):
                link(V.tensor_tensor(o, x, y, op), w)

            def ts(o, x, s1, s2, op0, op1=None, w=True):
                link(V.tensor_scalar(o, x, s1, s2, op0, op1) if op1 is not None else V.tensor_scalar(o, x, s1, None, op0), w)

            def stt(o, x, s, y, op0, op1, w=True):
                link(V.scalar_tensor_tensor(o, x, s, y, op0, op1), w)

            def red(o, x, op=ALU.add, w=True):
                link(V.tensor_reduce(o, x, X, op), w)

            def copy(o, x, w=True):
                link(V.tensor_copy(o, x), w)

            def recip(o, x):
                link(V.reciprocal(o, x))

            def center(x, mean, n):
                red(mean, x)
                ts(mean, mean, -1.0 / D, None, ALU.mult)
                tt(x, x, cols(mean), ALU.add)

            def dot(o, x, y, tmp):
                tt(tmp, x, y, ALU.mult)
                sum64(o, tmp)

            def sum64(o, x):
                n = x.shape[1]
                red(part[0:P, 0:n * 8], x.rearrange("p t (a b) -> p t a b", a=8))
                red(o, part[0:P, 0:n * 8].rearrange("p (t a) -> p t a", a=8))

            asked = {}

            def ask(ph, who):
                key = (id(ph), who)
                asked[key] = asked.get(key, 0) + 1
                done(ph[who + "_asked"])
                dve.wait_ge(ph[who], asked[key])

            def root(ph, o, x, t):
                ask(ph, "act")
                ts(o, o, 1e-19, None, ALU.max)
                recip(t, o)
                tt(t, t, x, ALU.mult)
                tt(o, o, t, ALU.add)
                ts(o, o, 0.5, None, ALU.mult)

            def artanh_ratio(o, c, lp, lm, t1, t2):
                tt(t1, c, c, ALU.mult)
                ts(o, t1, 1.0 / 13, None, ALU.mult)
                for k in (11, 9, 7, 5, 3):
                    stt(o, o, 1.0 / k, t1, ALU.add, ALU.mult)
                ts(o, o, 1.0, None, ALU.add)
                tt(t2, lp, lm, ALU.subtract)
                recip(t1, c)
                stt(t2, t2, 0.5, t1, ALU.mult, ALU.mult)
                ts(t1, c, 0.25, None, ALU.is_lt)
                tt(o, o, t2, ALU.subtract)
                tt(o, o, t1, ALU.mult)
                tt(o, o, t2, ALU.add)

            for l in range(L):
                link(V.memset(proj_w[l][D:D + 1, :], 0.0), False)
            link(V.memset(tr[D:D + 1, :, :], 1.0), False)
            dve.wait_ge(s_w, NW)
            for l in range(L):
                for k in range(2):
                    tt(w_prod, w_raw[l], a_raw[l][:, k * R * H * D:(k + 1) * R * H * D], ALU.mult)
                    red(w_red[:, k * R * H:(k + 1) * R * H], w_prod.rearrange("i (r c) -> i r c", c=D))
                for k in range(2):
                    for d in range(2):
                        copy(proj_w[l][0:D, k * 8 + d * 4:k * 8 + d * 4 + 4].rearrange("i (g h) -> i g h", g=2),
                             w_red[:, k * 8:(k + 1) * 8].rearrange("i (g d h) -> i g d h", g=2, d=2)[:, :, d, :])
            done(WP["dve"])
            for l in range(L):
                dve.wait_ge(WP["mm"], l + 1)
                tt(dense_w[l][D:D + 1, :], dense_w[l][D:D + 1, :], bank(3)[D:D + 1, 0:D], ALU.add)
                done(WP["row"])
            reset()

            dve.wait_ge(s_in, 64)
            dve.wait_ge(s_const, NCONST)
            copy(digits_row[:, :], digits_i[:, :], False)
            for k in range(2):
                copy(rec_v[:, :, k], (dst_i, src_i)[k][1][0:P, :], False)
                copy(rec_v[:, :, 2 + k], off[0][0:P, k, :], False)
            copy(rec_v[:, :, 4], position_i[0:P, :])

            def sort_pass(k):
                ph = SORT[k]
                key, high = k // 2, k % 2
                if k:
                    dve.wait_ge(SORT[k - 1]["rec"], SORT[k - 1].upto("rec", 16))
                copy(digit_i[0:P, :], rec_v[:, :, key])
                if high:
                    ts(digit_i[0:P, :], digit_i[0:P, :], 8, None, ALU.logical_shift_right)
                else:
                    ts(digit_i[0:P, :], digit_i[0:P, :], RADIX - 1, None, ALU.bitwise_and)
                copy(digit[0:P, :], digit_i[0:P, :])
                link(V.memset(hist[0:P, :], 0.0))
                link(V.memset(matched[0:P, :], 0.0))
                reset()
                with dve.Fori(0, NCHUNK) as c:
                    for j in range(CE):
                        if j > 1:
                            dve.wait_ge(s_link, chain[0] - 1)
                        h_ = (hist, matched)[j % 2][0:P, :]
                        stt(h_, digits_row[0:P, :], digit[0:P, bass.ds(c * CE + j, 1)], h_, ALU.is_equal, ALU.add, False)
                    reset()
                tt(hist[0:P, :], hist[0:P, :], matched[0:P, :], ALU.add)
                done(ph["hist"])
                dve.wait_ge(ph["base"], ph.upto("base", 1))
                copy(total[0:P, :], bank(7)[0:P, RADIX:2 * RADIX])
                link(V.tensor_tensor_scan(cursor[0:P, :], ones[0:P, 0:1].broadcast_to([P, RADIX]), total[0:P, :], 0.0, ALU.mult, ALU.add))
                tt(cursor[0:P, :], cursor[0:P, :], total[0:P, :], ALU.subtract)
                tt(cursor[0:P, :], cursor[0:P, :], bank(7)[0:P, 0:RADIX], ALU.add)
                reset()

                def places(it, s, c):
                    for j in range(CE):
                        mine = digit[0:P, bass.ds(c * CE + j, 1)]
                        link(V.scalar_tensor_tensor(matched[0:P, :], digits_row[0:P, :], mine, cursor[0:P, :], ALU.is_equal, ALU.mult,
                                                    accum_out=rank[0:P, j:j + 1]))
                        stt(cursor[0:P, :], digits_row[0:P, :], mine, cursor[0:P, :], ALU.is_equal, ALU.add)
                    wait(ph["scattered"][s], ph.upto("scattered", it * (16 * CE)))
                    copy(place_i[0:P, s, :], rank[0:P, :], False)
                    copy(rec_stage[0:P, s, :].rearrange("p (t c) -> p t c", c=REC), rec_v[:, bass.ds(c * CE, CE), :])
                    done(ph["staged"])
                    reset()
                steps(dve, NCHUNK, places)

            def order_info(o):
                key = rec_v[:, :, o]
                dve.wait_ge(SORT[2 * o + 1]["rec"], SORT[2 * o + 1].upto("rec", 16))
                copy(dst_i[o][0:P, :], rec_v[:, :, 0], False)
                copy(src_i[o][0:P, :], rec_v[:, :, 1], False)
                for g, op in enumerate((ALU.is_gt, ALU.is_lt)):
                    ts(off[o][0:P, g, :], rec_v[:, :, 2], 0.0, BIG, op, ALU.mult)
                    ts(off[o][0:P, g, :], off[o][0:P, g, :], -BIG, None, ALU.add)
                link(V.memset(keep[o][0:P, 0:1], 0.0), False)
                link(V.memset(keep_b[o][0:P, TE - 1:TE], 0.0), False)
                tt(keep[o][0:P, 1:TE], key[:, 1:TE], key[:, 0:TE - 1], ALU.is_equal, False)
                tt(keep_b[o][0:P, 0:TE - 1], key[:, 1:TE], key[:, 0:TE - 1], ALU.is_equal, False)
                ts(first[o][0:P, :], key, key[:, 0:1], None, ALU.is_equal, w=False)
                ts(last[o][0:P, :], key, key[:, TE - 1:TE], None, ALU.is_equal, w=False)
                for k, t in enumerate((0, TE - 1)):
                    ts(key_diag[0:P, k, 0:P], ident[0:P, 0:P], key[:, t:t + 1], None, ALU.mult, w=False)
                done(ORD[o]["diag"])
                dve.wait_ge(ORD[o]["bc"], ORD[o].upto("bc", 1))
                kf, kl = bank(7)[0:P, 0:P], bank(7)[0:P, 128:128 + P]
                k0, k1 = key[:, 0:1], key[:, TE - 1:TE]
                stt(carry_f[o][0:P, 0:P], kf, k1, tri_lt[0:P, 0:P], ALU.is_equal, ALU.mult, False)
                stt(carry_b[o][0:P, 0:P], kl, k0, tri_gt[0:P, 0:P], ALU.is_equal, ALU.mult, False)
                stt(far_f[o][0:P, 0:P], kl, k0, tri_gt[0:P, 0:P], ALU.is_equal, ALU.mult, False)
                stt(far_b[o][0:P, 0:P], kf, k1, tri_lt[0:P, 0:P], ALU.is_equal, ALU.mult)
                red(goes_on[0:P, :], far_b[o][0:P, 0:P], ALU.max)
                for m in (far_f, far_b):
                    ts(m[o][0:P, 0:P], m[o][0:P, 0:P], BIG, -BIG, ALU.mult, ALU.add, w=False)
                stt(digit[0:P, :], keep_b[o][0:P, :], float(SKIP), key, ALU.mult, ALU.add)
                stt(digit[0:P, TE - 1:TE], goes_on[0:P, :], float(SKIP), digit[0:P, TE - 1:TE], ALU.mult, ALU.add)
                copy(out_i[o][0:P, :], digit[0:P, :], False)
                if o:
                    copy(pair_i[0:P, :], rec_v[:, :, 4], False)
                    copy(weight1[0:P, :], rec_v[:, :, 3], False)
                done(ORD[o]["done"])

            for o in range(2):
                for k in range(2):
                    sort_pass(2 * o + k)
                order_info(o)
                if o == 0:
                    copy(rec_v[:, :, 4], position_i[0:P, :])
            reset()

            def edge_rows(l):
                ph = EDGE[l]

                def body(it, s, c):
                    wait(ph["gathered"][s], ph.upto("gathered", it * (32 * CE) + 32 * CE))
                    g, a_, b_ = G[0][:, bass.ds(c * CE, CE), :], g_src[s], g_dst[s]
                    es, ed = D, D + 8
                    tt(g[:, :, 0:D], a_[:, :, 0:D], b_[:, :, 0:D], ALU.subtract, False)
                    tt(g[:, :, D:D + 4], a_[:, :, es:es + 4], b_[:, :, ed:ed + 4], ALU.add, False)
                    tt(g[:, :, D + 4:D + 8], b_[:, :, es:es + 4], b_[:, :, ed:ed + 4], ALU.add, False)
                    tt(g[:, :, D + 8:D + 12], b_[:, :, es + 4:es + 8], a_[:, :, ed + 4:ed + 8], ALU.add, False)
                    tt(g[:, :, D + 12:D + 16], a_[:, :, es + 4:es + 8], a_[:, :, ed + 4:ed + 8], ALU.add, False)
                    done(ph["rows"])
                    reset()
                steps(dve, NCHUNK, body)

            def scan(o, d0, d1, init, op0, op1, back=False, w=False):
                if back:
                    o, d0, d1 = o[:, ::-1], d0[:, ::-1], d1[:, ::-1]
                link(V.tensor_tensor_scan(o, d0, d1, init, op0, op1), w)

            def attention(l, d):
                ph, o = ATT[l][d], d
                Es, Sf, F, B, mx, pp = att
                if d:
                    for s in range(2):
                        dve.wait_ge(EDGE[l]["copied"][s], EDGE[l].upto("copied", 16 * NCHUNK // 2))
                for k, m in enumerate((keep, keep_b, first, last)):
                    ts(seg_off[0:P, k, :], m[o][0:P, :], BIG, -BIG, ALU.mult, ALU.add, w=False)
                for to, at in ((Es, D + 8 * d), (Sf, D + 8 * d + 4)):
                    x = G[d][:, :, at:at + 4].rearrange("p t s -> p s t")
                    stt(to, x, 0.2, x, ALU.mult, ALU.max, False)
                dve.wait_ge(s_link, chain[0])
                for g in range(2):
                    tt(Es[:, 2 * g:2 * g + 2, :], Es[:, 2 * g:2 * g + 2, :], off[o][0:P, g:g + 1, :].broadcast_to([P, 2, TE]), ALU.add, False)
                dve.wait_ge(s_link, chain[0])
                for s in range(4):
                    scan(F[:, s, :], seg_off[0:P, 0, :], Es[:, s, :], -BIG, ALU.add, ALU.max)
                    scan(B[:, s, :], seg_off[0:P, 1, :], Es[:, s, :], -BIG, ALU.add, ALU.max, back=True)
                dve.wait_ge(s_link, chain[0])
                tt(mx, F, B, ALU.max)
                tt(mx, mx, Sf, ALU.max)
                for k, (edge, farm) in enumerate(((F[:, :, TE - 1], far_f), (B[:, :, 0], far_b))):
                    if k:
                        dve.wait_ge(ph["bc"], ph.upto("bc", k))
                    for s in range(4):
                        ts(diag[0:P, s, :], ident[0:P, 0:P], edge[:, s:s + 1], None, ALU.mult, w=False)
                    done(ph["diag"])
                    dve.wait_ge(ph["bc"], ph.upto("bc", k + 1))
                    tt(far[0:P, :, :], bank(6)[0:P, 0:4 * P].rearrange("p (s q) -> p s q", s=4),
                       farm[o][0:P, 0:P].unsqueeze(1).broadcast_to([P, 4, P]), ALU.add)
                    red(carry4[0:P, k, :], far[0:P, :, :], ALU.max)
                for k in range(2):
                    for s in range(4):
                        stt(mx[:, s, :], seg_off[0:P, 2 + k, :], carry4[0:P, k, s:s + 1], mx[:, s, :], ALU.add, ALU.max, False)
                    dve.wait_ge(s_link, chain[0])
                tt(F, Es, mx, ALU.subtract, False)
                tt(B, Sf, mx, ALU.subtract, False)
                done(ph["dve"])
                dve.wait_ge(ph["exp"], ph.upto("exp", 1))
                for s in range(4):
                    scan(F[:, s, :], keep[o][0:P, :], pp[:, s, :], 0.0, ALU.mult, ALU.add)
                    scan(B[:, s, :], keep_b[o][0:P, :], pp[:, s, :], 0.0, ALU.mult, ALU.add, back=True)
                done(ph["diag"])
                dve.wait_ge(ph["exp"], ph.upto("exp", 2))
                tt(F, F, B, ALU.add)
                tt(F, F, pp, ALU.subtract)
                tt(F, F, Sf, ALU.add)
                for k, m in ((2, first), (3, last)):
                    for s in range(4):
                        stt(F[:, s, :], m[o][0:P, :], carry4[0:P, k, s:s + 1], F[:, s, :], ALU.mult, ALU.add, False)
                    dve.wait_ge(s_link, chain[0])
                recip(F, F)
                stt(Es, pp, 1.0 if d == 0 else -1.0, F, ALU.mult, ALU.mult)
                if d == 0:
                    dve.wait_ge(EDGE[l]["pair"], EDGE[l].upto("pair", 16 * NCHUNK))
                reset()

                def group(it, s, g):
                    wait(ph["mm"], ph.upto("mm", g + 1))
                    pr = prod[0:P, :].rearrange("p (t s n) -> p t s n", t=GRP, s=4)
                    tt(pr, bank(2 + 2 * s, 2)[0:P, :].rearrange("p (t s n) -> p t s n", t=GRP, s=4),
                       Es[:, :, bass.ds(g * GRP, GRP)].rearrange("p s t -> p t s").unsqueeze(3).broadcast_to([P, GRP, 4, D]), ALU.mult)
                    dve.sem_inc(ph["prod"], 1)
                    red(G[d][:, bass.ds(g * GRP, GRP), 0:D], pr.rearrange("p t s n -> p t n s"))
                    reset()
                steps(dve, NGRP, group)

            def segment_sums(ph, v, o):
                with dve.Fori(0, D // 8) as f:
                    for j in range(8):
                        vf = v[:, :, bass.ds(f * 8 + j, 1)].rearrange("p t a -> p (t a)")
                        scan(vf, keep[o][0:P, :], vf, 0.0, ALU.mult, ALU.add)
                    reset()
                done(ph["scan"])
                dve.wait_ge(ph["cvc"], ph.upto("cvc", 1))

            def carry_in(ph, v, o, tmp):
                with dve.Fori(0, NCHUNK) as c:
                    at = bass.ds(c * CE, CE)
                    tt(tmp, cols(first[o][0:P, at]), rows_of(carry_v, CE), ALU.mult)
                    tt(v[:, at, 0:D], v[:, at, 0:D], tmp, ALU.add)
                    reset()
                done(ph["carried"])

            def node_update(l):
                ph, lags = NODE[l], NODE_LAGS[l]
                z_ps = [bank(b, 3)[0:P, 0:CN * D].rearrange("p (t w) -> p t w", w=D) for b in (2, 5)]

                def body(it, s, c, on):
                    if on(0):
                        wait(ph["corr"][s], ph.upto("corr", it * 32 + 32))
                        tt(n_f[s], n_f[s], n_r[s], ALU.add)
                        wait(ph["mm"], ph.upto("mm", groups_by(c, s, lags, 0)[0]))
                        tt(n_u[s], z_ps[0], n_f[s], ALU.add)
                        done(ph["u"])
                    if on(1):
                        z = n_z[1 - s]
                        wait(ph["mm"], ph.upto("mm", groups_by(c, s, lags, 1)[0]))
                        tt(z, z_ps[1], n_h[1 - s][:, :, 0:D], ALU.add)
                        done(ph["z"])
                        center(z, small[0:P, 0, :], CN)
                        done(ph["zc"])
                    if on(2):
                        z = n_z[s]
                        wait(ph["rstd"], ph.upto("rstd", c - 1))
                        tt(z, z, cols(small[0:P, 4 + s, :]), ALU.mult)
                        tt(z, z, rows_of(g_row[l], CN), ALU.mult)
                        wait(ph["store"][s], ph.upto("store", (it - 1) * 16))
                        tt(tab_rows[s][:, :, 0:D], z, rows_of(be_row[l], CN), ALU.add)
                        done(ph["h"] if l + 1 < L else ph["rows"])
                    if on(1):
                        wait(ph["sq"], ph.upto("sq", c))
                        red(small[0:P, 3 - s, :], n_q[1 - s])
                        ts(small[0:P, 3 - s, :], small[0:P, 3 - s, :], 1.0 / D, 1e-5, ALU.mult, ALU.add)
                        done(ph["var"])
                    reset()
                pipelined(dve, NCHUNK, 2, body, head=4)

            for l in range(L):
                edge_rows(l)
                for d in range(2):
                    attention(l, d)
                    segment_sums(ATT[l][d], G[d], d)
                    carry_in(ATT[l][d], G[d], d, prod[0:P, 0:CE * D].rearrange("p (t w) -> p t w", w=D))
                node_update(l)

            tt(products[0][:, 0, :], hyp_bias[0:P, :], hyp_bias[0:P, :], ALU.mult)
            red(bias_sc[0:P, 0:1], products[0][:, 0, :])
            root(HYP, bias_sc[0:P, 1:2], bias_sc[0:P, 0:1], bias_sc[0:P, 5:6])
            ts(bias_sc[0:P, 1:2], bias_sc[0:P, 1:2], MIN_NORM, None, ALU.max)
            ask(HYP, "act")
            ts(bias_sc[0:P, 2:3], bias_sc[0:P, 2:3], MAXNORM, None, ALU.min)
            recip(bias_sc[0:P, 3:4], bias_sc[0:P, 1:2])
            tt(bias_sc[0:P, 3:4], bias_sc[0:P, 3:4], bias_sc[0:P, 2:3], ALU.mult)
            ts(hyp_bias[0:P, :], hyp_bias[0:P, :], bias_sc[0:P, 3:4], None, ALU.mult)
            tt(products[0][:, 0, :], hyp_bias[0:P, :], hyp_bias[0:P, :], ALU.mult)
            red(bias_sc[0:P, 4:5], products[0][:, 0, :])
            y2 = bias_sc[0:P, 4:5]
            reset()
            ph = HYP

            def scol(k, c):
                return sc[k][:, bass.ds(c * CN, CN)]

            def squares_sum(key, k, sums, value=0):
                def stage(s, c):
                    wait(ph[key], c + value)
                    sums(scol(k, c - 1), squares[1 - s])
                return stage

            def residual(it, s, c, on):
                if on(0):
                    wait(ph["load"][s], it * 32 + 32)
                    x = nchunk(c)
                    tt(x, sp_a[s], sp_b[s], ALU.add)
                    done(ph["used"])
                    center(x, small[0:P, 0, :], CN)
                    done(ph["r0"])
                if on(1):
                    squares_sum("sq", 1, red)(s, c)
                reset()
            pipelined(dve, NCHUNK, 1, residual)
            ts(sc[2], sc[1], 1.0 / D, 1e-5, ALU.mult, ALU.add)
            root(ph, sc[3], sc[2], sc[4])
            recip(sc[3], sc[3])
            tt(sc[4], sc[1], sc[3], ALU.mult)
            tt(sc[4], sc[4], sc[3], ALU.mult)
            root(ph, sc[5], sc[4], sc[6])
            ts(sc[5], sc[5], MIN_NORM, None, ALU.max)
            ts(sc[6], sc[5], CLIP, None, ALU.min)
            ask(ph, "act")
            artanh_ratio(sc[9], sc[6], sc[7], sc[8], sc[10], sc[4])
            tt(sc[9], sc[9], sc[6], ALU.mult)
            recip(sc[5], sc[5])
            tt(sc[9], sc[9], sc[5], ALU.mult)
            reset()

            def linear(it, s, c, on):
                if on(0):
                    if not isinstance(c, int):
                        wait(ph["store"][s], it * 16)
                    tt(sp_a[s], nchunk(c), cols(scol(3, c)), ALU.mult)
                    done(ph["x0"])
                if on(1):
                    wait(ph["y"], c)
                    tt(products[1 - s], nchunk(c - 1), rows_of(hyp_bias, CN), ALU.mult)
                    sum64(scol(2, c - 1), products[1 - s])
                    squares_sum("y", 0, sum64)(s, c)
                reset()
            pipelined(dve, NCHUNK, 1, linear)
            root(ph, sc[4], sc[0], sc[5])
            tt(sc[5], sc[4], sc[9], ALU.mult)
            ts(sc[5], sc[5], MIN_NORM, None, ALU.max)
            ask(ph, "act")
            ts(sc[7], sc[6], MAXNORM, None, ALU.min)
            recip(sc[8], sc[5])
            tt(sc[8], sc[8], sc[7], ALU.mult)
            tt(sc[8], sc[8], sc[9], ALU.mult)
            tt(sc[10], sc[8], sc[8], ALU.mult)
            tt(sc[10], sc[10], sc[0], ALU.mult)
            tt(sc[6], sc[8], sc[2], ALU.mult)
            ts(sc[4], sc[6], 2.0, 1.0, ALU.mult, ALU.add)
            stt(sc[7], sc[10], y2, sc[4], ALU.mult, ALU.add)
            ts(sc[7], sc[7], MIN_NORM, None, ALU.max)
            recip(sc[7], sc[7])
            ts(sc[4], sc[4], y2, None, ALU.add)
            tt(sc[8], sc[8], sc[4], ALU.mult)
            tt(sc[8], sc[8], sc[7], ALU.mult)
            ts(sc[5], sc[10], -1.0, 1.0, ALU.mult, ALU.add)
            tt(sc[5], sc[5], sc[7], ALU.mult)
            reset()

            def point(it, s, c, on):
                if on(0):
                    x = nchunk(c)
                    tt(x, x, cols(scol(8, c)), ALU.mult, False)
                    tt(products[s], cols(scol(5, c)), rows_of(hyp_bias, CN), ALU.mult)
                    tt(x, x, products[s], ALU.add)
                    done(ph["point"])
                if on(1):
                    squares_sum("psq", 11, sum64)(s, c)
                reset()
            pipelined(dve, NCHUNK, 1, point)
            root(ph, sc[1], sc[11], sc[6])
            ts(sc[1], sc[1], MIN_NORM, None, ALU.max)
            ts(sc[6], sc[1], CLIP, None, ALU.min)
            ask(ph, "act")
            artanh_ratio(sc[9], sc[6], sc[7], sc[8], sc[10], sc[4])
            tt(sc[9], sc[9], sc[6], ALU.mult)
            recip(sc[1], sc[1])
            tt(sc[9], sc[9], sc[1], ALU.mult)
            for s in range(2):
                dve.wait_ge(ph["store"][s], 16 * NCHUNK // 2)
            done(ph["act_asked"])
            reset()

            def tables(it, s, c):
                r_, c_ = hyp_r[s], hyp_c[s]
                wait(ph["copied"], c + 1)
                wait(ph["mm"], (c + 1) * GROUPS + NCHUNK * GROUPS)
                pq = bank(2, 5)[0:P, 0:CN * 2 * D].rearrange("p (t w) -> p t w", w=2 * D)
                tt(c_[:, :, D:2 * D], pq[:, :, D:2 * D], cols(scol(9, c)), ALU.mult, False)
                tt(r_[:, :, D:2 * D], pq[:, :, 0:D], cols(scol(9, c)), ALU.mult)
                done(ph["pq"])
                tt(r_[:, :, D:2 * D], r_[:, :, D:2 * D], rows_of(hyp_row["b1"], CN), ALU.add)
                done(ph["rows"])
                reset()
            steps(dve, NCHUNK, tables)

            ph = HE

            def ecol(k, c=None):
                return sc[k][:, 0:TE] if c is None else sc[k][:, bass.ds(c * CE, CE)]

            def edge_points(it, s, c, on):
                if on(0):
                    wait(ph["gathered"][s], it * (32 * CE) + 32 * CE)
                    r_, c_ = h_row[s], h_col[s]
                    xr, xc, tmp = r_[:, :, 0:D], c_[:, :, 0:D], e_tmp[s]
                    v, pre = edges_v[:, bass.ds(c * CE, CE), :], edges_pre[:, bass.ds(c * CE, CE), :]
                    dot(ecol(0, c), xr, xc, tmp)
                    copy(ecol(1, c), r_[:, :, 2 * D], False)
                    copy(ecol(2, c), c_[:, :, 2 * D], False)
                    stt(small[0:P, 0, 0:CE], ecol(0, c), 2.0, c_[:, :, 2 * D], ALU.mult, ALU.subtract, False)
                    ts(small[0:P, 1, 0:CE], r_[:, :, 2 * D], -1.0, 1.0, ALU.mult, ALU.add)
                    ts(small[0:P, 0, 0:CE], small[0:P, 0, 0:CE], -1.0, None, ALU.add)
                    tt(v, xr, cols(small[0:P, 0, 0:CE]), ALU.mult, False)
                    tt(tmp, xc, cols(small[0:P, 1, 0:CE]), ALU.mult)
                    tt(v, v, tmp, ALU.add)
                    done(ph["v"])
                    tt(pre, r_[:, :, D:2 * D], c_[:, :, D:2 * D], ALU.add, False)
                    tt(tmp, cols(weight1[0:P, bass.ds(c * CE, CE)]), rows_of(hyp_row["wd"], CE), ALU.mult)
                    tt(pre, pre, tmp, ALU.add)
                    done(ph["rows"])
                if on(1):
                    wait(ph["sq"], c)
                    sum64(ecol(3, c - 1), e_sq[1 - s])
                reset()
            pipelined(dve, NCHUNK, 1, edge_points)
            tt(ecol(4), ecol(1), ecol(2), ALU.mult)
            stt(ecol(4), ecol(0), -2.0, ecol(4), ALU.mult, ALU.add)
            ts(ecol(4), ecol(4), 1.0, MIN_NORM, ALU.add, ALU.max)
            recip(ecol(4), ecol(4))
            root(ph, ecol(5), ecol(3), ecol(6))
            tt(ecol(5), ecol(5), ecol(4), ALU.mult)
            ts(ecol(5), ecol(5), MIN_NORM, None, ALU.max)
            ts(ecol(6), ecol(5), CLIP, None, ALU.min)
            ask(ph, "act")
            artanh_ratio(ecol(9), ecol(6), ecol(7), ecol(8), ecol(10), ecol(2))
            tt(ecol(9), ecol(9), ecol(6), ALU.mult)
            stt(ecol(10), ecol(9), 4.0, ecol(9), ALU.mult, ALU.mult)
            reset()

            def mlp(it, s, c, on):
                if on(0):
                    pre = edges_pre[:, bass.ds(c * CE, CE), :]
                    tt(e_tmp[s], cols(ecol(10, c)), rows_of(hyp_row["wg"], CE), ALU.mult)
                    tt(pre, pre, e_tmp[s], ALU.add)
                    done(ph["pre"])
                if on(1):
                    pre = edges_pre[:, bass.ds((c - 1) * CE, CE), :]
                    wait(ph["gate"], c)
                    tt(pre, pre, hyp_stage[1 - s], ALU.mult)
                    tt(pre, pre, rows_of(hyp_row["w2"], CE), ALU.mult)
                    red(ecol(0, c - 1), pre)
                reset()
            pipelined(dve, NCHUNK, 1, mlp)
            ask(ph, "act")
            tt(ecol(2), ecol(2), weight1[0:P, :], ALU.mult)
            ts(ecol(1), ecol(1), -1.0, 1.0, ALU.mult, ALU.add)
            ts(ecol(1), ecol(1), MIN_NORM, None, ALU.max)
            tt(ecol(1), ecol(1), ecol(9), ALU.mult)
            recip(ecol(5), ecol(5))
            tt(ecol(1), ecol(1), ecol(5), ALU.mult)
            tt(ecol(1), ecol(1), ecol(4), ALU.mult)
            stt(ecol(8), ecol(1), 1.0 / 100.0, ecol(2), ALU.mult, ALU.mult)
            tt(edges_v, edges_v, cols(ecol(8)), ALU.mult)
            reset()
            segment_sums(ph, edges_v, 1)
            carry_in(ph, edges_v, 1, hyp_stage[0])

            ph = FIN

            def dots(it, s, c):
                wait(ph["load1"][s], it * 32 + 32)
                tt(products[s], sp_a[s], sp_b[s], ALU.mult)
                red(scol(1, c), products[s])
                wait(ph["sq0"], c + 1)
                red(scol(0, c), squares[s])
                done(ph["used1"])
                reset()
            steps(dve, NCHUNK, dots)
            root(ph, sc[2], sc[0], sc[3])
            ts(sc[2], sc[2], MIN_NORM, None, ALU.max)
            ts(sc[3], sc[11], -1.0, 1.0, ALU.mult, ALU.add)
            ts(sc[3], sc[3], MIN_NORM, None, ALU.max)
            recip(sc[3], sc[3])
            tt(sc[4], sc[2], sc[3], ALU.mult)
            ask(ph, "act")
            recip(sc[6], sc[2])
            tt(sc[6], sc[6], sc[5], ALU.mult)
            tt(sc[7], sc[6], sc[6], ALU.mult)
            tt(sc[7], sc[7], sc[0], ALU.mult)
            tt(sc[8], sc[6], sc[1], ALU.mult)
            ts(sc[8], sc[8], 2.0, 1.0, ALU.mult, ALU.add)
            tt(sc[9], sc[8], sc[7], ALU.add)
            tt(sc[10], sc[11], sc[7], ALU.mult)
            tt(sc[10], sc[10], sc[8], ALU.add)
            ts(sc[10], sc[10], MIN_NORM, None, ALU.max)
            recip(sc[10], sc[10])
            ts(sc[4], sc[11], -1.0, 1.0, ALU.mult, ALU.add)
            tt(sc[4], sc[4], sc[6], ALU.mult)
            tt(sc[4], sc[4], sc[10], ALU.mult)
            tt(sc[9], sc[9], sc[10], ALU.mult)
            reset()

            def combine(it, s, c, on):
                if on(0):
                    wait(ph["load2"][s], it * 32 + 32)
                    x = nchunk(c)
                    tt(x, sp_a[s], cols(scol(9, c)), ALU.mult, False)
                    tt(sp_t, sp_b[s], cols(scol(4, c)), ALU.mult)
                    done(ph["used2"])
                    tt(x, x, sp_t, ALU.add)
                    done(ph["x"])
                if on(1):
                    squares_sum("sq", 0, sum64)(s, c)
                reset()
            pipelined(dve, NCHUNK, 1, combine)
            root(ph, sc[2], sc[0], sc[6])
            ts(sc[2], sc[2], MIN_NORM, None, ALU.max)
            ts(sc[6], sc[2], MAXNORM, None, ALU.min)
            ask(ph, "act")
            artanh_ratio(sc[9], sc[6], sc[7], sc[8], sc[10], sc[5])
            tt(sc[9], sc[9], sc[6], ALU.mult)
            recip(sc[2], sc[2])
            tt(sc[9], sc[9], sc[2], ALU.mult)
            reset()

            def tangent(it, s, c, on):
                if on(0):
                    x = nchunk(c)
                    tt(x, x, cols(scol(9, c)), ALU.mult)
                    center(x, small[0:P, 0, :], CN)
                    done(ph["x"])
                if on(1):
                    squares_sum("sq", 1, red, NCHUNK)(s, c)
                reset()
            pipelined(dve, NCHUNK, 1, tangent)
            ts(sc[1], sc[1], 1.0 / D, 1e-5, ALU.mult, ALU.add)
            root(ph, sc[2], sc[1], sc[6])
            recip(sc[2], sc[2])
            reset()

            def normed(it, s, c, on):
                if on(0):
                    x = nchunk(c)
                    tt(x, x, cols(scol(2, c)), ALU.mult)
                    tt(x, x, rows_of(hyp_row["g"], CN), ALU.mult)
                    tt(x, x, rows_of(hyp_row["b"], CN), ALU.add)
                    done(ph["x"])
                if on(1):
                    squares_sum("sq", 0, red, 2 * NCHUNK)(s, c)
                    red(scol(1, c - 1), products[1 - s])
                reset()
            pipelined(dve, NCHUNK, 1, normed)
            root(ph, sc[2], sc[0], sc[6])
            root(ph, sc[3], sc[1], sc[6])
            ts(sc[2], sc[2], MIN_NORM, None, ALU.max)
            ask(ph, "act")
            ts(sc[6], sc[4], MAXNORM, MIN_NORM, ALU.min, ALU.max)
            ask(ph, "act")
            artanh_ratio(sc[9], sc[6], sc[7], sc[8], sc[10], sc[5])
            recip(sc[2], sc[2])
            tt(sc[9], sc[9], sc[6], ALU.mult)
            tt(sc[9], sc[9], sc[2], ALU.mult)
            tt(sc[3], sc[3], sc[9], ALU.mult)
            ts(sc[3], sc[3], MIN_NORM, None, ALU.max)
            ask(ph, "act")
            ts(sc[4], sc[4], MAXNORM, None, ALU.min)
            recip(sc[3], sc[3])
            tt(sc[9], sc[9], sc[4], ALU.mult)
            tt(sc[9], sc[9], sc[3], ALU.mult)
            reset()

            def add_x0(it, s, c, on):
                if on(0):
                    wait(ph["load3"][s], it * 16 + 16)
                    x = nchunk(c)
                    tt(x, x, cols(scol(9, c)), ALU.mult)
                    tt(x, x, sp_a[s], ALU.add)
                    done(ph["used3"])
                    center(x, small[0:P, 0, :], CN)
                    done(ph["x"])
                if on(1):
                    squares_sum("sq", 1, red, 3 * NCHUNK)(s, c)
                reset()
            pipelined(dve, NCHUNK, 1, add_x0)
            ts(sc[1], sc[1], 1.0 / D, 1e-5, ALU.mult, ALU.add)
            root(ph, sc[2], sc[1], sc[6])
            recip(sc[2], sc[2])
            reset()

            def output(it, s, c):
                wait(ph["store"][s], ph.upto("store", it * 16))
                tt(sp_b[s], nchunk(c), cols(scol(2, c)), ALU.mult)
                done(ph["rows"])
                reset()
            steps(dve, NCHUNK, output)


_INS = ["x", "src", "dst", "edge_weight", "edge_weight1",
        "L0_gnn_gat_W", "L0_gnn_gat_asrc", "L0_gnn_gat_adst", "L0_gnn_gat_bias", "L0_gnn_mlp_W1", "L0_gnn_mlp_b1",
        "L0_gnn_mlp_W2", "L0_gnn_mlp_b2", "L0_gnn_ln_g", "L0_gnn_ln_b", "L1_gnn_lin_W", "L1_gnn_bias", "L1_gnn_att_W1",
        "L1_gnn_att_b1", "L1_gnn_att_W2", "L1_gnn_att_b2", "L1_gnn_ln_g", "L1_gnn_ln_b"]


def kernel(**inputs):
    import numpy as np
    import concourse.bacc as bacc
    from concourse.bass_utils import run_bass_kernel_spmd

    nc = bacc.Bacc("TRN2", target_bir_lowering=False, num_devices=1)
    arrays, aps = {}, {}
    for name in _INS:
        arr = np.ascontiguousarray(inputs[name])
        arrays["in_" + name] = arr
        aps[name] = nc.dram_tensor("in_" + name, arr.shape, mybir.dt.from_np(arr.dtype), kind="ExternalInput").ap()
    out = nc.dram_tensor("out", (N, D), mybir.dt.float32, kind="ExternalOutput").ap()
    build(nc, aps, out)
    return run_bass_kernel_spmd(nc, [arrays], core_ids=[0]).results[0]["out"]
```

```python
import concourse.bass as bass
from concourse import mybir
from concourse.alu_op_type import AluOpType as ALU
from contextlib import ExitStack

N, E, D = 50000, 25000, 64
P = 125
TN, TE = N // P, E // P
L, R, H = 2, 4, 2
NCHUNK = 20
CE, CN = TE // NCHUNK, TN // NCHUNK
NTAB = TN // CE
ROW = D + 16
HROW = 2 * D + 1
RADIX = 256
DIGITS = (RADIX, (N - 1) // RADIX + 1)
BIG = 1e30
MAXNORM = 1.0 - 0.004
MIN_NORM = 1e-15
CLIP = 1.0 - 1e-7
GRP = 4
NGRP = TE // GRP
GROUPS = CN // GRP
REC = 5
SKIP = 1000000


def build(nc, a, out):
    fp32, i32, bf16 = mybir.dt.float32, mybir.dt.int32, mybir.dt.bfloat16
    ACT = mybir.ActivationFunctionType
    X = mybir.AxisListType.X
    ctx = ExitStack()
    with ctx:
        def sb(name, shape, dt=fp32):
            return ctx.enter_context(nc.sbuf_tensor(name, shape, dt))

        def sem(name):
            return ctx.enter_context(nc.semaphore(name))

        def dram(name, shape):
            return nc.dram_tensor(name, shape, fp32, kind="Internal").ap()

        rec_dram = dram("rec_dram", (E, REC))
        gat_table = [dram(f"gat_table{l}", (N, ROW)) for l in range(L)]
        h2_dram = dram("h2_dram", (N, D))
        pair_dram = dram("pair_dram", (E, ROW))
        corr_dram = [dram(f"corr_dram{d}", (N, D)) for d in range(2)]
        agg_dram = dram("agg_dram", (N, D))
        x0_dram = dram("x0_dram", (N, D))
        row_table = dram("row_table", (N, HROW))
        col_table = dram("col_table", (N, HROW))

        def by_part(t):
            return t.rearrange("(p t) w -> p (t w)", p=P)

        def chunk(t, c, width, cols):
            return by_part(t)[:, bass.ds(c * (cols * width), cols * width)]


        arena = sb("arena", [128, 2 * TE * ROW])

        def area(at, cols, width):
            return arena[0:P, at:at + cols * width].rearrange("p (t w) -> p t w", w=width)

        G = [area(d * TE * ROW, TE, ROW) for d in range(2)]
        nodes = area(0, TN, D)
        edges_v = area(0, TE, D)
        SPARE = TN * D
        pool_a = sb("pool_a", [128, 2 * CE * HROW])
        pool_b = sb("pool_b", [128, 2 * CE * HROW])

        def slot_of(pool, s, cols, width):
            return pool[0:P, s * CE * HROW:s * CE * HROW + cols * width].rearrange("p (t w) -> p t w", w=width)

        scratch = sb("scratch", [128, 12 * TN])
        att = [scratch[0:P, k * 4 * TE:(k + 1) * 4 * TE].rearrange("p (s t) -> p s t", s=4) for k in range(6)]
        sc = [scratch[0:P, k * TN:(k + 1) * TN] for k in range(12)]
        ident = sb("ident", [128, 128])
        ones = sb("ones", [128, 128])
        tri_lt = sb("tri_lt", [128, 128])
        tri_gt = sb("tri_gt", [128, 128])
        position_i = sb("position_i", [128, TE], i32)
        rec = scratch[:, 0:TE * REC]
        rec_v = rec[0:P, :].rearrange("p (t c) -> p t c", c=REC)
        total, cursor, matched, digits_row, digits_i = (scratch[:, TE * REC + k * RADIX:TE * REC + (k + 1) * RADIX] for k in range(5))
        digits_i = digits_i.bitcast(i32)
        digit, digit_i = (scratch[:, TE * REC + 6 * RADIX + k * TE:TE * REC + 6 * RADIX + (k + 1) * TE] for k in range(2))
        digit_i = digit_i.bitcast(i32)
        spare_bf = arena[:, 9000:16000].bitcast(bf16)
        one_hot = [[spare_bf[0:P, (s * CE + j) * RADIX:(s * CE + j + 1) * RADIX] for j in range(CE)] for s in range(2)]
        digits_bf, tri_bf, all_bf = (spare_bf[0:P, (2 * CE + k) * RADIX:(2 * CE + k + 1) * RADIX] for k in range(3))
        rank = sb("rank", [128, CE])
        rec_stage = sb("rec_stage", [128, 2, CE * REC])
        place_i = sb("place_i", [128, 2, CE], i32)
        idx_a = sb("idx_a", [128, 2, CE], i32)
        idx_b = sb("idx_b", [128, 2, CE], i32)
        src_i = [sb(f"src_i{o}", [128, TE], i32) for o in range(2)]
        dst_i = [sb(f"dst_i{o}", [128, TE], i32) for o in range(2)]
        out_i = [sb(f"out_i{o}", [128, TE], i32) for o in range(2)]
        pair_i = sb("pair_i", [128, TE], i32)
        keep = [sb(f"keep{o}", [128, TE]) for o in range(2)]
        keep_b = [sb(f"keep_b{o}", [128, TE]) for o in range(2)]
        first = [sb(f"first{o}", [128, TE]) for o in range(2)]
        last = [sb(f"last{o}", [128, TE]) for o in range(2)]
        off = [sb(f"off{o}", [128, 2, TE]) for o in range(2)]
        carry_f = [sb(f"carry_f{o}", [128, 128]) for o in range(2)]
        carry_b = [sb(f"carry_b{o}", [128, 128]) for o in range(2)]
        far_f = [sb(f"far_f{o}", [128, 128]) for o in range(2)]
        far_b = [sb(f"far_b{o}", [128, 128]) for o in range(2)]
        weight1 = sb("weight1", [128, TE])
        prod = sb("prod", [128, GRP * 4 * D])
        diag = prod[:, 0:4 * P].rearrange("p (s q) -> p s q", s=4)
        far = prod[:, 4 * P:8 * P].rearrange("p (s q) -> p s q", s=4)
        key_diag = prod[:, 0:256].rearrange("p (k q) -> p k q", k=2)
        grp_stage = prod[:, 0:2 * GRP * 2 * D].rearrange("p (s n) -> p s n", s=2)
        goes_on = sb("goes_on", [128, 1])
        seg_off = scratch[:, 5 * 4 * TE:6 * 4 * TE].rearrange("p (k t) -> p k t", k=4)
        carry4 = sb("carry4", [128, 4, 4])
        carry_v = sb("carry_v", [128, D])
        tr = sb("tr", [128, 2, GRP * P])
        proj_w = [sb(f"proj_w{l}", [128, 2 * 16]) for l in range(L)]
        edge_w = [sb(f"edge_w{l}", [128, 2, 2 * D]) for l in range(L)]
        dense_w = [sb(f"dense_w{l}", [128, 2 * D]) for l in range(L)]
        mlp_w2 = [sb(f"mlp_w2{l}", [128, 2 * D]) for l in range(L)]
        bias_parts = [[sb(f"bias{k}_parts{l}", [128, D], bf16) for k in range(2)] for l in range(L)]
        ones_bf = sb("ones_bf", [128, P], bf16)
        bias_rounded = sb("bias_rounded", [128, D], bf16)
        g_row = [sb(f"g_row{l}", [128, D]) for l in range(L)]
        be_row = [sb(f"be_row{l}", [128, D]) for l in range(L)]
        lin_t = sb("lin_t", [128, 2 * D])
        att_t = sb("att_t", [128, 4 * D])
        hyp_bias = sb("hyp_bias", [128, D])
        hyp_row = {k: sb(f"hyp_{k}", [128, D]) for k in ("b1", "w2", "g", "b", "wd", "wg")}
        att_b2 = sb("att_b2", [128, 1])
        power = sb("power", [128, 2])
        bias_sc = sb("bias_sc", [128, 16])
        part = sb("part", [128, CN * 8])
        small = sb("small", [128, 6, 2 * CE])
        raw_at = [16000]

        def raw(parts, n):
            raw_at[0] += n
            return arena[0:parts, raw_at[0] - n:raw_at[0]]

        w_raw = [raw(128, R * H * D) for l in range(L)]
        a_raw = [raw(128, 2 * R * H * D) for l in range(L)]
        w_prod = raw(128, R * H * D)
        w_red = raw(128, 2 * R * H)
        w1_edge = [raw(128, R * D) for l in range(L)]
        w1_top = [raw(128, D) for l in range(L)]
        w2_raw = [raw(128, D) for l in range(L)]
        w_t = [raw(128, R * 2 * D) for l in range(L)]
        gat_b = [raw(128, R) for l in range(L)]
        bias_raw = [[raw(128, D) for k in range(2)] for l in range(L)]
        bias_left = raw(128, D)
        bias_part = raw(128, D)
        lin_raw = raw(64, 2 * D)
        att_dup = raw(64, 4 * D)
        att_raw = raw(64, 2 * D + 2)
        zeros = raw(128, CN * D)
        ps = ctx.enter_context(nc.psum_tensor("ps", [128, 8 * 512], fp32))

        def bank(b, n=1):
            return ps[:, b * 512:(b + n) * 512]

        spacer = {k: sem(f"s_spacer_{k}") for k in ("sp", "act", "pool", "pe", "dve")}

        def hold(eng, who, s, value):
            if isinstance(value, int):
                if value > 0:
                    eng.wait_ge(s, value)
            else:
                eng.wait_ge(s, value)
                eng.sem_inc(spacer[who], 1)

        def steps(eng, n, body, at=0):
            if at == 0:
                for s in range(2):
                    body(0, s, s)
                at = 2
            with eng.Fori(at // 2, n // 2) as it:
                for s in range(2):
                    body(it, s, it * 2 + s)

        def pipelined(eng, n, depth, body, head=0):
            head = head or depth + depth % 2

            def peel(c):
                body(c // 2, c % 2, c, lambda k: 0 <= c - k < n)
            for c in range(head):
                peel(c)
            with eng.Fori(head // 2, n // 2) as it:
                for s in range(2):
                    body(it, s, it * 2 + s, lambda k: True)
            for c in range(n, n + depth):
                peel(c)

        def groups_by(c, s, lags, upto=-1):
            if isinstance(c, int):
                v = sum(GROUPS * min(max(c - k, 0), NCHUNK) for k in lags)
                v += sum(GROUPS for k in lags if k <= upto and 0 <= c - k < NCHUNK)
                return v, v % 2
            more = sum(1 for k in lags if k <= upto) - sum(lags)
            return c * (GROUPS * len(lags)) + GROUPS * more, (GROUPS * (len(lags) * s + more)) % 2

        class Signals(dict):
            run, per_run = 0, {}

            def upto(self, key, value):
                return self.run * self.per_run[key] + value if self.run else value

        def sems(name, names, slotted=()):
            made = Signals({k: sem(f"s_{name}_{k}") for k in names})
            made.update({k: [sem(f"s_{name}_{k}{s}") for s in range(2)] for k in slotted})
            return made

        def runs(made, n, per_run):
            out_ = []
            for k in range(n):
                ph = Signals(made)
                ph.run, ph.per_run = k, per_run
                out_.append(ph)
            return out_

        s_w = sem("s_weights_loaded")
        s_in = sem("s_edges_loaded")
        s_const = sem("s_constants")
        s_zeroed = sem("s_tables_zeroed")
        WP = sems("wprep", ("dve", "bias", "t", "tc", "mm", "act", "row"))
        TAB = sems("tab", ("tr", "trc", "mm", "rows"), ("load", "store"))
        SORT = runs(sems("sort", ("rec", "hist", "counted", "staged"), ("scattered",)), 4,
                    dict(rec=16, hist=NCHUNK, counted=NCHUNK, staged=NCHUNK, scattered=16 * TE // 2))
        ORD = runs(sems("order", ("diag", "bc", "done")), 2, dict(diag=1, bc=1, done=1))
        EDGE = runs(sems("edge", ("idx", "rows", "pair"), ("gathered", "permuted", "copied")), L,
                    dict(idx=3 * NCHUNK, rows=NCHUNK, pair=16 * NCHUNK, copied=16 * NCHUNK // 2, gathered=16 * TE, permuted=16 * TE // 2))
        att_runs = runs(sems("att", ("diag", "bc", "dve", "exp", "sums", "copied", "tr", "trc", "mm", "prod", "scan", "cv", "cvc", "carried", "places"),
                             ("staged", "scattered")), 2 * L,
                        dict(diag=3, bc=2, dve=1, exp=2, sums=1, copied=NGRP, tr=NGRP, trc=NGRP, mm=NGRP, prod=NGRP, scan=1, cv=1, cvc=1,
                             carried=1, places=NCHUNK, staged=16 * NCHUNK // 2, scattered=16 * TE // 2))
        ATT = [att_runs[2 * l:2 * l + 2] for l in range(L)]
        NODE = runs(sems("node", ("tr", "trc", "mm", "u", "th", "z", "zc", "sq", "var", "rstd", "h", "rows"), ("corr", "hin", "store")), L,
                    dict(tr=3 * GROUPS * NCHUNK, trc=3 * GROUPS * NCHUNK, mm=3 * GROUPS * NCHUNK, u=NCHUNK, th=NCHUNK, z=NCHUNK,
                         zc=NCHUNK, sq=NCHUNK, var=NCHUNK, rstd=NCHUNK, h=NCHUNK, rows=NCHUNK,
                         corr=16 * NCHUNK, hin=16 * NCHUNK // 2, store=16 * NCHUNK // 2))
        HYP = sems("hyp", ("act_asked", "act", "used", "r0", "sq", "x0", "y", "point", "psq", "copied", "pq", "tr", "trc", "mm", "x1", "rows"), ("load", "store", "store2"))
        HE = sems("hedge", ("idx", "rows", "v", "sq", "act_asked", "act", "pre", "gate", "scan", "cv", "cvc", "carried", "places"), ("gathered", "staged", "scattered"))
        FIN = sems("fin", ("act_asked", "act", "used1", "used2", "used3", "x", "sq", "sq0", "relu", "rows"), ("load1", "load2", "load3", "store"))
        s_link = sem("s_dve_link")
        block = ctx.enter_context(nc.Block())


        NCONST = 10
        SCORES_AT = GRP // 2 * P + P % 2
        NODE_LAGS = [(0, 1, 2), (0, 1)]
        V, A, T, GP = nc.vector, nc.scalar, nc.tensor, nc.gpsimd

        def cols(v, width=D):
            return v.unsqueeze(2).broadcast_to([P, v.shape[1], width])

        def rows_of(r, n):
            return r[0:P, :].unsqueeze(1).broadcast_to([P, n, D])

        def flat(v):
            return v.rearrange("p t w -> p (t w)")

        def chunk3(t, c, width, ncols):
            return chunk(t, c, width, ncols).rearrange("p (t w) -> p t w", w=width)

        def nchunk(c):
            return nodes[:, bass.ds(c * CN, CN), :]

        tab_rows = [area(s * CN * ROW, CN, ROW) for s in range(2)]
        n_h = [area((2 + s) * CN * ROW, CN, D) for s in range(2)]
        n_f, n_r, n_u, n_z, n_q = ([area(4 * CN * ROW + (2 * k + s) * CN * D, CN, D) for s in range(2)] for k in range(5))
        x_in = n_f
        sp_a = [area(SPARE + s * CN * D, CN, D) for s in range(2)]
        sp_b = [area(SPARE + (2 + s) * CN * D, CN, D) for s in range(2)]
        sp_t = area(SPARE + 4 * CN * D, CN, D)
        squares = [slot_of(pool_a, s, CN, D) for s in range(2)]
        products = [slot_of(pool_b, s, CN, D) for s in range(2)]
        hyp_r = [pool_a[0:P, 0:CN * HROW].rearrange("p (t w) -> p t w", w=HROW), area(SPARE, CN, HROW)]
        hyp_c = [pool_b[0:P, 0:CN * HROW].rearrange("p (t w) -> p t w", w=HROW), area(SPARE + CN * HROW, CN, HROW)]
        x_flat = [scratch[0:P, s * CN * D:(s + 1) * CN * D].rearrange("p (t w) -> p t w", w=D) for s in range(2)]
        edges_pre = area(TE * D, TE, D)
        g_src = [slot_of(pool_a, s, CE, ROW) for s in range(2)]
        g_dst = [slot_of(pool_b, s, CE, ROW) for s in range(2)]
        h_row = [slot_of(pool_a, s, CE, HROW) for s in range(2)]
        h_col = [slot_of(pool_b, s, CE, HROW) for s in range(2)]
        gat_stage = [slot_of(pool_b, s, CE, ROW) for s in range(2)]
        e_sq, e_tmp = ([area(SPARE + (2 + 2 * k + s) * CE * D, CE, D) for s in range(2)] for k in range(2))
        hyp_stage = [area(SPARE + s * CE * D, CE, D) for s in range(2)]
        perm = g_src
        trv = [tr[:, s, :] for s in range(2)]

        weight_loads = []

        def bc(v, n=128):
            return v.rearrange("(a n) -> a n", a=1).broadcast_to([n, v.shape[0]])

        for l in range(L):
            for half in (slice(0, 64), slice(64, 128)):
                weight_loads += [
                    (w_raw[l][half].rearrange("i (r c) -> i r c", r=R), a["L0_gnn_gat_W"][l].rearrange("r i c -> i r c")),
                    (w1_top[l][half], a["L0_gnn_mlp_W1"][l, 0:D, :]),
                    (w2_raw[l][half], a["L0_gnn_mlp_W2"][l])]
            for k, name in enumerate(("L0_gnn_gat_asrc", "L0_gnn_gat_adst")):
                weight_loads.append((a_raw[l][:, k * R * H * D:(k + 1) * R * H * D], bc(a[name][l].rearrange("r h c -> (r h c)"))))
            weight_loads += [
                (w1_edge[l].rearrange("p (r n) -> p r n", r=R), a["L0_gnn_mlp_W1"][l, D:, :].rearrange("(r p) n -> p r n", r=R)),
                *((gat_b[l][:, r:r + 1], a["L0_gnn_gat_bias"][l, r].rearrange("(p a) -> p a", a=1)) for r in range(R)),
                (bias_raw[l][0], bc(a["L0_gnn_mlp_b1"][l])),
                (bias_raw[l][1], bc(a["L0_gnn_mlp_b2"][l])),
                (g_row[l][:, :], bc(a["L0_gnn_ln_g"][l])),
                (be_row[l][:, :], bc(a["L0_gnn_ln_b"][l]))]
        weight_loads += [
            (lin_raw[:, 0:D], a["L1_gnn_lin_W"]), (lin_raw[:, D:2 * D], a["L1_gnn_lin_W"]), (att_raw, a["L1_gnn_att_W1"]),
            *((att_dup[:, k * D:(k + 1) * D], a["L1_gnn_att_W1"][:, (k // 2) * D:(k // 2 + 1) * D]) for k in range(4)),
            (hyp_bias[:, :], a["L1_gnn_bias"].broadcast_to([128, D])),
            (hyp_row["b1"][:, :], bc(a["L1_gnn_att_b1"])),
            (hyp_row["w2"][:, :], a["L1_gnn_att_W2"].broadcast_to([128, D])),
            (hyp_row["g"][:, :], bc(a["L1_gnn_ln_g"])), (hyp_row["b"][:, :], bc(a["L1_gnn_ln_b"])),
            (att_b2[:, :], bc(a["L1_gnn_att_b2"]))]
        NW = 16 * len(weight_loads)

        def sp_load_inputs(sp):
            for dst, name in ((dst_i[1][0:P, :], "dst"), (src_i[1][0:P, :], "src"), (off[0][0:P, 0, :], "edge_weight")):
                sp.dma_start(dst, a[name].rearrange("(p t) -> p t", p=P)).then_inc(s_in, 16)
            sp.dma_start(off[0][0:P, 1, :], a["edge_weight1"].rearrange("(p t) a -> p (t a)", p=P)).then_inc(s_in, 16)
            for dst, src in weight_loads:
                sp.dma_start(dst, src).then_inc(s_w, 16)

        def sp_zeros(sp, t):
            sp.wait_ge(s_const, NCONST)
            with sp.Fori(0, NCHUNK) as c:
                sp.dma_start(chunk(t, c, D, CN), zeros[0:P, :]).then_inc(s_zeroed, 16)

        def sp_table0(sp, at, n):
            def load(s, c):
                sp.dma_start(flat(x_in[s]), chunk(a["x"], c, D, CN)).then_inc(TAB["load"][s], 16)

            def store(s, c):
                hold(sp, "sp", TAB["rows"], c + 1)
                sp.dma_start(chunk(gat_table[0], c, ROW, CN), flat(tab_rows[s])).then_inc(TAB["store"][s], 16)

            if at == 0:
                for s in range(2):
                    load(s, s)
            with sp.Fori(at // 2, min(n, NCHUNK - 2) // 2) as it:
                for s in range(2):
                    store(s, it * 2 + s)
                    load(s, it * 2 + s + 2)
            if n == NCHUNK:
                for s in range(2):
                    store(s, NCHUNK - 2 + s)

        def sp_sort(sp, k):
            for s in range(2):
                sp.wait_ge(SORT[k]["scattered"][s], SORT[k].upto("scattered", 16 * TE // 2))
            sp.dma_start(rec[0:P, :], by_part(rec_dram)).then_inc(SORT[k]["rec"], 16)

        def sp_pairs(sp, l):
            with sp.Fori(0, NCHUNK) as c:
                hold(sp, "sp", EDGE[l]["rows"], EDGE[l].upto("rows", c + 1))
                sp.dma_start(chunk(pair_dram, c, ROW, CE), flat(G[0][:, bass.ds(c * CE, CE), :])).then_inc(EDGE[l]["pair"], 16)

        def sp_permuted(sp, l):
            ph = EDGE[l]

            def body(it, s, c):
                hold(sp, "sp", ph["permuted"][s], ph.upto("permuted", (it + 1) * (16 * CE)))
                sp.dma_start(flat(G[1][:, bass.ds(c * CE, CE), :]), flat(perm[s])).then_inc(ph["copied"][s], 16)
            steps(sp, NCHUNK, body)

        def sp_stage(sp, ph, v, stage):
            sp.wait_ge(ph["carried"], ph.upto("carried", 1))

            def body(it, s, c):
                hold(sp, "sp", ph["scattered"][s], ph.upto("scattered", it * (16 * CE)))
                sp.dma_start(flat(stage[s]), flat(v[:, bass.ds(c * CE, CE), :])).then_inc(ph["staged"][s], 16)
            steps(sp, NCHUNK, body)

        def sp_node(sp, l):
            ph = NODE[l]
            for d in range(2):
                for s in range(2):
                    sp.wait_ge(ATT[l][d]["scattered"][s], ATT[l][d].upto("scattered", 16 * TE // 2))

            def body(it, s, c, on):
                if on(0):
                    hold(sp, "sp", ph["u"], ph.upto("u", c - 1))
                    for d, to in enumerate((n_f, n_r)):
                        sp.dma_start(flat(to[s]), chunk(corr_dram[d], c, D, CN)).then_inc(ph["corr"][s], 16)
                    hold(sp, "sp", ph["z"], ph.upto("z", c - 1))
                    if l == 0:
                        sp.dma_start(flat(n_h[s]), chunk(a["x"], c, D, CN)).then_inc(ph["hin"][s], 16)
                    else:
                        sp.dma_start(n_h[s], chunk3(gat_table[l], c, ROW, CN)[:, :, 0:D]).then_inc(ph["hin"][s], 16)
                if l + 1 < L and on(4):
                    hold(sp, "sp", ph["rows"], ph.upto("rows", c - 3))
                    sp.dma_start(chunk(gat_table[l + 1], c - 4, ROW, CN), flat(tab_rows[s])).then_inc(ph["store"][s], 16)
                if l + 1 == L and on(3):
                    hold(sp, "sp", ph["rows"], ph.upto("rows", c - 2))
                    sp.dma_start(chunk(h2_dram, c - 3, D, CN), flat(n_z[1 - s])).then_inc(ph["store"][1 - s], 16)
            pipelined(sp, NCHUNK, 4, body)
            for s in range(2):
                sp.wait_ge(ph["store"][s], ph.upto("store", 16 * NCHUNK // 2))

        def sp_hyp(sp):
            ph = HYP

            def load(s, c):
                sp.dma_start(flat(sp_a[s]), chunk(h2_dram, c, D, CN)).then_inc(ph["load"][s], 16)
                sp.dma_start(flat(sp_b[s]), chunk(a["x"], c, D, CN)).then_inc(ph["load"][s], 16)

            for s in range(2):
                load(s, s)
            with sp.Fori(0, NCHUNK // 2 - 1) as it:
                for s in range(2):
                    hold(sp, "sp", ph["used"], ph.upto("used", it * 2 + s + 1))
                    load(s, it * 2 + s + 2)
            with sp.Fori(0, NCHUNK // 2) as it:
                for s in range(2):
                    hold(sp, "sp", ph["x0"], ph.upto("x0", it * 2 + s + 1))
                    sp.dma_start(chunk(x0_dram, it * 2 + s, D, CN), flat(sp_a[s])).then_inc(ph["store"][s], 16)
            with sp.Fori(0, NCHUNK // 2) as it:
                for s in range(2):
                    hold(sp, "sp", ph["rows"], ph.upto("rows", it * 2 + s + 1))
                    sp.dma_start(chunk(row_table, it * 2 + s, HROW, CN), flat(hyp_r[s])).then_inc(ph["store2"][s], 16)
                    sp.dma_start(chunk(col_table, it * 2 + s, HROW, CN), flat(hyp_c[s])).then_inc(ph["store2"][s], 16)

        def sp_final(sp):
            ph = FIN

            def pass_in(key, used, srcs):
                def load(s, c):
                    for to, t, w in srcs:
                        sp.dma_start(to[s], chunk3(t, c, w, CN)[:, :, 0:D]).then_inc(ph[key][s], 16)
                for s in range(2):
                    load(s, s)
                with sp.Fori(0, NCHUNK // 2 - 1) as it:
                    for s in range(2):
                        hold(sp, "sp", ph[used], it * 2 + s + 1)
                        load(s, it * 2 + s + 2)

            for s in range(2):
                sp.wait_ge(HE["scattered"][s], 16 * TE // 2)
            pu = ((sp_a, row_table, HROW), (sp_b, agg_dram, D))
            pass_in("load1", "used1", pu)
            sp.wait_ge(ph["used1"], ph.upto("used1", NCHUNK))
            pass_in("load2", "used2", pu)
            sp.wait_ge(ph["used2"], ph.upto("used2", NCHUNK))
            pass_in("load3", "used3", ((sp_a, x0_dram, D),))
            with sp.Fori(0, NCHUNK // 2) as it:
                for s in range(2):
                    hold(sp, "sp", ph["rows"], ph.upto("rows", it * 2 + s + 1))
                    sp.dma_start(chunk(out, it * 2 + s, D, CN), flat(sp_b[s])).then_inc(ph["store"][s], 16)
            for s in range(2):
                sp.wait_ge(ph["store"][s], ph.upto("store", 16 * NCHUNK // 2))

        @block.sync
        def _(sp):
            sp_load_inputs(sp)
            sp_table0(sp, 0, 12)
            sp_sort(sp, 0)
            sp_table0(sp, 12, NCHUNK)
            for k, t in enumerate((corr_dram[0], corr_dram[1], agg_dram)):
                sp_zeros(sp, t)
                sp_sort(sp, 1 + k)
            for l in range(L):
                sp_pairs(sp, l)
                sp_permuted(sp, l)
                for d in range(2):
                    sp_stage(sp, ATT[l][d], G[d], gat_stage)
                sp_node(sp, l)
            sp_hyp(sp)
            sp_stage(sp, HE, edges_v, hyp_stage)
            sp_final(sp)

        def pool_constants(gp):
            GP.memset(ones[:, :], 1.0).then_inc(s_const, 1)
            GP.memset(ident[:, :], 0.0).then_inc(s_const, 1)
            GP.memset(zeros[:, :], 0.0).then_inc(s_const, 1)
            GP.memset(power[:, 0:1], 0.5).then_inc(s_const, 1)
            GP.memset(power[:, 1:2], -0.5).then_inc(s_const, 1)
            gp.wait_ge(s_const, 5)
            GP.affine_select(out=ident[:, :], in_=ident[:, :], compare_op=ALU.not_equal, fill=1.0, base=0,
                             pattern=[[-1, 128]], channel_multiplier=1).then_inc(s_const, 1)
            GP.affine_select(out=tri_lt[:, :], in_=ones[:, :], compare_op=ALU.is_gt, fill=0.0, base=0,
                             pattern=[[1, 128]], channel_multiplier=-1).then_inc(s_const, 1)
            GP.affine_select(out=tri_gt[:, :], in_=ones[:, :], compare_op=ALU.is_gt, fill=0.0, base=0,
                             pattern=[[-1, 128]], channel_multiplier=1).then_inc(s_const, 1)
            GP.iota(digits_i[:, :], pattern=[[1, RADIX]], base=0, channel_multiplier=0).then_inc(s_const, 1)
            GP.iota(position_i[:, :], pattern=[[1, TE]], base=0, channel_multiplier=TE).then_inc(s_const, 1)

        def pool_sort(gp, k, limit):
            if k:
                gp.wait_ge(SORT[k - 1]["rec"], SORT[k - 1].upto("rec", 16))

            def body(it, s, c):
                hold(gp, "pool", SORT[k]["staged"], SORT[k].upto("staged", c + 1))
                for j in range(CE):
                    gp.indirect_dma_start(rec_dram, bass.IndirectOffsetOnAxis(ap=place_i[0:P, s, j:j + 1], axis=0),
                                          rec_stage[0:P, s, j * REC:(j + 1) * REC], None,
                                          bounds_check=limit, oob_is_err=False).then_inc(SORT[k]["scattered"][s], 16)
            steps(gp, NCHUNK, body)

        def pool_gather(gp, dst, table, idx, limit, signal):
            gp.indirect_dma_start(dst, None, table, bass.IndirectOffsetOnAxis(ap=idx, axis=0),
                                  bounds_check=limit, oob_is_err=False).then_inc(signal, 16)

        def pool_edges(gp, l, limit, limit_e):
            ph = EDGE[l]
            before = TAB if l == 0 else NODE[l - 1]
            gp.wait_ge(ORD[0]["done"], 1)
            for s in range(2):
                gp.wait_ge(before["store"][s], before.upto("store", 16 * NCHUNK // 2))

            pool_ends(gp, ph, 0, (g_src, gat_table[l]), (g_dst, gat_table[l]), limit)
            gp.wait_ge(ORD[1]["done"], 2)
            gp.wait_ge(ph["pair"], ph.upto("pair", 16 * NCHUNK))

            def pairs(it, s, c):
                hold(gp, "pool", ph["copied"][s], ph.upto("copied", it * 16))
                GP.tensor_copy(idx_a[0:P, s, :], pair_i[0:P, bass.ds(c * CE, CE)]).then_inc(ph["idx"], 1)
                hold(gp, "pool", ph["idx"], ph.upto("idx", 2 * NCHUNK + c + 1))
                for j in range(CE):
                    pool_gather(gp, perm[s][:, j, :], pair_dram, idx_a[0:P, s, j:j + 1], limit_e, ph["permuted"][s])
            steps(gp, NCHUNK, pairs)

        def pool_ends(gp, ph, order, row_end, col_end, limit):
            def ends(it, s, c):
                hold(gp, "pool", ph["rows"], ph.upto("rows", c - 1))
                GP.tensor_copy(idx_a[0:P, s, :], src_i[order][0:P, bass.ds(c * CE, CE)]).then_inc(ph["idx"], 1)
                GP.tensor_copy(idx_b[0:P, s, :], dst_i[order][0:P, bass.ds(c * CE, CE)]).then_inc(ph["idx"], 1)
                hold(gp, "pool", ph["idx"], ph.upto("idx", c * 2 + 2))
                for j in range(CE):
                    pool_gather(gp, row_end[0][s][:, j, :], row_end[1], idx_a[0:P, s, j:j + 1], limit, ph["gathered"][s])
                    pool_gather(gp, col_end[0][s][:, j, :], col_end[1], idx_b[0:P, s, j:j + 1], limit, ph["gathered"][s])
            steps(gp, NCHUNK, ends)

        def pool_scatter(gp, ph, table, o, stage, limit):
            def body(it, s, c):
                hold(gp, "pool", ph["scattered"][s], ph.upto("scattered", it * (16 * CE)))
                GP.tensor_copy(idx_b[0:P, s, :], out_i[o][0:P, bass.ds(c * CE, CE)]).then_inc(ph["places"], 1)
                hold(gp, "pool", ph["places"], ph.upto("places", c + 1))
                hold(gp, "pool", ph["staged"][s], ph.upto("staged", it * 16 + 16))
                for j in range(CE):
                    gp.indirect_dma_start(table, bass.IndirectOffsetOnAxis(ap=idx_b[0:P, s, j:j + 1], axis=0),
                                          stage[s][:, j, 0:D], None, bounds_check=limit, oob_is_err=False).then_inc(ph["scattered"][s], 16)
            steps(gp, NCHUNK, body)

        def pool_node(gp, l):
            ph = NODE[l]

            def body(it, s, c):
                hold(gp, "pool", ph["var"], ph.upto("var", c + 1))
                GP.tensor_tensor(small[0:P, 4 + s, :], small[0:P, 2 + s, :], power[0:P, 1:2].broadcast_to([P, CN]), ALU.pow).then_inc(ph["rstd"], 1)
            steps(gp, NCHUNK, body)

        @block.gpsimd
        def _(gp):
            pool_constants(gp)
            limit, limit_e = gp.to_reg(N - 1), gp.to_reg(E - 1)
            for k in range(4):
                pool_sort(gp, k, limit_e)
            gp.wait_ge(s_zeroed, 16 * 3 * NCHUNK)
            for l in range(L):
                pool_edges(gp, l, limit, limit_e)
                for d in range(2):
                    pool_scatter(gp, ATT[l][d], corr_dram[d], d, gat_stage, limit)
                pool_node(gp, l)
            for s in range(2):
                gp.wait_ge(HYP["store2"][s], 32 * NCHUNK // 2)

            pool_ends(gp, HE, 1, (h_row, row_table), (h_col, col_table), limit)
            pool_scatter(gp, HE, agg_dram, 1, hyp_stage, limit)

        def act_copy(dst, src):
            return A.activation(dst, src, ACT.Copy)

        def act_weights(act):
            for l in range(L):
                act.wait_ge(WP["t"], l + 1)
                for k in range(2):
                    t = act_copy(w_t[l].rearrange("c (r k i) -> c r k i", r=R, k=2)[:, :, k, :], bank(0)[:, 0:R * D].rearrange("c (r i) -> c r i", r=R))
                t.then_inc(WP["tc"], 1)
                act.wait_ge(WP["mm"], l + 1)
                for g in range(2):
                    half = slice(g * D, (g + 1) * D)
                    for h in range(H):
                        act_copy(edge_w[l][half, :, h * D:(h + 1) * D],
                                 bank((1, 4)[h])[half, g * 2 * D:(g + 1) * 2 * D].rearrange("i (d n) -> i d n", d=2))
                    t = act_copy(dense_w[l][half, g * D:(g + 1) * D], bank(2)[half, 0:D])
                t.then_inc(WP["act"], 1)
            act.wait_ge(WP["mm"], L + 1)
            for g in range(2):
                half = slice(g * D, (g + 1) * D)
                act_copy(lin_t[half, g * D:(g + 1) * D], bank(0)[half, 0:D])
                act_copy(att_t[half, g * 2 * D:(g + 1) * 2 * D], bank(0)[half, D:3 * D])
            act_copy(hyp_row["wd"][:, :], bank(0)[:, 3 * D:4 * D])
            act_copy(hyp_row["wg"][:, :], bank(0)[:, 4 * D:5 * D]).then_inc(WP["act"], 1)

        def act_groups(act, ph, base, parity, n):
            for j in range(n):
                b = (parity + j) % 2
                hold(act, "act", ph["mm"], ph.upto("mm", base + j - 1))
                hold(act, "act", ph["tr"], ph.upto("tr", base + j + 1))
                act_copy(trv[b][:, 0:GRP // 2 * P], bank(b)[:, 0:GRP // 2 * P]).then_inc(ph["trc"], 1)

        def act_table0(act):
            def body(it, s, c):
                act_groups(act, TAB, c * GROUPS, s * GROUPS, GROUPS)
                hold(act, "act", TAB["store"][s], it * 16)
                act_copy(tab_rows[s][:, :, 0:D], x_in[s])
                hold(act, "act", TAB["mm"], (c + 1) * GROUPS)
                act_copy(tab_rows[s][:, :, D:ROW], bank(5)[0:P, 0:CN * 16].rearrange("p (t w) -> p t w", w=16)).then_inc(TAB["rows"], 1)
            steps(act, NCHUNK, body)

        def act_attention(act, l, d):
            ph = ATT[l][d]
            Es, Sf, F, B, mx, pp = att
            act.wait_ge(ph["dve"], ph.upto("dve", 1))
            A.activation(pp, F, ACT.Exp)
            A.activation(Sf, B, ACT.Exp).then_inc(ph["exp"], 1)
            act.wait_ge(ph["sums"], ph.upto("sums", 1))
            act_copy(carry4[0:P, 2:4, :], bank(7)[0:P, 0:8].rearrange("p (k s) -> p k s", k=2)).then_inc(ph["exp"], 1)

            def group(it, s, g, on):
                if on(1):
                    hold(act, "act", ph["mm"], ph.upto("mm", g - 2))
                    hold(act, "act", ph["tr"], ph.upto("tr", g))
                    act_copy(trv[1 - s], bank(1 - s)[:, 0:GRP * P]).then_inc(ph["trc"], 1)
            pipelined(act, NGRP, 1, group, head=4)
            act_carry(act, ph)

        def act_carry(act, ph):
            act.wait_ge(ph["cv"], ph.upto("cv", 1))
            act_copy(carry_v[0:P, :], bank(7)[0:P, 64:64 + D]).then_inc(ph["cvc"], 1)

        def act_node(act, l):
            ph, lags = NODE[l], NODE_LAGS[l]

            def copies(c, s, k):
                act_groups(act, ph, *groups_by(c, s, lags, k - 1), GROUPS)

            def body(it, s, c, on):
                if on(1):
                    hold(act, "act", ph["u"], ph.upto("u", c))
                    A.activation(n_u[1 - s], n_u[1 - s], ACT.Tanh).then_inc(ph["th"], 1)
                if on(0):
                    copies(c, s, 0)
                if on(1):
                    copies(c, s, 1)
                if l + 1 < L and on(2):
                    hold(act, "act", ph["store"][s], ph.upto("store", (it - 1) * 16))
                    hold(act, "act", ph["h"], ph.upto("h", c - 1))
                    act_copy(tab_rows[s][:, :, 0:D], n_z[s])
                    copies(c, s, 2)
                    hold(act, "act", ph["mm"], ph.upto("mm", groups_by(c, s, lags, 2)[0]))
                    parity = groups_by(c, s, lags, 1)[1]
                    for k in range(2):
                        mine = range(k, GROUPS, 2)
                        at = (parity + k) % 2 * 512 + SCORES_AT
                        t = act_copy(tab_rows[s][:, :, D:ROW].rearrange("p (j t) w -> p j t w", t=GRP)[:, k::2],
                                     ps[0:P, at:at + len(mine) * GRP * 16].rearrange("p (j t w) -> p j t w", t=GRP, w=16))
                    t.then_inc(ph["rows"], 1)
                if on(1):
                    hold(act, "act", ph["zc"], ph.upto("zc", c))
                    A.activation(n_q[1 - s], n_z[1 - s], ACT.Square).then_inc(ph["sq"], 1)
            pipelined(act, NCHUNK, 2 if l + 1 < L else 1, body, head=4)

        def act_square(act, ph, asked, told, value, out_, in_):
            hold(act, "act", ph[asked], value)
            A.activation(out_, in_, ACT.Square).then_inc(ph[told], 1)

        def act_square_in(act, it, s, c):
            hold(act, "act", FIN["load1"][s], it * 32 + 32)
            hold(act, "act", FIN["used1"], c - 1)
            A.activation(squares[s], sp_b[s], ACT.Square).then_inc(FIN["sq0"], 1)

        def act_logs(act, ph, n, c_, lp, lm):
            act.wait_ge(ph["act_asked"], ph.upto("act_asked", n + 1))
            A.activation(lp, c_, ACT.Ln, bias=1.0)
            A.activation(lm, c_, ACT.Ln, bias=1.0, scale=-1.0).then_inc(ph["act"], 1)

        def act_fn(act, ph, n, out_, in_, fn, **kw):
            act.wait_ge(ph["act_asked"], ph.upto("act_asked", n + 1))
            A.activation(out_, in_, fn, **kw).then_inc(ph["act"], 1)


        @block.scalar
        def _(act):
            act_weights(act)
            act_table0(act)
            for l in range(L):
                for d in range(2):
                    act_attention(act, l, d)
                act_node(act, l)
            act_fn(act, HYP, 0, bias_sc[0:P, 1:2], bias_sc[0:P, 5:6], ACT.Sqrt)
            act_fn(act, HYP, 1, bias_sc[0:P, 2:3], bias_sc[0:P, 1:2], ACT.Tanh)
            steps(act, NCHUNK, lambda it, s, c: act_square(act, HYP, "r0", "sq", c + 1, squares[s], nchunk(c)))
            act_fn(act, HYP, 2, sc[3], sc[4], ACT.Sqrt)
            act_fn(act, HYP, 3, sc[5], sc[6], ACT.Sqrt)
            act_logs(act, HYP, 4, sc[6], sc[7], sc[8])

            def linear(it, s, c):
                act_groups(act, HYP, c * GROUPS, s * GROUPS, GROUPS)
                hold(act, "act", HYP["mm"], (c + 1) * GROUPS)
                y = bank(2 + 3 * s, 3)[0:P, 0:CN * D].rearrange("p (t w) -> p t w", w=D)
                act_copy(nchunk(c), y)
                A.activation(squares[s], y, ACT.Square).then_inc(HYP["y"], 1)
            steps(act, NCHUNK, linear)
            act_fn(act, HYP, 5, sc[4], sc[5], ACT.Sqrt)
            act_fn(act, HYP, 6, sc[6], sc[5], ACT.Tanh)
            steps(act, NCHUNK, lambda it, s, c: act_square(act, HYP, "point", "psq", c + 1, squares[s], nchunk(c)))
            act_fn(act, HYP, 7, sc[1], sc[6], ACT.Sqrt)
            act_logs(act, HYP, 8, sc[6], sc[7], sc[8])
            act.wait_ge(HYP["act_asked"], 10)

            def tables(it, s, c):
                hold(act, "act", HYP["pq"], c - 1)
                act_copy(x_flat[s], nchunk(c)).then_inc(HYP["x1"], 1)
                act_groups(act, HYP, c * GROUPS + NCHUNK * GROUPS, s * GROUPS, GROUPS)
                hold(act, "act", HYP["store2"][s], it * 32)
                act_copy(hyp_r[s][:, :, 0:D], nchunk(c))
                act_copy(hyp_c[s][:, :, 0:D], nchunk(c))
                for t in (hyp_r[s], hyp_c[s]):
                    last_ = act_copy(t[:, :, 2 * D], sc[11][:, bass.ds(c * CN, CN)])
                last_.then_inc(HYP["copied"], 1)
            steps(act, NCHUNK, tables)
            steps(act, NCHUNK, lambda it, s, c: act_square(act, HE, "v", "sq", c + 1, e_sq[s], edges_v[:, bass.ds(c * CE, CE), :]))
            act_fn(act, HE, 0, sc[5][:, 0:TE], sc[6][:, 0:TE], ACT.Sqrt)
            act_logs(act, HE, 1, sc[6][:, 0:TE], sc[7][:, 0:TE], sc[8][:, 0:TE])

            def gate(it, s, c):
                hold(act, "act", HE["pre"], c + 1)
                A.activation(hyp_stage[s], edges_pre[:, bass.ds(c * CE, CE), :], ACT.Sigmoid).then_inc(HE["gate"], 1)
            steps(act, NCHUNK, gate)
            act_fn(act, HE, 2, sc[2][:, 0:TE], sc[0][:, 0:TE], ACT.Sigmoid, bias=att_b2[0:P, :])
            act_carry(act, HE)
            steps(act, NCHUNK, lambda it, s, c: act_square_in(act, it, s, c))
            act_fn(act, FIN, 0, sc[2], sc[3], ACT.Sqrt)
            act_fn(act, FIN, 1, sc[5], sc[4], ACT.Tanh)
            steps(act, NCHUNK, lambda it, s, c: act_square(act, FIN, "x", "sq", c + 1, squares[s], nchunk(c)))
            act_fn(act, FIN, 2, sc[2], sc[6], ACT.Sqrt)
            act_logs(act, FIN, 3, sc[6], sc[7], sc[8])
            steps(act, NCHUNK, lambda it, s, c: act_square(act, FIN, "x", "sq", c + 1 + NCHUNK, squares[s], nchunk(c)))

            act_fn(act, FIN, 4, sc[2], sc[6], ACT.Sqrt)

            def relu(it, s, c):
                hold(act, "act", FIN["x"], c + 1 + 2 * NCHUNK)
                A.activation(squares[s], nchunk(c), ACT.Square)
                A.activation(nchunk(c), nchunk(c), ACT.Relu).then_inc(FIN["relu"], 1)
                hold(act, "act", FIN["relu"], c + 1)
                A.activation(products[s], nchunk(c), ACT.Square).then_inc(FIN["sq"], 1)
            steps(act, NCHUNK, relu)
            act_fn(act, FIN, 5, sc[2], sc[6], ACT.Sqrt)
            act_fn(act, FIN, 6, sc[3], sc[6], ACT.Sqrt)
            act_fn(act, FIN, 7, sc[4], sc[2], ACT.Tanh)
            act_logs(act, FIN, 8, sc[6], sc[7], sc[8])
            act_fn(act, FIN, 9, sc[4], sc[3], ACT.Tanh)
            steps(act, NCHUNK, lambda it, s, c: act_square(act, FIN, "x", "sq", c + 1 + 3 * NCHUNK, squares[s], nchunk(c)))
            act_fn(act, FIN, 10, sc[2], sc[6], ACT.Sqrt)

        def mm(out_, w, x, start=True, stop=True):
            return T.matmul(out_, w, x, start=start, stop=stop)

        def pe_weights(pe):
            pe.wait_ge(s_w, NW)
            pe.wait_ge(s_const, NCONST)
            for l in range(L):
                if l:
                    pe.wait_ge(WP["act"], l)
                for r in range(R):
                    t = T.transpose(bank(0)[:, r * D:(r + 1) * D], w_raw[l][0:64, r * H * D:(r + 1) * H * D], ident[0:64, 0:64])
                t.then_inc(WP["t"], 1)
                pe.wait_ge(WP["tc"], l + 1)
                for r in range(R):
                    for h in range(H):
                        mm(bank((1, 4)[h])[:, r * D:(r + 1) * D], w_t[l][h * D:(h + 1) * D, r * 2 * D:(r + 1) * 2 * D],
                           w1_edge[l][h * D:(h + 1) * D, r * D:(r + 1) * D])
                for r in range(R):
                    mm(bank(2)[:, 0:D], w_t[l][:, r * 2 * D:(r + 1) * 2 * D], w1_edge[l][:, r * D:(r + 1) * D], start=(r == 0), stop=False)
                mm(bank(2)[:, 0:D], ident[:, :], w1_top[l], start=False)
                for r in range(R):
                    t = mm(bank(3)[:, 0:D], gat_b[l][:, r:r + 1].broadcast_to([128, 128]), w1_edge[l][:, r * D:(r + 1) * D],
                           start=(r == 0), stop=(r == R - 1))
                t.then_inc(WP["mm"], 1)
                pe.wait_ge(WP["row"], l + 1)
            pe.wait_ge(WP["act"], L)
            T.transpose(bank(0)[:, 0:D], lin_raw, ident[0:64, 0:64])
            for k in range(2):
                T.transpose(bank(0)[:, (1 + k) * D:(2 + k) * D], att_dup[:, k * 2 * D:(k + 1) * 2 * D], ident[0:64, 0:64])
            for k in range(2):
                t = mm(bank(0)[:, (3 + k) * D:(4 + k) * D], att_raw[:, 2 * D + k:2 * D + k + 1].broadcast_to([64, 128]), ident[0:64, 0:64])
            t.then_inc(WP["mm"], 1)
            pe.wait_ge(WP["act"], L + 1)

        def pe_transposes(pe, ph, b, value, n, tile):
            hold(pe, "pe", ph["trc"], ph.upto("trc", value - 1))
            for i in range(n):
                t = T.transpose(bank(b)[:, i * P:(i + 1) * P], tile(i), ident[0:P, 0:P])
            t.then_inc(ph["tr"], 1)

        def pe_groups(pe, ph, base, parity, n, tiles, w, out_, start=True, free=None):
            pairs = GRP // 2

            def products(j):
                hold(pe, "pe", ph["trc"], ph.upto("trc", base + j + 1))
                b = (parity + j) % 2
                for i in range(pairs):
                    k = j * pairs + i
                    full = (k + 1) * w.shape[1] % 512 == 0 or k == n * pairs - 1
                    t = mm(out_(k), trv[b][:, i * P:(i + 1) * P], w[:, :], start=start, stop=start or full)
                t.then_inc(ph["mm"], 1)
            for j in range(n):
                pe_transposes(pe, ph, (parity + j) % 2, base + j, pairs, lambda i: tiles(2 * (j * pairs + i)))
                if j == 1 and free:
                    free()
                if j:
                    products(j - 1)
            products(n - 1)

        def pair_of(v, t):
            return v[:, t:t + 2, :].rearrange("p t w -> p (t w)")

        def pe_bias(b, parts):
            for k in range(b, b + 3):
                n = min(512, CN * D - (k - b) * 512)
                mm(bank(k)[0:P, 0:n].rearrange("p (t w) -> p t w", w=D), ones_bf[:, 0:P],
                   parts[:, :].unsqueeze(1).broadcast_to([128, n // D, D]), stop=False)

        def out_tile(b, width):
            return lambda k: ps[0:P, b * 512 + k * 2 * width:b * 512 + (k + 1) * 2 * width]

        def pe_table0(pe, at, n):
            def body(it, s, c):
                hold(pe, "pe", TAB["load"][s], it * 16 + 16)
                hold(pe, "pe", TAB["rows"], c)
                pe_groups(pe, TAB, c * GROUPS, s * GROUPS, GROUPS, lambda t: pair_of(x_in[s], t), proj_w[0], out_tile(5, 16))
            steps(pe, n, body, at)

        def pe_sort(pe, k):
            ph, n = SORT[k], DIGITS[k % 2]
            if k == 0:
                pe.wait_ge(s_const, NCONST)

            def count(it, s, c, start=False, stop=False):
                hold(pe, "pe", ph["hist"], ph.upto("hist", c + 1))
                for j in range(CE):
                    ends = dict(start=start and j == 0, stop=stop and j == CE - 1)
                    mm(bank(7)[0:P, 0:n], tri_bf[:, 0:P], one_hot[s][j][:, 0:n], **ends)
                    t = mm(bank(6)[0:P, 0:n], all_bf[:, 0:P], one_hot[s][j][:, 0:n], **ends)
                t.then_inc(ph["counted"], 1)
            for s in range(2):
                count(0, s, s, start=s == 0)
            with pe.Fori(1, NCHUNK // 2 - 1) as it:
                for s in range(2):
                    count(it, s, it * 2 + s)
            for s in range(2):
                count(NCHUNK // 2 - 1, s, NCHUNK - 2 + s, stop=s == 1)

        def pe_order(pe, o):
            pe.wait_ge(ORD[o]["diag"], ORD[o].upto("diag", 1))
            for k in range(2):
                t = mm(bank(7)[0:P, k * 128:k * 128 + P], ones[0:P, 0:P], key_diag[0:P, k, 0:P])
            t.then_inc(ORD[o]["bc"], 1)

        def pe_carry(pe, ph, o, v_last):
            pe.wait_ge(ph["scan"], ph.upto("scan", 1))
            mm(bank(7)[0:P, 64:64 + D], carry_f[o][0:P, 0:P], v_last).then_inc(ph["cv"], 1)

        def pe_attention(pe, l, d):
            ph = ATT[l][d]
            for k in range(2):
                pe.wait_ge(ph["diag"], ph.upto("diag", k + 1))
                mm(bank(6)[0:P, 0:4 * P], ones[0:P, 0:P], diag[0:P, :, :].rearrange("p s q -> p (s q)")).then_inc(ph["bc"], 1)
            pe.wait_ge(ph["diag"], ph.upto("diag", 3))
            mm(bank(7)[0:P, 0:4], carry_f[d][0:P, 0:P], att[2][:, :, TE - 1])
            mm(bank(7)[0:P, 4:8], carry_b[d][0:P, 0:P], att[3][:, :, 0]).then_inc(ph["sums"], 1)

            def group(it, s, g, on):
                if on(0):
                    hold(pe, "pe", ph["copied"], ph.upto("copied", g + 1))
                    pe_transposes(pe, ph, s, g, GRP, lambda i: grp_stage[0:P, s, i * 2 * D:(i + 1) * 2 * D])
                if on(1):
                    hold(pe, "pe", ph["trc"], ph.upto("trc", g))
                    hold(pe, "pe", ph["prod"], ph.upto("prod", g - 2))
                    for i in range(GRP):
                        t = mm(bank(2 + (1 - s))[0:P, i * 2 * D:(i + 1) * 2 * D], trv[1 - s][:, i * P:(i + 1) * P], edge_w[l][:, d, :])
                    t.then_inc(ph["mm"], 1)
            pipelined(pe, NGRP, 1, group, head=4)
            pe_carry(pe, ph, d, G[d][:, TE - 1, 0:D])

        def pe_node(pe, l):
            ph, lags = NODE[l], NODE_LAGS[l]

            def body(it, s, c, on):
                def groups(k, tiles, w, out_, start=False):
                    pe_groups(pe, ph, *groups_by(c, s, lags, k - 1), GROUPS, tiles, w, out_, start)
                if on(0):
                    if l + 1 < L:
                        hold(pe, "pe", ph["rows"], ph.upto("rows", c - 2))
                    hold(pe, "pe", ph["hin"][s], ph.upto("hin", it * 16 + 16))
                    hold(pe, "pe", ph["u"], ph.upto("u", c))
                    pe_bias(2, bias_parts[l][0])
                    groups(0, lambda t: pair_of(n_h[s], t), dense_w[l], out_tile(2, D))
                if on(1):
                    hold(pe, "pe", ph["th"], ph.upto("th", c))
                    hold(pe, "pe", ph["z"], ph.upto("z", c - 1))
                    pe_bias(5, bias_parts[l][1])
                    groups(1, lambda t: pair_of(n_u[1 - s], t), mlp_w2[l], out_tile(5, D))
                if l + 1 < L and on(2):
                    hold(pe, "pe", ph["h"], ph.upto("h", c - 1))
                    hold(pe, "pe", ph["rows"], ph.upto("rows", c - 2))
                    parity = groups_by(c, s, lags, 1)[1]

                    def scores(k):
                        j, i = k // (GRP // 2), k % (GRP // 2)
                        at = (parity + j) % 2 * 512 + SCORES_AT + (j // 2 * GRP + 2 * i) * 16
                        return ps[0:P, at:at + 32]
                    groups(2, lambda t: pair_of(n_z[s], t), proj_w[l + 1], scores, True)
            pipelined(pe, NCHUNK, 2 if l + 1 < L else 1, body, head=4)

        def pe_hyp(pe):
            ph = HYP

            def lin(it, s, c):
                hold(pe, "pe", ph["x0"], c + 1)
                hold(pe, "pe", ph["y"], c - 1)
                pe_groups(pe, ph, c * GROUPS, s * GROUPS, GROUPS, lambda t: pair_of(sp_a[s], t), lin_t, out_tile(2 + 3 * s, D))
            steps(pe, NCHUNK, lin)

            def mlp(it, s, c):
                hold(pe, "pe", ph["x1"], c + 1)
                pe_groups(pe, ph, c * GROUPS + NCHUNK * GROUPS, s * GROUPS, GROUPS, lambda t: pair_of(x_flat[s], t), att_t, out_tile(2, 2 * D),
                          free=lambda: hold(pe, "pe", ph["pq"], c))
            steps(pe, NCHUNK, mlp)

        @block.tensor
        def _(pe):
            pe_sort(pe, 0)
            pe_weights(pe)
            pe.wait_ge(WP["dve"], 1)
            pe.wait_ge(WP["bias"], 1)
            pe_table0(pe, 0, 12)
            pe_sort(pe, 1)
            pe_table0(pe, 12, NCHUNK)
            pe_order(pe, 0)
            pe_sort(pe, 2)
            pe_sort(pe, 3)
            pe_order(pe, 1)
            for l in range(L):
                for d in range(2):
                    pe_attention(pe, l, d)
                pe_node(pe, l)
            pe_hyp(pe)
            pe_carry(pe, HE, 1, edges_v[:, TE - 1, :])

        @block.vector
        def _(dve):
            chain = [0]

            def link(ins, wait=True):
                chain[0] += 1
                ins.then_inc(s_link, 1)
                if wait:
                    dve.wait_ge(s_link, chain[0])

            def reset():
                if chain[0]:
                    dve.wait_ge(s_link, chain[0])
                    dve.sem_clear(s_link)
                    chain[0] = 0

            def done(s):
                if chain[0]:
                    dve.wait_ge(s_link, chain[0])
                dve.sem_inc(s, 1)

            def wait(s, v):
                hold(dve, "dve", s, v)

            def tt(o, x, y, op, w=True):
                link(V.tensor_tensor(o, x, y, op), w)

            def ts(o, x, s1, s2, op0, op1=None, w=True):
                link(V.tensor_scalar(o, x, s1, s2, op0, op1) if op1 is not None else V.tensor_scalar(o, x, s1, None, op0), w)

            def stt(o, x, s, y, op0, op1, w=True):
                link(V.scalar_tensor_tensor(o, x, s, y, op0, op1), w)

            def red(o, x, op=ALU.add, w=True):
                link(V.tensor_reduce(o, x, X, op), w)

            def copy(o, x, w=True):
                link(V.tensor_copy(o, x), w)

            def recip(o, x):
                link(V.reciprocal(o, x))

            def center(x, mean, n):
                red(mean, x)
                ts(mean, mean, -1.0 / D, None, ALU.mult)
                tt(x, x, cols(mean), ALU.add)

            def dot(o, x, y, tmp):
                tt(tmp, x, y, ALU.mult)
                sum64(o, tmp)

            def sum64(o, x):
                n = x.shape[1]
                red(part[0:P, 0:n * 8], x.rearrange("p t (a b) -> p t a b", a=8))
                red(o, part[0:P, 0:n * 8].rearrange("p (t a) -> p t a", a=8))

            asked = {}

            def ask(ph, who):
                key = (id(ph), who)
                asked[key] = asked.get(key, 0) + 1
                done(ph[who + "_asked"])
                dve.wait_ge(ph[who], asked[key])

            def root(ph, o, x, t):
                ts(t, x, 1e-34, None, ALU.max)
                ask(ph, "act")
                ts(o, o, 1e-19, None, ALU.max)
                recip(t, o)
                tt(t, t, x, ALU.mult)
                tt(o, o, t, ALU.add)
                ts(o, o, 0.5, None, ALU.mult)

            def artanh_ratio(o, c, lp, lm, t1, t2):
                tt(t1, c, c, ALU.mult)
                ts(o, t1, 1.0 / 13, None, ALU.mult)
                for k in (11, 9, 7, 5, 3):
                    stt(o, o, 1.0 / k, t1, ALU.add, ALU.mult)
                ts(o, o, 1.0, None, ALU.add)
                tt(t2, lp, lm, ALU.subtract)
                recip(t1, c)
                stt(t2, t2, 0.5, t1, ALU.mult, ALU.mult)
                ts(t1, c, 0.25, None, ALU.is_lt)
                tt(o, o, t2, ALU.subtract)
                tt(o, o, t1, ALU.mult)
                tt(o, o, t2, ALU.add)

            dve.wait_ge(s_in, 64)
            dve.wait_ge(s_const, NCONST)
            copy(digits_row[:, :], digits_i[:, :], False)
            copy(digits_bf, digits_i[0:P, :], False)
            copy(tri_bf[:, 0:P], tri_lt[0:P, 0:P], False)
            copy(all_bf[:, 0:P], ones[0:P, 0:P], False)
            for k in range(2):
                copy(rec_v[:, :, k], (dst_i, src_i)[k][1][0:P, :], False)
                copy(rec_v[:, :, 2 + k], off[0][0:P, k, :], False)
            copy(rec_v[:, :, 4], position_i[0:P, :])

            def weights():
                for w in (*proj_w, *dense_w, *mlp_w2, lin_t, att_t):
                    n = w.shape[1] // 2
                    link(V.memset(w[0:64, n:2 * n], 0.0), False)
                    link(V.memset(w[64:128, 0:n], 0.0), False)
                link(V.memset(ones_bf[:, :], 1.0), False)
                for l in range(L):
                    for k in range(2):
                        link(V.memset(bias_parts[l][k][:, :], 0.0), False)
                dve.wait_ge(s_w, NW)
                for l in range(L):
                    for k in range(2):
                        tt(w_prod, w_raw[l], a_raw[l][:, k * R * H * D:(k + 1) * R * H * D], ALU.mult)
                        red(w_red[:, k * R * H:(k + 1) * R * H], w_prod.rearrange("i (r c) -> i r c", c=D))
                    for g in range(2):
                        half = slice(g * D, (g + 1) * D)
                        for k in range(2):
                            for d in range(2):
                                at = g * 16 + k * 8 + d * 4
                                copy(proj_w[l][half, at:at + 4].rearrange("i (g h) -> i g h", g=2),
                                     w_red[half, k * 8:(k + 1) * 8].rearrange("i (g d h) -> i g d h", g=2, d=2)[:, :, d, :])
                        copy(mlp_w2[l][half, g * D:(g + 1) * D], w2_raw[l][half, :])
                done(WP["dve"])
                for l in range(L):
                    dve.wait_ge(WP["mm"], l + 1)
                    tt(bias_raw[l][0], bias_raw[l][0], bank(3)[:, 0:D], ALU.add)
                    done(WP["row"])
                    for k in range(2):
                        left, parts = bias_raw[l][k], bias_parts[l][k]
                        for row in (0, 32, 64):
                            copy(parts[row:row + 1, :], left[row:row + 1, :])
                            copy(bias_rounded[:, :], left)
                            copy(bias_part, bias_rounded[:, :])
                            tt(bias_left, left, bias_part, ALU.subtract)
                            copy(left, bias_left)
                done(WP["bias"])
                reset()

            def sort_pass(k):
                ph = SORT[k]
                key, high = k // 2, k % 2
                n = DIGITS[high]
                if k:
                    dve.wait_ge(SORT[k - 1]["rec"], SORT[k - 1].upto("rec", 16))
                copy(digit_i[0:P, :], rec_v[:, :, key])
                if high:
                    ts(digit_i[0:P, :], digit_i[0:P, :], 8, None, ALU.logical_shift_right)
                else:
                    ts(digit_i[0:P, :], digit_i[0:P, :], RADIX - 1, None, ALU.bitwise_and)
                copy(digit[0:P, :], digit_i[0:P, :])
                reset()

                def count(it, s, c):
                    wait(ph["counted"], ph.upto("counted", c - 1))
                    for j in range(CE):
                        ts(one_hot[s][j][:, 0:n], digits_bf[:, 0:n], digit[0:P, bass.ds(c * CE + j, 1)], None, ALU.is_equal, w=False)
                    done(ph["hist"])
                    if s:
                        reset()
                steps(dve, NCHUNK, count)
                reset()
                if k == 0:
                    weights()
                dve.wait_ge(ph["counted"], ph.upto("counted", NCHUNK))
                copy(total[0:P, 0:n], bank(6)[0:P, 0:n])
                link(V.tensor_tensor_scan(cursor[0:P, 0:n], ones[0:P, 0:1].broadcast_to([P, n]), total[0:P, 0:n], 0.0, ALU.mult, ALU.add))
                tt(cursor[0:P, 0:n], cursor[0:P, 0:n], total[0:P, 0:n], ALU.subtract)
                tt(cursor[0:P, 0:n], cursor[0:P, 0:n], bank(7)[0:P, 0:n], ALU.add)
                reset()

                def places(it, s, c):
                    for j in range(CE):
                        mine = digit[0:P, bass.ds(c * CE + j, 1)]
                        link(V.scalar_tensor_tensor(matched[0:P, 0:n], digits_row[0:P, 0:n], mine, cursor[0:P, 0:n], ALU.is_equal, ALU.mult,
                                                    accum_out=rank[0:P, j:j + 1]), False)
                        stt(cursor[0:P, 0:n], digits_row[0:P, 0:n], mine, cursor[0:P, 0:n], ALU.is_equal, ALU.add)
                    wait(ph["scattered"][s], ph.upto("scattered", it * (16 * CE)))
                    copy(place_i[0:P, s, :], rank[0:P, :], False)
                    copy(rec_stage[0:P, s, :].rearrange("p (t c) -> p t c", c=REC), rec_v[:, bass.ds(c * CE, CE), :])
                    done(ph["staged"])
                    if s:
                        reset()
                steps(dve, NCHUNK, places)
                reset()

            def order_info(o):
                key = rec_v[:, :, o]
                dve.wait_ge(SORT[2 * o + 1]["rec"], SORT[2 * o + 1].upto("rec", 16))
                copy(dst_i[o][0:P, :], rec_v[:, :, 0], False)
                copy(src_i[o][0:P, :], rec_v[:, :, 1], False)
                for g, op in enumerate((ALU.is_gt, ALU.is_lt)):
                    ts(off[o][0:P, g, :], rec_v[:, :, 2], 0.0, BIG, op, ALU.mult)
                    ts(off[o][0:P, g, :], off[o][0:P, g, :], -BIG, None, ALU.add)
                link(V.memset(keep[o][0:P, 0:1], 0.0), False)
                link(V.memset(keep_b[o][0:P, TE - 1:TE], 0.0), False)
                tt(keep[o][0:P, 1:TE], key[:, 1:TE], key[:, 0:TE - 1], ALU.is_equal, False)
                tt(keep_b[o][0:P, 0:TE - 1], key[:, 1:TE], key[:, 0:TE - 1], ALU.is_equal, False)
                ts(first[o][0:P, :], key, key[:, 0:1], None, ALU.is_equal, w=False)
                ts(last[o][0:P, :], key, key[:, TE - 1:TE], None, ALU.is_equal, w=False)
                for k, t in enumerate((0, TE - 1)):
                    ts(key_diag[0:P, k, 0:P], ident[0:P, 0:P], key[:, t:t + 1], None, ALU.mult, w=False)
                done(ORD[o]["diag"])
                dve.wait_ge(ORD[o]["bc"], ORD[o].upto("bc", 1))
                kf, kl = bank(7)[0:P, 0:P], bank(7)[0:P, 128:128 + P]
                k0, k1 = key[:, 0:1], key[:, TE - 1:TE]
                stt(carry_f[o][0:P, 0:P], kf, k1, tri_lt[0:P, 0:P], ALU.is_equal, ALU.mult, False)
                stt(carry_b[o][0:P, 0:P], kl, k0, tri_gt[0:P, 0:P], ALU.is_equal, ALU.mult, False)
                stt(far_f[o][0:P, 0:P], kl, k0, tri_gt[0:P, 0:P], ALU.is_equal, ALU.mult, False)
                stt(far_b[o][0:P, 0:P], kf, k1, tri_lt[0:P, 0:P], ALU.is_equal, ALU.mult)
                red(goes_on[0:P, :], far_b[o][0:P, 0:P], ALU.max)
                for m in (far_f, far_b):
                    ts(m[o][0:P, 0:P], m[o][0:P, 0:P], BIG, -BIG, ALU.mult, ALU.add, w=False)
                stt(digit[0:P, :], keep_b[o][0:P, :], float(SKIP), key, ALU.mult, ALU.add)
                stt(digit[0:P, TE - 1:TE], goes_on[0:P, :], float(SKIP), digit[0:P, TE - 1:TE], ALU.mult, ALU.add)
                copy(out_i[o][0:P, :], digit[0:P, :], False)
                if o:
                    copy(pair_i[0:P, :], rec_v[:, :, 4], False)
                    copy(weight1[0:P, :], rec_v[:, :, 3], False)
                done(ORD[o]["done"])

            for o in range(2):
                for k in range(2):
                    sort_pass(2 * o + k)
                order_info(o)
                if o == 0:
                    copy(rec_v[:, :, 4], position_i[0:P, :])
            reset()

            def edge_rows(l):
                ph = EDGE[l]

                def body(it, s, c):
                    wait(ph["gathered"][s], ph.upto("gathered", it * (32 * CE) + 32 * CE))
                    g, a_, b_ = G[0][:, bass.ds(c * CE, CE), :], g_src[s], g_dst[s]
                    es, ed = D, D + 8
                    tt(g[:, :, 0:D], a_[:, :, 0:D], b_[:, :, 0:D], ALU.subtract, False)
                    tt(g[:, :, D:D + 4], a_[:, :, es:es + 4], b_[:, :, ed:ed + 4], ALU.add, False)
                    tt(g[:, :, D + 4:D + 8], b_[:, :, es:es + 4], b_[:, :, ed:ed + 4], ALU.add, False)
                    tt(g[:, :, D + 8:D + 12], b_[:, :, es + 4:es + 8], a_[:, :, ed + 4:ed + 8], ALU.add, False)
                    tt(g[:, :, D + 12:D + 16], a_[:, :, es + 4:es + 8], a_[:, :, ed + 4:ed + 8], ALU.add, False)
                    done(ph["rows"])
                    if s:
                        reset()
                steps(dve, NCHUNK, body)
                reset()

            def scan(o, d0, d1, init, op0, op1, back=False, w=False):
                if back:
                    o, d0, d1 = o[:, ::-1], d0[:, ::-1], d1[:, ::-1]
                link(V.tensor_tensor_scan(o, d0, d1, init, op0, op1), w)

            def attention(l, d):
                ph, o = ATT[l][d], d
                Es, Sf, F, B, mx, pp = att
                if d:
                    for s in range(2):
                        dve.wait_ge(EDGE[l]["copied"][s], EDGE[l].upto("copied", 16 * NCHUNK // 2))
                for k, m in enumerate((keep, keep_b, first, last)):
                    ts(seg_off[0:P, k, :], m[o][0:P, :], BIG, -BIG, ALU.mult, ALU.add, w=False)
                for to, at in ((Es, D + 8 * d), (Sf, D + 8 * d + 4)):
                    x = G[d][:, :, at:at + 4].rearrange("p t s -> p s t")
                    stt(to, x, 0.2, x, ALU.mult, ALU.max, False)
                dve.wait_ge(s_link, chain[0])
                for g in range(2):
                    tt(Es[:, 2 * g:2 * g + 2, :], Es[:, 2 * g:2 * g + 2, :], off[o][0:P, g:g + 1, :].broadcast_to([P, 2, TE]), ALU.add, False)
                dve.wait_ge(s_link, chain[0])
                for s in range(4):
                    scan(F[:, s, :], seg_off[0:P, 0, :], Es[:, s, :], -BIG, ALU.add, ALU.max)
                    scan(B[:, s, :], seg_off[0:P, 1, :], Es[:, s, :], -BIG, ALU.add, ALU.max, back=True)
                dve.wait_ge(s_link, chain[0])
                tt(mx, F, B, ALU.max)
                tt(mx, mx, Sf, ALU.max)
                for k, (edge, farm) in enumerate(((F[:, :, TE - 1], far_f), (B[:, :, 0], far_b))):
                    if k:
                        dve.wait_ge(ph["bc"], ph.upto("bc", k))
                    for s in range(4):
                        ts(diag[0:P, s, :], ident[0:P, 0:P], edge[:, s:s + 1], None, ALU.mult, w=False)
                    done(ph["diag"])
                    dve.wait_ge(ph["bc"], ph.upto("bc", k + 1))
                    tt(far[0:P, :, :], bank(6)[0:P, 0:4 * P].rearrange("p (s q) -> p s q", s=4),
                       farm[o][0:P, 0:P].unsqueeze(1).broadcast_to([P, 4, P]), ALU.add)
                    red(carry4[0:P, k, :], far[0:P, :, :], ALU.max)
                for k in range(2):
                    for s in range(4):
                        stt(mx[:, s, :], seg_off[0:P, 2 + k, :], carry4[0:P, k, s:s + 1], mx[:, s, :], ALU.add, ALU.max, False)
                    dve.wait_ge(s_link, chain[0])
                tt(F, Es, mx, ALU.subtract, False)
                tt(B, Sf, mx, ALU.subtract, False)
                done(ph["dve"])
                dve.wait_ge(ph["exp"], ph.upto("exp", 1))
                for s in range(4):
                    scan(F[:, s, :], keep[o][0:P, :], pp[:, s, :], 0.0, ALU.mult, ALU.add)
                    scan(B[:, s, :], keep_b[o][0:P, :], pp[:, s, :], 0.0, ALU.mult, ALU.add, back=True)
                done(ph["diag"])
                dve.wait_ge(ph["exp"], ph.upto("exp", 2))
                tt(F, F, B, ALU.add)
                tt(F, F, pp, ALU.subtract)
                tt(F, F, Sf, ALU.add)
                for k, m in ((2, first), (3, last)):
                    for s in range(4):
                        stt(F[:, s, :], m[o][0:P, :], carry4[0:P, k, s:s + 1], F[:, s, :], ALU.mult, ALU.add, False)
                    dve.wait_ge(s_link, chain[0])
                recip(F, F)
                stt(Es, pp, 1.0 if d == 0 else -1.0, F, ALU.mult, ALU.mult)
                if d == 0:
                    dve.wait_ge(EDGE[l]["pair"], EDGE[l].upto("pair", 16 * NCHUNK))
                tt(Es[:, 0:2, :], Es[:, 0:2, :], Es[:, 2:4, :], ALU.add, False)
                ts(F[:, 0:2, :], off[o][0:P, :, :], 0.0, None, ALU.is_equal)
                reset()

                def each(v, g):
                    return v[:, 0:2, bass.ds(g * GRP, GRP)].rearrange("p k t -> p t k").unsqueeze(3).broadcast_to([P, GRP, 2, D])

                def group(it, s, g, on):
                    pr = scratch[0:P, 4 * 4 * TE:4 * 4 * TE + GRP * 2 * D].rearrange("p (t k n) -> p t k n", t=GRP, k=2)
                    if on(0):
                        wait(ph["tr"], ph.upto("tr", g - 1))
                        V.tensor_tensor(grp_stage[0:P, s, :].rearrange("p (t k n) -> p t k n", t=GRP, k=2),
                                        G[d][:, bass.ds(g * GRP, GRP), 0:D].unsqueeze(2).broadcast_to([P, GRP, 2, D]),
                                        each(F, g), ALU.mult).then_inc(ph["copied"], 1)
                    if on(2):
                        wait(ph["mm"], ph.upto("mm", g - 1))
                        tt(pr, bank(2 + s)[0:P, :].rearrange("p (t k n) -> p t k n", t=GRP, k=2), each(Es, g - 2), ALU.mult)
                        done(ph["prod"])
                        tt(G[d][:, bass.ds((g - 2) * GRP, GRP), 0:D], pr[:, :, 0, :], pr[:, :, 1, :], ALU.add)
                    if s:
                        reset()
                pipelined(dve, NGRP, 2, group, head=4)
                reset()

            def segment_sums(ph, v, o):
                with dve.Fori(0, D // 16) as f:
                    for j in range(16):
                        vf = v[:, :, bass.ds(f * 16 + j, 1)].rearrange("p t a -> p (t a)")
                        scan(vf, keep[o][0:P, :], vf, 0.0, ALU.mult, ALU.add)
                    reset()
                done(ph["scan"])
                dve.wait_ge(ph["cvc"], ph.upto("cvc", 1))

            def carry_in(ph, v, o):
                with dve.Fori(0, D // 16) as f:
                    for j in range(16):
                        at = bass.ds(f * 16 + j, 1)
                        vf = v[:, :, at].rearrange("p t a -> p (t a)")
                        stt(vf, first[o][0:P, :], carry_v[0:P, at], vf, ALU.mult, ALU.add, False)
                    reset()
                done(ph["carried"])

            def node_update(l):
                ph, lags = NODE[l], NODE_LAGS[l]
                z_ps = [bank(b, 3)[0:P, 0:CN * D].rearrange("p (t w) -> p t w", w=D) for b in (2, 5)]

                def body(it, s, c, on):
                    if on(0):
                        wait(ph["corr"][s], ph.upto("corr", it * 32 + 32))
                        tt(n_f[s], n_f[s], n_r[s], ALU.add)
                        wait(ph["mm"], ph.upto("mm", groups_by(c, s, lags, 0)[0]))
                        tt(n_u[s], z_ps[0], n_f[s], ALU.add)
                        done(ph["u"])
                    if on(2):
                        z = n_z[s]
                        wait(ph["rstd"], ph.upto("rstd", c - 1))
                        tt(z, z, cols(small[0:P, 4 + s, :]), ALU.mult)
                        tt(z, z, rows_of(g_row[l], CN), ALU.mult)
                        tt(z, z, rows_of(be_row[l], CN), ALU.add)
                        done(ph["h"] if l + 1 < L else ph["rows"])
                    if on(1):
                        z = n_z[1 - s]
                        if l + 1 < L:
                            wait(ph["rows"], ph.upto("rows", c - 2))
                        else:
                            wait(ph["store"][1 - s], ph.upto("store", (it - 1 + s) * 16))
                        wait(ph["mm"], ph.upto("mm", groups_by(c, s, lags, 1)[0]))
                        tt(z, z_ps[1], n_h[1 - s][:, :, 0:D], ALU.add)
                        done(ph["z"])
                        center(z, small[0:P, 0, :], CN)
                        done(ph["zc"])
                    if on(1):
                        wait(ph["sq"], ph.upto("sq", c))
                        red(small[0:P, 3 - s, :], n_q[1 - s])
                        ts(small[0:P, 3 - s, :], small[0:P, 3 - s, :], 1.0 / D, 1e-5, ALU.mult, ALU.add)
                        done(ph["var"])
                    if s:
                        reset()
                pipelined(dve, NCHUNK, 2, body, head=4)
                reset()

            for l in range(L):
                edge_rows(l)
                for d in range(2):
                    attention(l, d)
                    segment_sums(ATT[l][d], G[d], d)
                    carry_in(ATT[l][d], G[d], d)
                node_update(l)

            tt(products[0][:, 0, :], hyp_bias[0:P, :], hyp_bias[0:P, :], ALU.mult)
            red(bias_sc[0:P, 0:1], products[0][:, 0, :])
            root(HYP, bias_sc[0:P, 1:2], bias_sc[0:P, 0:1], bias_sc[0:P, 5:6])
            ts(bias_sc[0:P, 1:2], bias_sc[0:P, 1:2], MIN_NORM, None, ALU.max)
            ask(HYP, "act")
            ts(bias_sc[0:P, 2:3], bias_sc[0:P, 2:3], MAXNORM, None, ALU.min)
            recip(bias_sc[0:P, 3:4], bias_sc[0:P, 1:2])
            tt(bias_sc[0:P, 3:4], bias_sc[0:P, 3:4], bias_sc[0:P, 2:3], ALU.mult)
            ts(hyp_bias[0:P, :], hyp_bias[0:P, :], bias_sc[0:P, 3:4], None, ALU.mult)
            tt(products[0][:, 0, :], hyp_bias[0:P, :], hyp_bias[0:P, :], ALU.mult)
            red(bias_sc[0:P, 4:5], products[0][:, 0, :])
            y2 = bias_sc[0:P, 4:5]
            reset()
            ph = HYP

            def scol(k, c):
                return sc[k][:, bass.ds(c * CN, CN)]

            def squares_sum(key, k, sums, value=0):
                def stage(s, c):
                    wait(ph[key], c + value)
                    sums(scol(k, c - 1), squares[1 - s])
                return stage

            def residual(it, s, c, on):
                if on(0):
                    wait(ph["load"][s], it * 32 + 32)
                    x = nchunk(c)
                    tt(x, sp_a[s], sp_b[s], ALU.add)
                    done(ph["used"])
                    center(x, small[0:P, 0, :], CN)
                    done(ph["r0"])
                if on(1):
                    squares_sum("sq", 1, red)(s, c)
                if s:
                    reset()
            pipelined(dve, NCHUNK, 1, residual)
            reset()
            ts(sc[2], sc[1], 1.0 / D, 1e-5, ALU.mult, ALU.add)
            root(ph, sc[3], sc[2], sc[4])
            recip(sc[3], sc[3])
            tt(sc[4], sc[1], sc[3], ALU.mult)
            tt(sc[4], sc[4], sc[3], ALU.mult)
            root(ph, sc[5], sc[4], sc[6])
            ts(sc[5], sc[5], MIN_NORM, None, ALU.max)
            ts(sc[6], sc[5], CLIP, None, ALU.min)
            ask(ph, "act")
            artanh_ratio(sc[9], sc[6], sc[7], sc[8], sc[10], sc[4])
            tt(sc[9], sc[9], sc[6], ALU.mult)
            recip(sc[5], sc[5])
            tt(sc[9], sc[9], sc[5], ALU.mult)
            reset()

            def linear(it, s, c, on):
                if on(2):
                    wait(ph["y"], c - 1)
                    tt(products[s], nchunk(c - 2), rows_of(hyp_bias, CN), ALU.mult)
                    sum64(scol(2, c - 2), products[s])
                    sum64(scol(0, c - 2), squares[s])
                if on(0):
                    if not isinstance(c, int):
                        wait(ph["store"][s], it * 16)
                    tt(sp_a[s], nchunk(c), cols(scol(3, c)), ALU.mult)
                    done(ph["x0"])
                if s:
                    reset()
            pipelined(dve, NCHUNK, 2, linear)
            reset()
            reset()
            root(ph, sc[4], sc[0], sc[5])
            tt(sc[5], sc[4], sc[9], ALU.mult)
            ts(sc[5], sc[5], MIN_NORM, None, ALU.max)
            ask(ph, "act")
            ts(sc[7], sc[6], MAXNORM, None, ALU.min)
            recip(sc[8], sc[5])
            tt(sc[8], sc[8], sc[7], ALU.mult)
            tt(sc[8], sc[8], sc[9], ALU.mult)
            tt(sc[10], sc[8], sc[8], ALU.mult)
            tt(sc[10], sc[10], sc[0], ALU.mult)
            tt(sc[6], sc[8], sc[2], ALU.mult)
            ts(sc[4], sc[6], 2.0, 1.0, ALU.mult, ALU.add)
            stt(sc[7], sc[10], y2, sc[4], ALU.mult, ALU.add)
            ts(sc[7], sc[7], MIN_NORM, None, ALU.max)
            recip(sc[7], sc[7])
            ts(sc[4], sc[4], y2, None, ALU.add)
            tt(sc[8], sc[8], sc[4], ALU.mult)
            tt(sc[8], sc[8], sc[7], ALU.mult)
            ts(sc[5], sc[10], -1.0, 1.0, ALU.mult, ALU.add)
            tt(sc[5], sc[5], sc[7], ALU.mult)
            reset()

            def point(it, s, c, on):
                if on(0):
                    x = nchunk(c)
                    tt(x, x, cols(scol(8, c)), ALU.mult, False)
                    tt(products[s], cols(scol(5, c)), rows_of(hyp_bias, CN), ALU.mult)
                    tt(x, x, products[s], ALU.add)
                    done(ph["point"])
                if on(1):
                    squares_sum("psq", 11, sum64)(s, c)
                if s:
                    reset()
            pipelined(dve, NCHUNK, 1, point)
            reset()
            root(ph, sc[1], sc[11], sc[6])
            ts(sc[1], sc[1], MIN_NORM, None, ALU.max)
            ts(sc[6], sc[1], CLIP, None, ALU.min)
            ask(ph, "act")
            artanh_ratio(sc[9], sc[6], sc[7], sc[8], sc[10], sc[4])
            tt(sc[9], sc[9], sc[6], ALU.mult)
            recip(sc[1], sc[1])
            tt(sc[9], sc[9], sc[1], ALU.mult)
            for s in range(2):
                dve.wait_ge(ph["store"][s], 16 * NCHUNK // 2)
            done(ph["act_asked"])
            reset()

            def tables(it, s, c):
                r_, c_ = hyp_r[s], hyp_c[s]
                wait(ph["copied"], c + 1)
                wait(ph["mm"], (c + 1) * GROUPS + NCHUNK * GROUPS)
                pq = bank(2, 5)[0:P, 0:CN * 2 * D].rearrange("p (t w) -> p t w", w=2 * D)
                tt(c_[:, :, D:2 * D], pq[:, :, D:2 * D], cols(scol(9, c)), ALU.mult, False)
                tt(r_[:, :, D:2 * D], pq[:, :, 0:D], cols(scol(9, c)), ALU.mult)
                done(ph["pq"])
                tt(r_[:, :, D:2 * D], r_[:, :, D:2 * D], rows_of(hyp_row["b1"], CN), ALU.add)
                done(ph["rows"])
                if s:
                    reset()
            steps(dve, NCHUNK, tables)

            reset()
            ph = HE

            def ecol(k, c=None):
                return sc[k][:, 0:TE] if c is None else sc[k][:, bass.ds(c * CE, CE)]

            def edge_points(it, s, c, on):
                if on(0):
                    wait(ph["gathered"][s], it * (32 * CE) + 32 * CE)
                    r_, c_ = h_row[s], h_col[s]
                    xr, xc, tmp = r_[:, :, 0:D], c_[:, :, 0:D], e_tmp[s]
                    v, pre = edges_v[:, bass.ds(c * CE, CE), :], edges_pre[:, bass.ds(c * CE, CE), :]
                    dot(ecol(0, c), xr, xc, tmp)
                    copy(ecol(1, c), r_[:, :, 2 * D], False)
                    copy(ecol(2, c), c_[:, :, 2 * D], False)
                    stt(small[0:P, 0, 0:CE], ecol(0, c), 2.0, c_[:, :, 2 * D], ALU.mult, ALU.subtract, False)
                    ts(small[0:P, 1, 0:CE], r_[:, :, 2 * D], -1.0, 1.0, ALU.mult, ALU.add)
                    ts(small[0:P, 0, 0:CE], small[0:P, 0, 0:CE], -1.0, None, ALU.add)
                    tt(v, xr, cols(small[0:P, 0, 0:CE]), ALU.mult, False)
                    tt(tmp, xc, cols(small[0:P, 1, 0:CE]), ALU.mult)
                    tt(v, v, tmp, ALU.add)
                    done(ph["v"])
                    tt(pre, r_[:, :, D:2 * D], c_[:, :, D:2 * D], ALU.add, False)
                    tt(tmp, cols(weight1[0:P, bass.ds(c * CE, CE)]), rows_of(hyp_row["wd"], CE), ALU.mult)
                    tt(pre, pre, tmp, ALU.add)
                    done(ph["rows"])
                if on(1):
                    wait(ph["sq"], c)
                    sum64(ecol(3, c - 1), e_sq[1 - s])
                if s:
                    reset()
            pipelined(dve, NCHUNK, 1, edge_points)
            reset()
            tt(ecol(4), ecol(1), ecol(2), ALU.mult)
            stt(ecol(4), ecol(0), -2.0, ecol(4), ALU.mult, ALU.add)
            ts(ecol(4), ecol(4), 1.0, MIN_NORM, ALU.add, ALU.max)
            recip(ecol(4), ecol(4))
            root(ph, ecol(5), ecol(3), ecol(6))
            tt(ecol(5), ecol(5), ecol(4), ALU.mult)
            ts(ecol(5), ecol(5), MIN_NORM, None, ALU.max)
            ts(ecol(6), ecol(5), CLIP, None, ALU.min)
            ask(ph, "act")
            artanh_ratio(ecol(9), ecol(6), ecol(7), ecol(8), ecol(10), ecol(2))
            tt(ecol(9), ecol(9), ecol(6), ALU.mult)
            stt(ecol(10), ecol(9), 4.0, ecol(9), ALU.mult, ALU.mult)
            reset()

            def mlp(it, s, c, on):
                if on(0):
                    pre = edges_pre[:, bass.ds(c * CE, CE), :]
                    tt(e_tmp[s], cols(ecol(10, c)), rows_of(hyp_row["wg"], CE), ALU.mult)
                    tt(pre, pre, e_tmp[s], ALU.add)
                    done(ph["pre"])
                if on(1):
                    pre = edges_pre[:, bass.ds((c - 1) * CE, CE), :]
                    wait(ph["gate"], c)
                    tt(pre, pre, hyp_stage[1 - s], ALU.mult)
                    tt(pre, pre, rows_of(hyp_row["w2"], CE), ALU.mult)
                    red(ecol(0, c - 1), pre)
                if s:
                    reset()
            pipelined(dve, NCHUNK, 1, mlp)
            reset()
            ask(ph, "act")
            tt(ecol(2), ecol(2), weight1[0:P, :], ALU.mult)
            ts(ecol(1), ecol(1), -1.0, 1.0, ALU.mult, ALU.add)
            ts(ecol(1), ecol(1), MIN_NORM, None, ALU.max)
            tt(ecol(1), ecol(1), ecol(9), ALU.mult)
            recip(ecol(5), ecol(5))
            tt(ecol(1), ecol(1), ecol(5), ALU.mult)
            tt(ecol(1), ecol(1), ecol(4), ALU.mult)
            stt(ecol(8), ecol(1), 1.0 / 100.0, ecol(2), ALU.mult, ALU.mult)
            tt(edges_v, edges_v, cols(ecol(8)), ALU.mult)
            reset()
            segment_sums(ph, edges_v, 1)
            carry_in(ph, edges_v, 1)

            ph = FIN

            def dots(it, s, c):
                wait(ph["load1"][s], it * 32 + 32)
                tt(products[s], sp_a[s], sp_b[s], ALU.mult)
                red(scol(1, c), products[s])
                wait(ph["sq0"], c + 1)
                red(scol(0, c), squares[s])
                done(ph["used1"])
                if s:
                    reset()
            steps(dve, NCHUNK, dots)
            reset()
            root(ph, sc[2], sc[0], sc[3])
            ts(sc[2], sc[2], MIN_NORM, None, ALU.max)
            ts(sc[3], sc[11], -1.0, 1.0, ALU.mult, ALU.add)
            ts(sc[3], sc[3], MIN_NORM, None, ALU.max)
            recip(sc[3], sc[3])
            tt(sc[4], sc[2], sc[3], ALU.mult)
            ask(ph, "act")
            recip(sc[6], sc[2])
            tt(sc[6], sc[6], sc[5], ALU.mult)
            tt(sc[7], sc[6], sc[6], ALU.mult)
            tt(sc[7], sc[7], sc[0], ALU.mult)
            tt(sc[8], sc[6], sc[1], ALU.mult)
            ts(sc[8], sc[8], 2.0, 1.0, ALU.mult, ALU.add)
            tt(sc[9], sc[8], sc[7], ALU.add)
            tt(sc[10], sc[11], sc[7], ALU.mult)
            tt(sc[10], sc[10], sc[8], ALU.add)
            ts(sc[10], sc[10], MIN_NORM, None, ALU.max)
            recip(sc[10], sc[10])
            ts(sc[4], sc[11], -1.0, 1.0, ALU.mult, ALU.add)
            tt(sc[4], sc[4], sc[6], ALU.mult)
            tt(sc[4], sc[4], sc[10], ALU.mult)
            tt(sc[9], sc[9], sc[10], ALU.mult)
            reset()

            def combine(it, s, c, on):
                if on(0):
                    wait(ph["load2"][s], it * 32 + 32)
                    x = nchunk(c)
                    tt(x, sp_a[s], cols(scol(9, c)), ALU.mult, False)
                    tt(sp_t, sp_b[s], cols(scol(4, c)), ALU.mult)
                    done(ph["used2"])
                    tt(x, x, sp_t, ALU.add)
                    done(ph["x"])
                if on(1):
                    squares_sum("sq", 0, sum64)(s, c)
                if s:
                    reset()
            pipelined(dve, NCHUNK, 1, combine)
            reset()
            root(ph, sc[2], sc[0], sc[6])
            ts(sc[2], sc[2], MIN_NORM, None, ALU.max)
            ts(sc[6], sc[2], MAXNORM, None, ALU.min)
            ask(ph, "act")
            artanh_ratio(sc[9], sc[6], sc[7], sc[8], sc[10], sc[5])
            tt(sc[9], sc[9], sc[6], ALU.mult)
            recip(sc[2], sc[2])
            tt(sc[9], sc[9], sc[2], ALU.mult)
            reset()

            def tangent(it, s, c, on):
                if on(0):
                    x = nchunk(c)
                    tt(x, x, cols(scol(9, c)), ALU.mult)
                    center(x, small[0:P, 0, :], CN)
                    done(ph["x"])
                if on(1):
                    squares_sum("sq", 1, red, NCHUNK)(s, c)
                if s:
                    reset()
            pipelined(dve, NCHUNK, 1, tangent)
            reset()
            ts(sc[1], sc[1], 1.0 / D, 1e-5, ALU.mult, ALU.add)
            root(ph, sc[2], sc[1], sc[6])
            recip(sc[2], sc[2])
            reset()

            def normed(it, s, c, on):
                if on(0):
                    x = nchunk(c)
                    tt(x, x, cols(scol(2, c)), ALU.mult)
                    tt(x, x, rows_of(hyp_row["g"], CN), ALU.mult)
                    tt(x, x, rows_of(hyp_row["b"], CN), ALU.add)
                    done(ph["x"])
                if on(1):
                    squares_sum("sq", 0, red, 2 * NCHUNK)(s, c)
                    red(scol(1, c - 1), products[1 - s])
                if s:
                    reset()
            pipelined(dve, NCHUNK, 1, normed)
            reset()
            root(ph, sc[2], sc[0], sc[6])
            root(ph, sc[3], sc[1], sc[6])
            ts(sc[2], sc[2], MIN_NORM, None, ALU.max)
            ask(ph, "act")
            ts(sc[6], sc[4], MAXNORM, MIN_NORM, ALU.min, ALU.max)
            ask(ph, "act")
            artanh_ratio(sc[9], sc[6], sc[7], sc[8], sc[10], sc[5])
            recip(sc[2], sc[2])
            tt(sc[9], sc[9], sc[6], ALU.mult)
            tt(sc[9], sc[9], sc[2], ALU.mult)
            tt(sc[3], sc[3], sc[9], ALU.mult)
            ts(sc[3], sc[3], MIN_NORM, None, ALU.max)
            ask(ph, "act")
            ts(sc[4], sc[4], MAXNORM, None, ALU.min)
            recip(sc[3], sc[3])
            tt(sc[9], sc[9], sc[4], ALU.mult)
            tt(sc[9], sc[9], sc[3], ALU.mult)
            reset()

            def add_x0(it, s, c, on):
                if on(0):
                    wait(ph["load3"][s], it * 16 + 16)
                    x = nchunk(c)
                    tt(x, x, cols(scol(9, c)), ALU.mult)
                    tt(x, x, sp_a[s], ALU.add)
                    done(ph["used3"])
                    center(x, small[0:P, 0, :], CN)
                    done(ph["x"])
                if on(1):
                    squares_sum("sq", 1, red, 3 * NCHUNK)(s, c)
                if s:
                    reset()
            pipelined(dve, NCHUNK, 1, add_x0)
            reset()
            ts(sc[1], sc[1], 1.0 / D, 1e-5, ALU.mult, ALU.add)
            root(ph, sc[2], sc[1], sc[6])
            recip(sc[2], sc[2])
            reset()

            def output(it, s, c):
                wait(ph["store"][s], ph.upto("store", it * 16))
                tt(sp_b[s], nchunk(c), cols(scol(2, c)), ALU.mult)
                done(ph["rows"])
                if s:
                    reset()
            steps(dve, NCHUNK, output)


            reset()
_INS = ["x", "src", "dst", "edge_weight", "edge_weight1",
        "L0_gnn_gat_W", "L0_gnn_gat_asrc", "L0_gnn_gat_adst", "L0_gnn_gat_bias", "L0_gnn_mlp_W1", "L0_gnn_mlp_b1",
        "L0_gnn_mlp_W2", "L0_gnn_mlp_b2", "L0_gnn_ln_g", "L0_gnn_ln_b", "L1_gnn_lin_W", "L1_gnn_bias", "L1_gnn_att_W1",
        "L1_gnn_att_b1", "L1_gnn_att_W2", "L1_gnn_att_b2", "L1_gnn_ln_g", "L1_gnn_ln_b"]


def kernel(**inputs):
    import numpy as np
    import concourse.bacc as bacc
    from concourse.bass_utils import run_bass_kernel_spmd

    nc = bacc.Bacc("TRN2", target_bir_lowering=False, num_devices=1)
    arrays, aps = {}, {}
    for name in _INS:
        arr = np.ascontiguousarray(inputs[name])
        arrays["in_" + name] = arr
        aps[name] = nc.dram_tensor("in_" + name, arr.shape, mybir.dt.from_np(arr.dtype), kind="ExternalInput").ap()
    out = nc.dram_tensor("out", (N, D), mybir.dt.float32, kind="ExternalOutput").ap()
    build(nc, aps, out)
    return run_bass_kernel_spmd(nc, [arrays], core_ids=[0]).results[0]["out"]
```
